# Optimizing a Trainium2 kernel written in Bass

```python
import numpy as np
import jax
import jax.numpy as jnp

def _softmax(x, axis=-1):
    return jax.nn.softmax(x, axis=axis)

def _gelu(x):
    return jax.nn.gelu(x, approximate=True)

def _silu(x):
    return jax.nn.silu(x)

def _sigmoid(x):
    return jax.nn.sigmoid(x)

def _layernorm(x, axis=-1, eps=1e-05):
    m = jnp.mean(x, axis=axis, keepdims=True)
    v = jnp.var(x, axis=axis, keepdims=True)
    return (x - m) / jnp.sqrt(v + eps)

def _scatter_add(tgt, idx, src, axis=0):
    return tgt.at[idx].add(src)

def _segment_sum(src, seg, n):
    return jax.ops.segment_sum(src, seg, n)
kernel_name = 'mk_flamingo_gated_d4_seqx_r8_ae5a50'

def setup_inputs(seed: int=0):
    np.random.seed(seed)
    _w = jnp.asarray

    def _rec_inputs():
        import jax
        import jax.numpy as jnp
        _rk = jax.random.key(seed)
        x = -0.0002928 + 1 * jax.random.normal(jax.random.fold_in(_rk, 1), (4, 256, 128), jnp.float32)
        _lenS = 256 - jax.random.randint(jax.random.fold_in(_rk, 7), (4,), 0, max(1, 256 // 4) + 1, jnp.int32)
        _lenS2 = 256 - jax.random.randint(jax.random.fold_in(_rk, 8), (4,), 0, max(1, 256 // 4) + 1, jnp.int32)
        _ctx_1024P = jax.random.normal(jax.random.fold_in(_rk, 11), (4, 16, 128), jnp.float32)
        _ctx_1024c = jax.random.dirichlet(jax.random.fold_in(_rk, 511), 0.3 * jnp.ones((16,), jnp.float32), (4, 256))
        _ctx_1024t = jnp.einsum('bsk,bkd->bsd', _ctx_1024c, _ctx_1024P)
        _ctx_1024t = _ctx_1024t * jax.lax.rsqrt(jnp.mean(jnp.square(_ctx_1024t)) + 1e-12) * 0.953939
        ctx_1024 = -1.39393e-06 + 0.999914 * (_ctx_1024t + 0.3 * jax.random.normal(jax.random.fold_in(_rk, 611), (4, 256, 128), jnp.float32))
        _validS = jnp.arange(256)[None, :] < _lenS[:, None]
        _validS2 = jnp.arange(256)[None, :] < _lenS2[:, None]
        _causal = jnp.tril(jnp.ones((256, 256), dtype=bool))
        mask_BxS2_ff1 = jnp.where(jnp.ones((4, 256), dtype=bool), 1.0, 0.0).astype(jnp.float32)
        mask_BxS2_ik0 = jnp.where(jnp.broadcast_to(_validS2[:, :], (4, 256)), 0, 1).astype(jnp.int32)
        _g = jax.random.normal(jax.random.fold_in(_rk, 9001), (2, 4), jnp.float32)
        _g = jnp.sign(_g) * jnp.maximum(jnp.abs(_g), 1.0) + (_g == 0) * 1.0
        g_xattn = _g[0]
        g_ffn = _g[1]
        return (x, ctx_1024, mask_BxS2_ff1, mask_BxS2_ik0, g_xattn, g_ffn)
    x, ctx_1024, mask_BxS2_ff1, mask_BxS2_ik0, g_xattn, g_ffn = _rec_inputs()

    def _L0_xattn_setup():
        import jax, jax.numpy as jnp
        import numpy as np
        import math
        D_MODEL = 128
        NUM_HEADS = 16
        MAX_LEN = 256
        D_HEAD = D_MODEL // NUM_HEADS
        BATCH = 2
        SEQ = 256

        def _skew(QEr):
            B, H, R, C = QEr.shape
            padded = jnp.pad(QEr, ((0, 0), (0, 0), (0, 0), (1, 0)))
            reshaped = padded.reshape(B, H, C + 1, R)
            return reshaped[:, :, 1:, :]
        root = jax.random.key(seed)
        ks = jax.random.split(root, 10)
        s = 1.0 / math.sqrt(D_MODEL)
        return {'query': jax.random.normal(ks[0], (BATCH, SEQ, D_MODEL), jnp.float32), 'key': jax.random.normal(ks[1], (BATCH, SEQ, D_MODEL), jnp.float32), 'value': jax.random.normal(ks[2], (BATCH, SEQ, D_MODEL), jnp.float32), 'Wq': jax.random.normal(ks[3], (D_MODEL, D_MODEL), jnp.float32) * s, 'bq': jax.random.normal(ks[4], (D_MODEL,), jnp.float32) * s, 'Wk': jax.random.normal(ks[5], (D_MODEL, D_MODEL), jnp.float32) * s, 'bk': jax.random.normal(ks[6], (D_MODEL,), jnp.float32) * s, 'Wv': jax.random.normal(ks[7], (D_MODEL, D_MODEL), jnp.float32) * s, 'bv': jax.random.normal(ks[8], (D_MODEL,), jnp.float32) * s, 'Er': jax.random.normal(ks[9], (MAX_LEN, D_HEAD), jnp.float32)}
    _L0_xattn_all = _L0_xattn_setup()
    _L0_xattn_in = {k: v for k, v in _L0_xattn_all.items() if k in ('Wq', 'bq', 'Wk', 'bk', 'Wv', 'bv', 'Er')}
    del _L0_xattn_all

    def _L0_ffn_setup():
        import jax, jax.numpy as jnp
        import numpy as np
        E, D, DFF = (8, 128, 512)
        key = jax.random.key(seed)
        ks = jax.random.split(key, 10)
        s = 0.02
        return {'x': jax.random.normal(ks[0], (4, 256, D), dtype=jnp.float32), 'Wr': jax.random.normal(ks[1], (D, E), dtype=jnp.float32) * s, 'br': jnp.zeros((E,), dtype=jnp.float32), 'W1': jax.random.normal(ks[2], (E, D, DFF), dtype=jnp.float32) * s, 'b1': jnp.zeros((E, DFF), dtype=jnp.float32), 'W2': jax.random.normal(ks[3], (E, D, DFF), dtype=jnp.float32) * s, 'b2': jnp.zeros((E, DFF), dtype=jnp.float32), 'W3': jax.random.normal(ks[4], (E, DFF, D), dtype=jnp.float32) * s, 'b3': jnp.zeros((E, D), dtype=jnp.float32)}
    _L0_ffn_all = _L0_ffn_setup()
    _L0_ffn_in = {k: v for k, v in _L0_ffn_all.items() if k in ('Wr', 'br', 'W1', 'b1', 'W2', 'b2', 'W3', 'b3')}
    del _L0_ffn_all

    def _L1_xattn_setup():
        import jax, jax.numpy as jnp
        import numpy as np
        import math
        B, L, D, NUM_HEADS = (4, 256, 128, 16)
        HEAD_SIZE = D // NUM_HEADS
        key = jax.random.key(seed)
        ks = jax.random.split(key, 9)
        s = 1.0 / math.sqrt(D)
        return {'query_states': jax.random.normal(ks[0], (B, L, D), jnp.float32), 'key_states': jax.random.normal(ks[1], (B, L, D), jnp.float32), 'value_states': jax.random.normal(ks[2], (B, L, D), jnp.float32), 'attention_mask': jnp.ones((B, L), jnp.float32), 'Wq': jax.random.normal(ks[3], (D, D), jnp.float32) * s, 'bq': jnp.zeros((D,), jnp.float32), 'Wk': jax.random.normal(ks[4], (D, D), jnp.float32) * s, 'bk': jnp.zeros((D,), jnp.float32), 'Wv': jax.random.normal(ks[5], (D, D), jnp.float32) * s, 'bv': jnp.zeros((D,), jnp.float32)}
    _L1_xattn_all = _L1_xattn_setup()
    _L1_xattn_in = {k: v for k, v in _L1_xattn_all.items() if k in ('Wq', 'bq', 'Wk', 'bk', 'Wv', 'bv')}
    del _L1_xattn_all

    def _L1_ffn_setup():
        import jax, jax.numpy as jnp
        import numpy as np
        QMAX = 127.0

        def _ste_round(v):
            return v + jax.lax.stop_gradient(jnp.round(v) - v)

        def _act_fake_quant(x, clip_factor):
            scale = jax.nn.sigmoid(clip_factor) * jnp.max(jnp.abs(x)) / QMAX
            return jnp.clip(_ste_round(x / scale), -QMAX - 1.0, QMAX) * scale

        def _weight_fake_quant(w):
            scale = jnp.max(jnp.abs(w), axis=1, keepdims=True) / QMAX
            return jnp.clip(_ste_round(w / scale), -QMAX - 1.0, QMAX) * scale
        key = jax.random.key(seed)
        k1, k2, k3, k4 = jax.random.split(key, 4)
        B, S, H, I = (8, 1024, 128, 352)
        return {'x': jax.random.normal(k1, (B, S, H), dtype=jnp.float32), 'clip_x': jnp.full((1,), 4.0, dtype=jnp.float32), 'clip_down': jnp.full((1,), 4.0, dtype=jnp.float32), 'w_gate': jax.random.normal(k2, (I, H), dtype=jnp.float32) * 0.02, 'w_up': jax.random.normal(k3, (I, H), dtype=jnp.float32) * 0.02, 'w_down': jax.random.normal(k4, (H, I), dtype=jnp.float32) * 0.02}
    _L1_ffn_all = _L1_ffn_setup()
    _L1_ffn_in = {k: v for k, v in _L1_ffn_all.items() if k in ('clip_x', 'clip_down', 'w_gate', 'w_up', 'w_down')}
    del _L1_ffn_all

    def _L2_xattn_setup():
        import jax, jax.numpy as jnp
        import numpy as np
        B, S, D, H = (2, 256, 128, 16)
        DK = D // H
        SQRT_DK = DK ** 0.5
        NEG = -1000000000.0
        key = jax.random.key(seed)
        ks = jax.random.split(key, 7)
        scale = 1.0 / np.sqrt(D)
        return {'x': jax.random.normal(ks[0], (B, S, D), jnp.float32), 'encoder_output': jax.random.normal(ks[1], (B, S, D), jnp.float32), 'mask': jax.random.randint(ks[2], (B, S), 0, 2, jnp.int32), 'WQ': jax.random.normal(ks[3], (D, D), jnp.float32) * scale, 'WK': jax.random.normal(ks[4], (D, D), jnp.float32) * scale, 'WV': jax.random.normal(ks[5], (D, D), jnp.float32) * scale, 'WO': jax.random.normal(ks[6], (D, D), jnp.float32) * scale}
    _L2_xattn_all = _L2_xattn_setup()
    _L2_xattn_in = {k: v for k, v in _L2_xattn_all.items() if k in ('WQ', 'WK', 'WV', 'WO')}
    del _L2_xattn_all

    def _L2_ffn_setup():
        import jax, jax.numpy as jnp
        import numpy as np
        B, S, D, H, E = (8, 512, 128, 256, 8)
        key = jax.random.key(seed)
        ks = jax.random.split(key, 7)
        scale = 0.02
        return {'x': jax.random.normal(ks[0], (B, S, D), dtype=jnp.float32), 'W1': jax.random.normal(ks[1], (E, D, H), dtype=jnp.float32) * scale, 'b1': jnp.zeros((E, H), dtype=jnp.float32), 'W2': jax.random.normal(ks[2], (E, H, D), dtype=jnp.float32) * scale, 'b2': jnp.zeros((E, D), dtype=jnp.float32), 'Wg': jax.random.normal(ks[3], (D, E), dtype=jnp.float32) * scale, 'bg': jnp.zeros((E,), dtype=jnp.float32)}
    _L2_ffn_all = _L2_ffn_setup()
    _L2_ffn_in = {k: v for k, v in _L2_ffn_all.items() if k in ('W1', 'b1', 'W2', 'b2', 'Wg', 'bg')}
    del _L2_ffn_all

    def _L3_xattn_setup():
        import jax, jax.numpy as jnp
        import numpy as np
        DIM = 128
        HEAD_DIM = 64
        NUM_HEADS = 8
        INNER = HEAD_DIM * NUM_HEADS
        ROT_DIM = HEAD_DIM
        ROPE_BASE = 10000.0
        EPS = 1e-05

        def layer_norm(x, g, b):
            mu = jnp.mean(x, axis=-1, keepdims=True)
            var = jnp.var(x, axis=-1, keepdims=True)
            return (x - mu) * jax.lax.rsqrt(var + EPS) * g + b

        def rope_rotate_k(k):
            n = k.shape[1]
            half = ROT_DIM // 2
            inv_freq = 1.0 / ROPE_BASE ** (jnp.arange(0, ROT_DIM, 2, dtype=jnp.float32) / ROT_DIM)
            theta = jnp.arange(n, dtype=jnp.float32)[:, None] * inv_freq[None, :]
            angles = jnp.concatenate([theta, theta], axis=-1)
            cos = jnp.cos(angles)[None, :, None, :].astype(k.dtype)
            sin = jnp.sin(angles)[None, :, None, :].astype(k.dtype)
            k_rope, k_pass = (k[..., :ROT_DIM], k[..., ROT_DIM:])
            neg_half = jnp.concatenate([-k_rope[..., half:], k_rope[..., :half]], axis=-1)
            k_rope = k_rope * cos + neg_half * sin
            return jnp.concatenate([k_rope, k_pass], axis=-1)
        key = jax.random.key(seed)
        ks = jax.random.split(key, 5)
        b, n, m = (8, 1024, 64)
        s = 1.0 / np.sqrt(DIM)
        return {'x': jax.random.normal(ks[0], (b, n, DIM), jnp.float32), 'latents': jax.random.normal(ks[1], (b, m, DIM), jnp.float32), 'gamma_x': jnp.ones((DIM,), jnp.float32), 'beta_x': jnp.zeros((DIM,), jnp.float32), 'gamma_l': jnp.ones((DIM,), jnp.float32), 'beta_l': jnp.zeros((DIM,), jnp.float32), 'Wq': jax.random.normal(ks[2], (DIM, INNER), jnp.float32) * s, 'Wkv': jax.random.normal(ks[3], (DIM, 2 * INNER), jnp.float32) * s, 'Wo': jax.random.normal(ks[4], (INNER, DIM), jnp.float32) * (1.0 / np.sqrt(INNER))}
    _L3_xattn_all = _L3_xattn_setup()
    _L3_xattn_in = {k: v for k, v in _L3_xattn_all.items() if k in ('gamma_x', 'beta_x', 'gamma_l', 'beta_l', 'Wq', 'Wkv', 'Wo')}
    del _L3_xattn_all

    def _L3_ffn_setup():
        import jax, jax.numpy as jnp
        import numpy as np
        B, N, D, E, R, K = (4, 256, 128, 8, 32, 2)
        key = jax.random.key(seed)
        ks = jax.random.split(key, 5)
        scale = 0.02
        return {'x': jax.random.normal(ks[0], (B, N, D), dtype=jnp.float32), 'gate_w': jax.random.normal(ks[1], (D, E), dtype=jnp.float32) * scale, 'Wu': jax.random.normal(ks[2], (E, D, R), dtype=jnp.float32) * scale, 'Wv': jax.random.normal(ks[3], (E, D, R), dtype=jnp.float32) * scale, 'Wo': jax.random.normal(ks[4], (E, R, D), dtype=jnp.float32) * scale}
    _L3_ffn_all = _L3_ffn_setup()
    _L3_ffn_in = {k: v for k, v in _L3_ffn_all.items() if k in ('gate_w', 'Wu', 'Wv', 'Wo')}
    del _L3_ffn_all
    return {'x': x, 'ctx_1024': ctx_1024, 'mask_BxS2_ff1': mask_BxS2_ff1, 'mask_BxS2_ik0': mask_BxS2_ik0, 'g_xattn': g_xattn, 'g_ffn': g_ffn, 'L0_xattn_Wq': _L0_xattn_in['Wq'], 'L0_xattn_bq': _L0_xattn_in['bq'], 'L0_xattn_Wk': _L0_xattn_in['Wk'], 'L0_xattn_bk': _L0_xattn_in['bk'], 'L0_xattn_Wv': _L0_xattn_in['Wv'], 'L0_xattn_bv': _L0_xattn_in['bv'], 'L0_xattn_Er': _L0_xattn_in['Er'], 'L0_ffn_Wr': _L0_ffn_in['Wr'], 'L0_ffn_br': _L0_ffn_in['br'], 'L0_ffn_W1': _L0_ffn_in['W1'], 'L0_ffn_b1': _L0_ffn_in['b1'], 'L0_ffn_W2': _L0_ffn_in['W2'], 'L0_ffn_b2': _L0_ffn_in['b2'], 'L0_ffn_W3': _L0_ffn_in['W3'], 'L0_ffn_b3': _L0_ffn_in['b3'], 'L1_xattn_Wq': _L1_xattn_in['Wq'], 'L1_xattn_bq': _L1_xattn_in['bq'], 'L1_xattn_Wk': _L1_xattn_in['Wk'], 'L1_xattn_bk': _L1_xattn_in['bk'], 'L1_xattn_Wv': _L1_xattn_in['Wv'], 'L1_xattn_bv': _L1_xattn_in['bv'], 'L1_ffn_clip_x': _L1_ffn_in['clip_x'], 'L1_ffn_clip_down': _L1_ffn_in['clip_down'], 'L1_ffn_w_gate': _L1_ffn_in['w_gate'], 'L1_ffn_w_up': _L1_ffn_in['w_up'], 'L1_ffn_w_down': _L1_ffn_in['w_down'], 'L2_xattn_WQ': _L2_xattn_in['WQ'], 'L2_xattn_WK': _L2_xattn_in['WK'], 'L2_xattn_WV': _L2_xattn_in['WV'], 'L2_xattn_WO': _L2_xattn_in['WO'], 'L2_ffn_W1': _L2_ffn_in['W1'], 'L2_ffn_b1': _L2_ffn_in['b1'], 'L2_ffn_W2': _L2_ffn_in['W2'], 'L2_ffn_b2': _L2_ffn_in['b2'], 'L2_ffn_Wg': _L2_ffn_in['Wg'], 'L2_ffn_bg': _L2_ffn_in['bg'], 'L3_xattn_gamma_x': _L3_xattn_in['gamma_x'], 'L3_xattn_beta_x': _L3_xattn_in['beta_x'], 'L3_xattn_gamma_l': _L3_xattn_in['gamma_l'], 'L3_xattn_beta_l': _L3_xattn_in['beta_l'], 'L3_xattn_Wq': _L3_xattn_in['Wq'], 'L3_xattn_Wkv': _L3_xattn_in['Wkv'], 'L3_xattn_Wo': _L3_xattn_in['Wo'], 'L3_ffn_gate_w': _L3_ffn_in['gate_w'], 'L3_ffn_Wu': _L3_ffn_in['Wu'], 'L3_ffn_Wv': _L3_ffn_in['Wv'], 'L3_ffn_Wo': _L3_ffn_in['Wo']}

def reference(x, ctx_1024, mask_BxS2_ff1, mask_BxS2_ik0, g_xattn, g_ffn, L0_xattn_Wq, L0_xattn_bq, L0_xattn_Wk, L0_xattn_bk, L0_xattn_Wv, L0_xattn_bv, L0_xattn_Er, L0_ffn_Wr, L0_ffn_br, L0_ffn_W1, L0_ffn_b1, L0_ffn_W2, L0_ffn_b2, L0_ffn_W3, L0_ffn_b3, L1_xattn_Wq, L1_xattn_bq, L1_xattn_Wk, L1_xattn_bk, L1_xattn_Wv, L1_xattn_bv, L1_ffn_clip_x, L1_ffn_clip_down, L1_ffn_w_gate, L1_ffn_w_up, L1_ffn_w_down, L2_xattn_WQ, L2_xattn_WK, L2_xattn_WV, L2_xattn_WO, L2_ffn_W1, L2_ffn_b1, L2_ffn_W2, L2_ffn_b2, L2_ffn_Wg, L2_ffn_bg, L3_xattn_gamma_x, L3_xattn_beta_x, L3_xattn_gamma_l, L3_xattn_beta_l, L3_xattn_Wq, L3_xattn_Wkv, L3_xattn_Wo, L3_ffn_gate_w, L3_ffn_Wu, L3_ffn_Wv, L3_ffn_Wo):
    import jax
    import jax.numpy as jnp

    def _L0_xattn_ref(query, key, value, Wq, bq, Wk, bk, Wv, bv, Er):
        import jax, jax.numpy as jnp
        import numpy as np
        import math
        D_MODEL = 128
        NUM_HEADS = 16
        MAX_LEN = 256
        D_HEAD = D_MODEL // NUM_HEADS
        BATCH = 2
        SEQ = 256

        def _skew(QEr):
            B, H, R, C = QEr.shape
            padded = jnp.pad(QEr, ((0, 0), (0, 0), (0, 0), (1, 0)))
            reshaped = padded.reshape(B, H, C + 1, R)
            return reshaped[:, :, 1:, :]
        B, S, D = query.shape
        H, dh = (NUM_HEADS, D_HEAD)
        q = (jnp.einsum('bsd,ed->bse', query, Wq) + bq).reshape(B, S, H, dh).transpose(0, 2, 1, 3)
        k = (jnp.einsum('bsd,ed->bse', key, Wk) + bk).reshape(B, S, H, dh).transpose(0, 2, 1, 3)
        v = (jnp.einsum('bsd,ed->bse', value, Wv) + bv).reshape(B, S, H, dh).transpose(0, 2, 1, 3)
        start = MAX_LEN - S
        Er_s = Er[start:, :]
        QEr = jnp.einsum('bhsd,ld->bhsl', q, Er_s)
        Srel = _skew(QEr)
        QK = jnp.einsum('bhsd,bhtd->bhst', q, k)
        attn = (QK + Srel) / math.sqrt(dh)
        causal = jnp.tril(jnp.ones((S, S), dtype=bool))
        attn = jnp.where(causal[None, None], attn, -jnp.inf)
        attn = jax.nn.softmax(attn, axis=-1)
        out = jnp.einsum('bhst,bhtd->bhsd', attn, v)
        out = out.transpose(0, 2, 1, 3).reshape(B, S, D)
        return out

    def _L0_ffn_ref(x, Wr, br, W1, b1, W2, b2, W3, b3):
        import jax, jax.numpy as jnp
        import numpy as np
        E, D, DFF = (8, 128, 512)
        b, s, d = x.shape
        xt = x.reshape(b * s, d)
        logits = xt @ Wr + br
        pr, idx = jax.lax.top_k(logits, 2)
        w = jax.nn.softmax(pr, axis=-1)
        onehot = jax.nn.one_hot(idx, W1.shape[0], dtype=x.dtype)
        cw = jnp.einsum('tk,tke->te', w, onehot)
        y = jnp.zeros_like(xt)
        for e in range(W1.shape[0]):
            h = jax.nn.silu(xt @ W1[e] + b1[e]) * (xt @ W2[e] + b2[e])
            y = y + (h @ W3[e] + b3[e]) * cw[:, e:e + 1]
        return y.reshape(b, s, d)

    def _L1_xattn_ref(query_states, key_states, value_states, attention_mask, Wq, bq, Wk, bk, Wv, bv):
        import jax, jax.numpy as jnp
        import numpy as np
        import math
        B, L, D, NUM_HEADS = (4, 256, 128, 16)
        HEAD_SIZE = D // NUM_HEADS
        q = jnp.einsum('bld,de->ble', query_states, Wq) + bq
        k = jnp.einsum('bld,de->ble', key_states, Wk) + bk
        v = jnp.einsum('bld,de->ble', value_states, Wv) + bv
        scores = jnp.einsum('bqd,bkd->bqk', q, k) / math.sqrt(HEAD_SIZE)
        scores = scores + (1.0 - attention_mask)[:, None, :] * -10000.0
        probs = jax.nn.softmax(scores, axis=-1)
        context = jnp.einsum('bqk,bkd->bqd', probs, v)
        return context

    def _L1_ffn_ref(x, clip_x, clip_down, w_gate, w_up, w_down):
        import jax, jax.numpy as jnp
        import numpy as np
        QMAX = 127.0

        def _ste_round(v):
            return v + jax.lax.stop_gradient(jnp.round(v) - v)

        def _act_fake_quant(x, clip_factor):
            scale = jax.nn.sigmoid(clip_factor) * jnp.max(jnp.abs(x)) / QMAX
            return jnp.clip(_ste_round(x / scale), -QMAX - 1.0, QMAX) * scale

        def _weight_fake_quant(w):
            scale = jnp.max(jnp.abs(w), axis=1, keepdims=True) / QMAX
            return jnp.clip(_ste_round(w / scale), -QMAX - 1.0, QMAX) * scale
        xq = _act_fake_quant(x, clip_x[0])
        gate = jnp.einsum('bsh,ih->bsi', xq, _weight_fake_quant(w_gate))
        up = jnp.einsum('bsh,ih->bsi', xq, _weight_fake_quant(w_up))
        h = _act_fake_quant(jax.nn.silu(gate) * up, clip_down[0])
        return jnp.einsum('bsi,hi->bsh', h, _weight_fake_quant(w_down))

    def _L2_xattn_ref(x, encoder_output, mask, WQ, WK, WV, WO):
        import jax, jax.numpy as jnp
        import numpy as np
        B, S, D, H = (2, 256, 128, 16)
        DK = D // H
        SQRT_DK = DK ** 0.5
        NEG = -1000000000.0
        b, s, d = x.shape
        q = (x @ WQ).reshape(b, s, H, DK).transpose(0, 2, 1, 3)
        k = (encoder_output @ WK).reshape(b, s, H, DK).transpose(0, 2, 1, 3)
        v = (encoder_output @ WV).reshape(b, s, H, DK).transpose(0, 2, 1, 3)
        scores = jnp.einsum('bhqd,bhkd->bhqk', q, k) / SQRT_DK
        future = jnp.triu(jnp.ones((s, s), jnp.int32), 1)
        m = mask[:, None, :, None] + future[None, None, :, :]
        scores = jnp.where(m != 0, NEG, scores)
        attn = jax.nn.softmax(scores, axis=-1)
        ctx = jnp.einsum('bhqk,bhkd->bqhd', attn, v).reshape(b, s, d)
        return ctx @ WO

    def _L2_ffn_ref(x, W1, b1, W2, b2, Wg, bg):
        import jax, jax.numpy as jnp
        import numpy as np
        B, S, D, H, E = (8, 512, 128, 256, 8)
        logits = jnp.einsum('bsd,de->bse', x, Wg) + bg
        probs = jax.nn.softmax(logits, axis=-1)
        top1 = jnp.argmax(probs, axis=-1)
        out = jnp.zeros_like(x)
        for e in range(E):
            coef = jnp.where(top1 == e, probs[..., e], 0.0)[..., None]
            h = jax.nn.gelu(jnp.einsum('bsd,dh->bsh', x, W1[e]) + b1[e], approximate=False)
            y = jnp.einsum('bsh,hd->bsd', h, W2[e]) + b2[e]
            out = out + coef * y
        return out

    def _L3_xattn_ref(x, latents, gamma_x, beta_x, gamma_l, beta_l, Wq, Wkv, Wo):
        import jax, jax.numpy as jnp
        import numpy as np
        DIM = 128
        HEAD_DIM = 64
        NUM_HEADS = 8
        INNER = HEAD_DIM * NUM_HEADS
        ROT_DIM = HEAD_DIM
        ROPE_BASE = 10000.0
        EPS = 1e-05

        def layer_norm(x, g, b):
            mu = jnp.mean(x, axis=-1, keepdims=True)
            var = jnp.var(x, axis=-1, keepdims=True)
            return (x - mu) * jax.lax.rsqrt(var + EPS) * g + b

        def rope_rotate_k(k):
            n = k.shape[1]
            half = ROT_DIM // 2
            inv_freq = 1.0 / ROPE_BASE ** (jnp.arange(0, ROT_DIM, 2, dtype=jnp.float32) / ROT_DIM)
            theta = jnp.arange(n, dtype=jnp.float32)[:, None] * inv_freq[None, :]
            angles = jnp.concatenate([theta, theta], axis=-1)
            cos = jnp.cos(angles)[None, :, None, :].astype(k.dtype)
            sin = jnp.sin(angles)[None, :, None, :].astype(k.dtype)
            k_rope, k_pass = (k[..., :ROT_DIM], k[..., ROT_DIM:])
            neg_half = jnp.concatenate([-k_rope[..., half:], k_rope[..., :half]], axis=-1)
            k_rope = k_rope * cos + neg_half * sin
            return jnp.concatenate([k_rope, k_pass], axis=-1)
        b, n, _ = x.shape
        m = latents.shape[1]
        h, d = (NUM_HEADS, HEAD_DIM)
        scale = d ** (-0.5)
        xn = layer_norm(x, gamma_x, beta_x)
        ln = layer_norm(latents, gamma_l, beta_l)
        q = (ln @ Wq).reshape(b, m, h, d)
        kv_x = xn @ Wkv
        k_x, v_x = (kv_x[..., :INNER], kv_x[..., INNER:])
        kv_l = ln @ Wkv
        k_l, v_l = (kv_l[..., :INNER], kv_l[..., INNER:])
        k_x = k_x.reshape(b, n, h, d)
        v_x = v_x.reshape(b, n, h, d)
        k_x = rope_rotate_k(k_x)
        q = jnp.transpose(q, (0, 2, 1, 3)) * scale
        k_x = jnp.transpose(k_x, (0, 2, 1, 3))
        v_x = jnp.transpose(v_x, (0, 2, 1, 3))
        k_l = jnp.transpose(k_l.reshape(b, m, h, d), (0, 2, 1, 3))
        v_l = jnp.transpose(v_l.reshape(b, m, h, d), (0, 2, 1, 3))
        k = jnp.concatenate([k_x, k_l], axis=2)
        v = jnp.concatenate([v_x, v_l], axis=2)
        sim = jnp.einsum('bhid,bhjd->bhij', q, k)
        attn = jax.nn.softmax(sim, axis=-1)
        out = jnp.einsum('bhij,bhjd->bhid', attn, v)
        out = jnp.transpose(out, (0, 2, 1, 3)).reshape(b, m, INNER)
        return out @ Wo

    def _L3_ffn_ref(x, gate_w, Wu, Wv, Wo):
        import jax, jax.numpy as jnp
        import numpy as np
        B, N, D, E, R, K = (4, 256, 128, 8, 32, 2)
        logits = jnp.einsum('bnd,de->bne', x, gate_w)
        topv, topi = jax.lax.top_k(logits, K)
        w = jax.nn.softmax(topv, axis=-1)
        u = jnp.einsum('bnd,edr->bner', x, Wu)
        v = jnp.einsum('bnd,edr->bner', x, Wv)
        s = jax.nn.silu(u) * v
        Y = jnp.einsum('bner,erd->bned', s, Wo)
        y_sel = jnp.take_along_axis(Y, topi[..., None], axis=2)
        out = jnp.einsum('bnkd,bnk->bnd', y_sel, w)
        return out
    x = x + jnp.tanh(g_xattn[0]) * _L0_xattn_ref(_layernorm(x, axis=-1), ctx_1024, ctx_1024, L0_xattn_Wq, L0_xattn_bq, L0_xattn_Wk, L0_xattn_bk, L0_xattn_Wv, L0_xattn_bv, L0_xattn_Er)
    x = x + jnp.tanh(g_ffn[0]) * _L0_ffn_ref(_layernorm(x, axis=-1), L0_ffn_Wr, L0_ffn_br, L0_ffn_W1, L0_ffn_b1, L0_ffn_W2, L0_ffn_b2, L0_ffn_W3, L0_ffn_b3)
    x = x + jnp.tanh(g_xattn[1]) * _L1_xattn_ref(_layernorm(x, axis=-1), ctx_1024, ctx_1024, mask_BxS2_ff1, L1_xattn_Wq, L1_xattn_bq, L1_xattn_Wk, L1_xattn_bk, L1_xattn_Wv, L1_xattn_bv)
    x = x + jnp.tanh(g_ffn[1]) * _L1_ffn_ref(_layernorm(x, axis=-1), L1_ffn_clip_x, L1_ffn_clip_down, L1_ffn_w_gate, L1_ffn_w_up, L1_ffn_w_down)
    x = x + jnp.tanh(g_xattn[2]) * _L2_xattn_ref(_layernorm(x, axis=-1), ctx_1024, mask_BxS2_ik0, L2_xattn_WQ, L2_xattn_WK, L2_xattn_WV, L2_xattn_WO)
    x = x + jnp.tanh(g_ffn[2]) * _L2_ffn_ref(_layernorm(x, axis=-1), L2_ffn_W1, L2_ffn_b1, L2_ffn_W2, L2_ffn_b2, L2_ffn_Wg, L2_ffn_bg)
    x = x + jnp.tanh(g_xattn[3]) * _L3_xattn_ref(ctx_1024, _layernorm(x, axis=-1), L3_xattn_gamma_x, L3_xattn_beta_x, L3_xattn_gamma_l, L3_xattn_beta_l, L3_xattn_Wq, L3_xattn_Wkv, L3_xattn_Wo)
    x = x + jnp.tanh(g_ffn[3]) * _L3_ffn_ref(_layernorm(x, axis=-1), L3_ffn_gate_w, L3_ffn_Wu, L3_ffn_Wv, L3_ffn_Wo)
    return x

_drawn_inputs = setup_inputs


def setup_inputs(seed=0):
    import zlib

    import numpy as np

    out = dict(_drawn_inputs(seed))
    spreads = {'L0_ffn_br': (0.0, 0.1),
     'L0_ffn_b1': (0.0, 0.8),
     'L0_ffn_b2': (0.0, 0.8),
     'L0_ffn_b3': (0.0, 0.1),
     'L1_xattn_bq': (0.0, 0.1),
     'L1_xattn_bk': (0.0, 2.0),
     'L1_xattn_bv': (0.0, 0.1),
     'L2_ffn_b1': (0.0, 0.8),
     'L2_ffn_b2': (0.0, 0.8),
     'L2_ffn_bg': (0.0, 0.8),
     'L3_xattn_gamma_x': (1.0, 0.6),
     'L3_xattn_beta_x': (0.0, 1.571),
     'L3_xattn_gamma_l': (1.0, 0.6),
     'L3_xattn_beta_l': (0.0, 0.8)}
    factors = {'g_ffn': 8.0,
     'L0_xattn_bk': 64.0,
     'L0_ffn_W1': 8.0,
     'L0_ffn_W2': 8.0,
     'L0_ffn_W3': 7.269,
     'L1_ffn_w_gate': 8.0,
     'L1_ffn_w_up': 8.0,
     'L1_ffn_w_down': 8.0,
     'L2_ffn_W1': 8.0,
     'L2_ffn_W2': 8.0,
     'L2_ffn_Wg': 6.353,
     'L3_ffn_gate_w': 8.0,
     'L3_ffn_Wu': 8.0,
     'L3_ffn_Wv': 8.0,
     'L3_ffn_Wo': 8.0,
     'L3_xattn_Wq': 3.919}
    for name, (base, spread) in spreads.items():
        noise = np.random.default_rng([zlib.crc32(name.encode()), seed]).standard_normal(out[name].shape)
        drawn = base * np.exp(spread * noise) if base else spread * noise
        out[name] = jnp.asarray(drawn.astype(out[name].dtype))
    for name, factor in factors.items():
        out[name] = (out[name] * factor).astype(out[name].dtype)
    return out
```

```python
from contextlib import ExitStack

import concourse.bass as bass
import numpy as np
from concourse import mybir

F32 = mybir.dt.float32
BF16 = mybir.dt.bfloat16
U32 = mybir.dt.uint32
I32 = mybir.dt.int32
ALU = mybir.AluOpType
ACT = mybir.ActivationFunctionType
AX = mybir.AxisListType
RMAX = bass.bass_isa.ReduceOp.max

P = 128
NB, S, D = 4, 256, 128
NT = NB * S // P
TOK = NB * S
NH, DH = 16, 8
NPART = 3
STACK = NPART * NPART * DH
E = 8
NH3, DH3 = 8, 64
CI, NI = 88, 4
EPS = 1e-5
BIG = 1e30
ROUND = 1.5 * 2.0 ** 23
QMAX = 127.0
LEAD = 8
STAGE, SKEW = 4, 8
SLICE8 = float(DH) ** -0.5

UNITS8 = [(t, h, (4, 2)[t % 2], (128, 256)[t % 2]) for t in range(NT) for h in range(0, NH, (4, 2)[t % 2])]
UNITS1 = [(2 * b, 0, 2, 256) for b in range(NB)]
UNITS3 = [(t, h, 1, 512) for t in range(NT) for h in range(NH3)]
N8, N1, N3 = len(UNITS8), len(UNITS1), len(UNITS3)
BASE = {0: 0, 1: N8, 2: N8 + N1, 3: 2 * N8 + N1}
UNITS = {0: UNITS8, 1: UNITS1, 2: UNITS8, 3: UNITS3}
LAST = {k: [i for i, u in enumerate(v) if i + 1 == len(v) or v[i + 1][0] != u[0]] for k, v in UNITS.items()}
GROUPS = {0: 0, 1: 8, 2: 12, 3: 20}
COPIER = ["V"] * (2 * N8 + N1) + ["AV"[i % 2] for i in range(N3)]


def _plan_misc():
    m = []

    def add(name, n, who):
        m.extend((f"{name}.{i}", who) for i in range(n))

    add("k0", 2, "A"); add("v0", 2, "V")
    add("ln0", 2, "A"); add("q0", 2, "A"); add("qer", N8, "A")
    add("ln1", 2, "A"); add("router0", 1, "V"); add("cwT0", 2, "V"); add("bias0", 2, "V")
    add("k1", 2, "A"); add("v1", 2, "V"); add("ln2", 2, "A"); add("q1", 2, "A")
    add("wgT", 1, "V"); add("wuT", 1, "V"); add("wdT", 1, "V"); add("wdrow", 1, "V")
    add("ln3", 2, "A")
    add("k2", 2, "A"); add("v2", 2, "V"); add("mean", 2, "V"); add("ln4", 2, "A"); add("q2", 2, "A")
    add("oT2", 2, "A"); add("wo2", 2, "V")
    add("ln5", 2, "A"); add("router2", 1, "V"); add("cwT2", 2, "V"); add("bias2", 2, "V")
    add("lnc", 2, "V")
    for c in range(4):
        for n in range(2):
            m.append((f"kc.{c}.{n}", "V")); m.append((f"kr.{c}.{n}", "V"))
    for t in range(NT):
        m.append((f"vc.{t}", "AV"[t % 2]))
    add("ln8", 2, "V")
    for c in range(4):
        for n in range(2):
            m.append((f"kl.{c}.{n}", "A")); m.append((f"q3.{c}.{n}", "A"))
    for t in range(NT):
        m.append((f"vl.{t}", "AV"[t % 2]))
    for i in range(N3 + 6):
        if i - 3 in LAST[3]:
            m.append((f"oT3.{LAST[3].index(i - 3)}", "A"))
        if i - 4 in LAST[3]:
            m.append((f"wo3.{LAST[3].index(i - 4)}", "V"))
    add("ln9", 2, "A"); add("router3", 1, "V")
    for t in range(NT + 2):
        if t < NT:
            m.append((f"uv.{t}", "V"))
        if 1 <= t <= NT:
            m.append((f"sT.{t - 1}", "A"))
        if t >= 2:
            m.append((f"y3.{t - 2}", "V"))
    return m


MISC = _plan_misc()
AT = {name: i for i, (name, _) in enumerate(MISC)}
EMPTIED = [sum(w == who for _, w in MISC[:i + 1]) for i, (_, who) in enumerate(MISC)]


def build(nc, I, out):
    with ExitStack() as ctx:
        def sb(name, shape, dt=F32):
            return ctx.enter_context(nc.sbuf_tensor(name, shape, dt))

        def sem(name):
            return ctx.enter_context(nc.semaphore(name))

        def dram(name, shape, dt):
            return nc.dram_tensor(name, shape, dt, kind="Internal").ap()

        x = sb("x", [P, NT, D])
        ctxr = sb("ctxr", [P, NT, D])
        ctxT = sb("ctxT", [P, TOK])
        xn = sb("xn", [P, NT, D])
        xnT = sb("xnT", [P, TOK])
        cnT = sb("cnT", [P, TOK])
        arenaA = sb("arenaA", [P, 16384])
        QS = arenaA[0:STACK, 0:8192].bitcast(BF16).rearrange("p (h t) -> p h t", h=NH)
        KS = arenaA[0:STACK, 8192:16384].bitcast(BF16).rearrange("p (h t) -> p h t", h=NH)
        KT3 = arenaA[:, 0:8192].rearrange("p (c b k) -> p c b k", c=4, b=NB)
        QT3 = arenaA[:, 8192:8192 + 4096].rearrange("p (c t) -> p c t", c=4)
        arenaB = sb("arenaB", [P, 8320])
        stage = arenaB[:, 0:STAGE * 512].rearrange("p (n w) -> p n w", n=STAGE)
        skewed = arenaB[:, STAGE * 512:(STAGE + SKEW) * 512].rearrange("p (n w) -> p n w", n=SKEW)
        hid = arenaB[:, 0:8192].rearrange("p (n c t) -> p n c t", n=2, c=4)
        h1 = arenaB[:, 0:4096].rearrange("p (c t) -> p c t", c=NI)
        h1q = arenaB[:, 4096:6144].bitcast(BF16).rearrange("p (c t) -> p c t", c=NI)
        VX = arenaB[:, 0:8320].rearrange("p (k h e) -> p k h e", k=16, h=NH3)
        ring = sb("ring", [P, 2, 1536])
        W1r = ring[:, :, 0:512]
        W2r = ring[:, :, 512:1024]
        W3r = ring[:, :, 1024:1536].rearrange("p n (c d) -> p n c d", c=4)
        W1s = ring[:, :, 0:256]
        W2s = ring[:, :, 256:512].rearrange("p n (c d) -> p n c d", c=2)
        qparts = ring[:, 0, :].bitcast(BF16).rearrange("p (a t) -> p a t", a=NPART)
        kparts = ring[:, 1, :].bitcast(BF16).rearrange("p (a t) -> p a t", a=NPART)
        qkf = sb("qkf", [P, 2, TOK])
        qf, kf = qkf[:, 0, :], qkf[:, 1, :]
        rope = qkf[:, :, :].rearrange("p a (n t) -> p a n t", n=2)
        V9 = sb("V9", [P, NT, NH, DH + 1])
        VA = sb("VA", [P, NT, D + 1])
        Sx = sb("Sx", [P, 2, 512])
        PR = sb("PR", [P, 2, 512])
        PT = sb("PT", [P, 2, 512])
        sg = sb("sg", [P, 2, 512])
        stage3 = sb("stage3", [P, 512])
        xq = sb("xq", [P, TOK], BF16)
        ones = sb("ones", [P, P])
        identb = sb("identb", [P, P], BF16)
        maskb = sb("maskb", [P, 2, 512], BF16)
        erp = sb("erp", [DH, NPART, S], BF16)
        erf = sb("erf", [DH, S])
        ES = sb("ES", [STACK, S], BF16)
        mrow = sb("mrow", [1, TOK])
        mk2 = sb("mk2", [P, NT])
        mean = sb("mean", [P, NB, NH, DH + 1])
        cwT = sb("cwT", [E, TOK])
        tg = sb("tg", [P, 8])
        small = sb("small", [P, 64])
        nbq0, nbq1 = small[:, 0:1], small[:, 1:2]
        amx, sx, isx, gx = small[:, 2:3], small[:, 3:4], small[:, 4:5], small[:, 5:6]
        amh, sh, ish, fac = small[:, 6:7], small[:, 7:8], small[:, 8:9], small[:, 9:10]
        amxg, amhg = small[:, 10:11], small[:, 11:12]
        sg2 = small[:, 12:14]
        wgs, wus, wds = small[0:CI, 16:20], small[0:CI, 20:24], small[:, 24:25]
        iwg, iwu, iwd = small[0:CI, 28:32], small[0:CI, 32:36], small[:, 36:37]
        fg, fu = small[0:CI, 40:44], small[0:CI, 44:48]
        mhalf = sb("mhalf", [P, NT])
        st = sb("st", [P, NT, 6])
        mv = sb("mv", [P, NT, 2])
        veps = sb("veps", [P, NT])
        rstd = sb("rstd", [P, NT])
        smin = sb("smin", [P, 2, 4])
        rsum = sb("rsum", [P, NH])
        lg = sb("lg", [P, NT, E])
        lmx = sb("lmx", [P, NT, 8])
        lix = sb("lix", [P, NT, 8], U32)
        lixf = sb("lixf", [P, NT, 8])
        rw = sb("rw", [P, 4, NT])
        oh = sb("oh", [P, 2, NT, E])
        cw = sb("cw", [P, NT, E])
        wgT = sb("wgT", [P, NI * CI], BF16)
        wuT = sb("wuT", [P, NI * CI], BF16)
        wdT = sb("wdT", [CI, NI, D], BF16)
        wdrow = sb("wdrow", [P, D])
        diag = sb("diag", [P, P])
        loads = {}

        def load(name, shape, dt=F32):
            loads[name] = (sb("in_" + name, shape, dt), sem("ld_" + name))
            return loads[name][0]

        ident = load("ident", [P, P]); maskf = load("maskf", [P, P]); iota = load("iota", [P, E])
        cos = load("cos", [P, S]); sin = load("sin", [P, S])
        gates = load("gates", [P, 8]); clips = load("clips", [P, 2])
        wq0 = load("wq0", [D, D]); wk0 = load("wk0", [D, D]); wv0 = load("wv0", [D, D])
        b0 = load("b0", [D, 2]); bv0 = load("bv0", [P, D])
        wq1 = load("wq1", [D, D]); wk1 = load("wk1", [D, D]); wv1 = load("wv1", [D, D])
        b1 = load("b1", [D, 2]); bv1 = load("bv1", [P, D])
        wq2 = load("wq2", [D, D]); wk2 = load("wk2", [D, D]); wv2 = load("wv2", [D, D]); wo2 = load("wo2", [D, D])
        maski = load("maski", [P, NT], I32)
        wr0 = load("wr0", [D, E]); br0 = load("br0", [P, E])
        hb1 = load("hb1", [P, E, 4]); hb2 = load("hb2", [P, E, 4]); hb3 = load("hb3", [E, D])
        wr2 = load("wr2", [D, E]); br2 = load("br2", [P, E])
        gb1 = load("gb1", [P, E, 2]); gb2 = load("gb2", [E, D])
        wg = load("wg", [CI, NI, D]); wu = load("wu", [CI, NI, D]); wd = load("wd", [D, NI * CI])
        lnp = load("lnp", [D, 4])
        wr3 = load("wr3", [D, E])

        def load_late(name, at, n):
            loads[name] = (arenaA[:, 12288 + at:12288 + at + n], sem("ld_" + name))
            return loads[name][0]

        wq3, wkv3, wkr3 = load_late("wq3", 0, 512), load_late("wkv3", 512, 1024), load_late("wkr3", 1536, 512)
        wo3 = load_late("wo3", 2048, 512).rearrange("p (c d) -> p c d", c=4)
        wuv = load_late("wuv", 2560, 512)
        wf3 = load_late("wf3", 3072, 256).rearrange("p (c d) -> p c d", c=2)

        ps = ctx.enter_context(nc.psum_tensor("ps", [P, 8, 512], F32))
        SC = [ps[:, 0, :], ps[:, 1, :]]
        TP = [ps[:, 2, :], ps[:, 3, :]]
        OB = [ps[:, 4, :], ps[:, 5, :]]
        MB = [ps[:, 6, :], ps[:, 7, :]]

        relpos = dram("relpos", (N8, P, 512), F32)
        qpd = dram("qpd", (2, NPART, P, TOK), BF16)
        kpd = dram("kpd", (2, NPART, P, TOK), BF16)

        ld_x, ld_ctx, ld_ctxT, ld_er, ld_mrow = (sem("ld_" + n) for n in ("x", "ctx", "ctxT", "er", "mrow"))
        stats_ready, moments_ready, variance_ready = sem("stats_ready"), sem("moments_ready"), sem("variance_ready")
        rstd_ready, rows_normed, x_updated = sem("rstd_ready"), sem("rows_normed"), sem("x_updated")
        misc_ready, misc_emptied_v, misc_emptied_a = sem("misc_ready"), sem("misc_emptied_v"), sem("misc_emptied_a")
        v_step, a_step, g_step = sem("v_step"), sem("a_step"), sem("g_step")
        constants_ready = sem("constants_ready")
        nbq_ready, gates_ready, sig_exp, pool_consts = sem("nbq_ready"), sem("gates_ready"), sem("sig_exp"), sem("pool_consts")
        kparts_ready, qparts_ready, erparts_ready = sem("kparts_ready"), sem("qparts_ready"), sem("erparts_ready")
        kp_stored, qp_stored = sem("kp_stored"), sem("qp_stored")
        ks_loaded, qs_loaded, es_loaded = sem("ks_loaded"), sem("qs_loaded"), sem("es_loaded")
        rel_stored = [sem(f"rel_stored{i}") for i in range(STAGE)]
        rel_loaded = [sem(f"rel_loaded{i}") for i in range(SKEW)]
        rel_masked = sem("rel_masked")
        scores_ready, min_ready, probs_ready = sem("scores_ready"), sem("min_ready"), sem("probs_ready")
        probsT_ready, pv_done, out_read = sem("probsT_ready"), sem("pv_done"), sem("out_read")
        probsT_copied = {"V": sem("probsT_copied_v"), "A": sem("probsT_copied_a")}
        mask_ready = sem("mask_ready")
        weights_scaled = sem("weights_scaled")
        xmax_ready, xmax_all, xq_ready = sem("xmax_ready"), sem("xmax_all"), sem("xq_ready")
        hmax_ready, hmax_all, hq_ready = sem("hmax_ready"), sem("hmax_all"), sem("hq_ready")
        l1_gate, l1_silu, l1_up, l1_hidden, l1_down = (sem("l1_" + n) for n in ("gate", "silu", "up", "hidden", "down"))
        router_in, router_exp, cw_ready = sem("router_in"), sem("router_exp"), sem("cw_ready")
        moe = {l: {n: sem(f"moe{l}_{n}") for n in ("gate", "act", "up", "hidden", "down", "summed", "slot0", "slot1")}
               for l in (0, 2)}
        rope_in, rope_done, vones = sem("rope_in"), sem("rope_done"), sem("vones")
        heads_ready = sem("heads_ready")
        silu3, s3_ready, out_ready, out_stored = sem("silu3"), sem("s3_ready"), sem("out_ready"), sem("out_stored")

        block = ctx.enter_context(nc.Block())

        def loaded(eng, *names):
            for n in names:
                eng.wait_ge(loads[n][1], 16)

        def emptied(eng, name):
            i = AT[name]
            eng.wait_ge(misc_emptied_v if MISC[i][1] == "V" else misc_emptied_a, EMPTIED[i])

        def filled(eng, name):
            eng.wait_ge(misc_ready, AT[name] + 1)
            return MB[AT[name] % 2]

        def copied(eng, u):
            eng.wait_ge(probsT_copied[COPIER[u]], sum(c == COPIER[u] for c in COPIER[:u + 1]))

        def bc(ap, n):
            return ap.unsqueeze(2).to_broadcast([ap.shape[0], ap.shape[1], n])

        @block.sync
        def _(sp):
            def fetch(name, ap):
                sp.dma_start(loads[name][0][:], ap).then_inc(loads[name][1], 16)

            sp.dma_start(x[:], I["x"].rearrange("(t p) d -> p t d", p=P)).then_inc(ld_x, 16)
            sp.dma_start(ctxT[:], I["ctxT"]).then_inc(ld_ctxT, 16)
            for n in ("wk0", "b0", "ident", "wv0"):
                fetch(n, I[n])
            fetch("bv0", I["bv0"].partition_broadcast(P))
            sp.dma_start(erf[:], I["erT"]).then_inc(ld_er, 16)
            for n in ("wq0", "iota", "maskf"):
                fetch(n, I[n])
            fetch("gates", I["gates"].partition_broadcast(P))
            fetch("clips", I["clips"].partition_broadcast(P))
            for n in ("wq1", "wk1", "wv1", "b1", "wq2", "wk2", "wv2", "wo2", "maski", "wr0", "hb1", "hb2",
                      "hb3", "wr2", "gb1", "gb2", "wg", "wu", "wd"):
                fetch(n, I[n])
            for n in ("bv1", "br0", "br2"):
                fetch(n, I[n].partition_broadcast(P))
            sp.dma_start(mrow[:], I["mrow"]).then_inc(ld_mrow, 16)

            def restack(parts_ready, parts, store, stored, stack, stack_loaded, n, key):
                sp.wait_ge(parts_ready, n + 1)
                sp.dma_start(store[n].rearrange("a p t -> p a t"), parts).then_inc(stored, 16)
                sp.wait_ge(stored, 16 * (n + 1))
                for c in range(NPART * NPART):
                    a = c % NPART if key else c // NPART
                    sp.dma_start(stack[c * DH:(c + 1) * DH],
                                 store[n, a].rearrange("(h d) t -> d h t", d=DH)).then_inc(stack_loaded, 16)

            def experts(layer, e):
                s = e % 2
                m = moe[layer]
                if e >= 2:
                    sp.wait_ge(m["down"], 2 * (e - 1))
                if layer == 0:
                    sp.dma_start(W1r[:, s], I["f1"][e]).then_inc(m[f"slot{s}"], 16)
                    sp.dma_start(W2r[:, s], I["f2"][e]).then_inc(m[f"slot{s}"], 16)
                    sp.dma_start(W3r[:, s], I["f3"][e].rearrange("(c p) d -> p c d", p=P)).then_inc(m[f"slot{s}"], 16)
                else:
                    sp.dma_start(W1s[:, s], I["g1"][e]).then_inc(m[f"slot{s}"], 16)
                    sp.dma_start(W2s[:, s], I["g2"][e].rearrange("(c p) d -> p c d", p=P)).then_inc(m[f"slot{s}"], 16)

            sp.wait_ge(erparts_ready, 1)
            for c in range(NPART * NPART):
                sp.dma_start(ES[c * DH:(c + 1) * DH, :], erp[:, c % NPART, :]).then_inc(es_loaded, 16)
            restack(kparts_ready, kparts, kpd, kp_stored, KS, ks_loaded, 0, True)
            restack(qparts_ready, qparts, qpd, qp_stored, QS, qs_loaded, 0, False)

            def store_rel(r):
                emptied(sp, f"qer.{r}")
                sp.dma_start(relpos[r], stage[:, r % STAGE, :]).then_inc(rel_stored[r % STAGE], 16)

            def load_rel(r):
                w = UNITS8[r][3]
                sp.wait_ge(rel_stored[r % STAGE], 16 * (r // STAGE + 1))
                if r >= SKEW:
                    sp.wait_ge(min_ready, r - SKEW + 1)
                src = bass.AP(relpos.tensor, relpos[r].offset + P - 1, [[512 - 1, P], [w, 512 // w], [1, w]])
                sp.dma_start(skewed[:, r % SKEW, :].rearrange("p (g w) -> p g w", w=w), src) \
                    .then_inc(rel_loaded[r % SKEW], 16)

            for r in range(N8 + 1):
                if r < N8:
                    store_rel(r)
                if r >= 1:
                    load_rel(r - 1)
                if r == 4:
                    sp.wait_ge(qs_loaded, 16 * 9)
                    sp.wait_ge(ks_loaded, 16 * 9)
                    experts(0, 0)
                    experts(0, 1)
            sp.dma_start(ctxr[:], I["ctx"].rearrange("(t p) d -> p t d", p=P)).then_inc(ld_ctx, 16)
            for n in ("cos", "sin", "lnp", "wr3"):
                fetch(n, I[n])
            for e in range(2, E):
                experts(0, e)
            restack(kparts_ready, kparts, kpd, kp_stored, KS, ks_loaded, 1, True)
            restack(qparts_ready, qparts, qpd, qp_stored, QS, qs_loaded, 1, False)
            sp.wait_ge(ks_loaded, 16 * 18)
            sp.wait_ge(qs_loaded, 16 * 18)
            experts(2, 0)
            experts(2, 1)
            sp.wait_ge(scores_ready, BASE[3])
            for n in ("wq3", "wkv3", "wkr3", "wo3", "wuv", "wf3"):
                fetch(n, I[n])
            for e in range(2, E):
                experts(2, e)
            for t in range(NT):
                sp.wait_ge(x_updated, 8 * NT - NT + t + 1)
                sp.dma_start(out[t * P:(t + 1) * P, :], x[:, t, :]).then_inc(out_stored, 16)
            sp.wait_ge(out_stored, 16 * NT)

        @block.gpsimd
        def _(pool):
            nc.gpsimd.memset(ones[:], 1.0).then_inc(pool_consts, 1)
            nc.gpsimd.memset(mhalf[:], -0.5).then_inc(pool_consts, 1)
            nc.gpsimd.memset(V9[:, :, :, DH:DH + 1], 1.0).then_inc(pool_consts, 1)
            nc.gpsimd.memset(VA[:, :, D:D + 1], 1.0).then_inc(pool_consts, 1)
            nc.gpsimd.memset(amh, 0.0).then_inc(pool_consts, 1)

            count = [0]

            def link(ins):
                count[0] += 1
                ins.then_inc(g_step, 1)
                pool.wait_ge(g_step, count[0])

            def rsqrt(n):
                if n == 0:
                    pool.wait_ge(pool_consts, 2)
                pool.wait_ge(variance_ready, n + 1)
                nc.gpsimd.tensor_tensor(rstd[:], veps[:], mhalf[:], ALU.pow).then_inc(rstd_ready, 1)

            def split_keys(n, names):
                for name in names:
                    emptied(pool, name)
                link(nc.gpsimd.tensor_copy(kparts[:, 0, :], kf))
                link(nc.gpsimd.tensor_tensor(kf, kf, kparts[:, 0, :], ALU.subtract))
                link(nc.gpsimd.tensor_copy(kparts[:, 1, :], kf))
                nc.gpsimd.tensor_tensor(kparts[:, 2, :], kf, kparts[:, 1, :], ALU.subtract).then_inc(kparts_ready, 1)

            rsqrt(0)
            split_keys(0, ("k0.0", "k0.1"))
            for r in range(N8):
                w = UNITS8[r][3]
                pool.wait_ge(rel_loaded[r % SKEW], 16 * (r // SKEW + 1))
                v = skewed[:, r % SKEW, :].rearrange("p (g w) -> p g w", w=w)[:, :, w - P:w]
                nc.gpsimd.affine_select(out=v, in_=v, pattern=[[0, 512 // w], [-1, P]], compare_op=ALU.is_ge,
                                        fill=BIG, base=0, channel_multiplier=1).then_inc(rel_masked, 1)
            for n in (1, 2, 3):
                rsqrt(n)
            pool.wait_ge(xmax_ready, 1)
            nc.gpsimd.partition_all_reduce(amxg, amx, P, RMAX).then_inc(xmax_all, 1)
            pool.wait_ge(hmax_ready, 1)
            nc.gpsimd.partition_all_reduce(amhg, amh, P, RMAX).then_inc(hmax_all, 1)
            split_keys(1, ("k2.0", "k2.1"))
            rsqrt(4)
            rsqrt(5)
            rsqrt(6)
            pool.wait_ge(moe[2]["down"], 2 * E)
            nc.gpsimd.memset(VX[:, :, :, DH3:DH3 + 1], 1.0).then_inc(vones, 1)
            for k in range(8):
                c, n = k // 2, k % 2
                pool.wait_ge(rope_in, k + 1)
                nc.gpsimd.tensor_tensor(KT3[:, c, 2 * n:2 * n + 2, 0:S],
                                        rope[:, 0, k % 2, :].rearrange("p (b t) -> p b t", b=2),
                                        rope[:, 1, k % 2, :].rearrange("p (b t) -> p b t", b=2),
                                        ALU.add).then_inc(rope_done, 1)
            rsqrt(7)
            rsqrt(8)
            rsqrt(9)

        @block.scalar
        def _(act):
            loaded(act, "gates", "clips")
            nc.scalar.activation(tg[:], gates[:], ACT.Tanh).then_inc(gates_ready, 1)
            nc.scalar.activation(sg2, clips[:], ACT.Exp, scale=-1.0).then_inc(sig_exp, 1)

            def take(name, dst, func=ACT.Copy, **kw):
                bank = filled(act, name)
                nc.scalar.activation(dst, bank, func, **kw).then_inc(misc_emptied_a, 1)

            def halves(name, dst, func=ACT.Copy, **kw):
                for n in range(2):
                    take(f"{name}.{n}", dst[:, 512 * n:512 * n + 512], func, **kw)

            def rel(r):
                if r >= STAGE:
                    act.wait_ge(rel_stored[r % STAGE], 16 * (r // STAGE))
                take(f"qer.{r}", stage[:, r % STAGE, :])

            def exps(layer, i):
                _, _, g, w = UNITS[layer][i]
                u = BASE[layer] + i
                act.wait_ge(min_ready, u + 1)
                if u >= 2:
                    act.wait_ge(probsT_ready, u - 1)
                src = Sx[:, u % 2, :] if layer == 0 else SC[u % 2]
                for k in range(g):
                    ins = nc.scalar.activation(PR[:, u % 2, k * w:(k + 1) * w], src[:, k * w:(k + 1) * w], ACT.Exp,
                                               bias=smin[:, u % 2, k:k + 1], scale=-1.0)
                ins.then_inc(probs_ready, 1)

            def copy_probs(layer, i):
                u = BASE[layer] + i
                if COPIER[u] == "A":
                    act.wait_ge(probsT_ready, u + 1)
                    if u >= 2:
                        act.wait_ge(pv_done, u - 1)
                    nc.scalar.activation(PT[:, u % 2, :], TP[u % 2], ACT.Copy).then_inc(probsT_copied["A"], 1)

            def attention(layer):
                for i in range(len(UNITS[layer]) + 5):
                    if layer == 0 and i + LEAD < N8:
                        rel(i + LEAD)
                    if i < len(UNITS[layer]):
                        exps(layer, i)
                    if 1 <= i <= len(UNITS[layer]):
                        copy_probs(layer, i - 1)
                    if layer == 3 and i - 3 in LAST[3]:
                        t = LAST[3].index(i - 3)
                        if t >= 1:
                            emptied(act, f"wo3.{t - 1}")
                        take(f"oT3.{t}", sg[:, 0, :])

            def experts(layer, nch, func, bias):
                m = moe[layer]
                for j in range(E * nch * 2):
                    e, c, n = j // (2 * nch), j // 2 % nch, j % 2
                    act.wait_ge(m["gate"], j + 1)
                    if layer == 0:
                        if j >= 2:
                            act.wait_ge(m["hidden"], j - 1)
                        nc.scalar.activation(sg[:, j % 2, :], SC[j % 2], func,
                                             bias=bias[:, e, c:c + 1]).then_inc(m["act"], 1)
                    else:
                        if e >= 2:
                            act.wait_ge(m["down"], 2 * (e - 1))
                        nc.scalar.activation(hid[:, e % 2, c, 512 * n:512 * n + 512], SC[j % 2], func,
                                             bias=bias[:, e, c:c + 1]).then_inc(m["hidden"], 1)

            def router(n):
                act.wait_ge(router_in, n + 1)
                if n == 1:
                    nc.scalar.activation(lg[:], lg[:], ACT.Exp).then_inc(router_exp, 1)
                else:
                    nc.scalar.activation(rw[:, 1, :], rw[:, 0, :], ACT.Exp).then_inc(router_exp, 1)

            loaded(act, "b0")
            halves("k0", kf, ACT.Identity, bias=b0[:, 1:2])
            halves("ln0", xnT)
            act.wait_ge(nbq_ready, 1)
            halves("q0", qf, ACT.Identity, bias=nbq0, scale=-SLICE8)
            for r in range(LEAD):
                rel(r)
            attention(0)
            halves("ln1", xnT)
            router(0)
            loaded(act, "hb1")
            experts(0, 4, ACT.Silu, hb1)
            loaded(act, "b1")
            halves("k1", kf, ACT.Identity, bias=b1[:, 1:2])
            halves("ln2", xnT)
            act.wait_ge(nbq_ready, 2)
            halves("q1", qf, ACT.Identity, bias=nbq1, scale=-SLICE8)
            attention(1)
            halves("ln3", xnT)
            for j in range(2 * NI):
                act.wait_ge(l1_gate, j + 1)
                if j >= 2:
                    act.wait_ge(l1_hidden, j - 1)
                if j == 0:
                    act.wait_ge(xq_ready, 1)
                nc.scalar.activation(sg[0:CI, j % 2, :], SC[j % 2][0:CI, :], ACT.Silu,
                                     scale=fg[:, j // 2:j // 2 + 1]).then_inc(l1_silu, 1)
            halves("k2", kf)
            halves("ln4", xnT)
            halves("q2", qf, scale=-SLICE8)
            attention(2)
            halves("oT2", xnT)
            halves("ln5", xnT)
            router(1)
            loaded(act, "gb1")
            experts(2, 2, ACT.Gelu, gb1)
            act.wait_ge(vones, 1)

            def values(kind):
                for t in range(0, NT, 2):
                    k = 4 * (t // 2) + 2 * (kind == "vl")
                    bank = filled(act, f"{kind}.{t}")
                    nc.scalar.activation(VX[:, k, :, 0:DH3], bank.rearrange("p (h e) -> p h e", h=NH3),
                                         ACT.Copy).then_inc(misc_emptied_a, 1)

            values("vc")
            for c in range(4):
                for n in range(2):
                    bank = filled(act, f"kl.{c}.{n}")
                    nc.scalar.activation(KT3[:, c, 2 * n:2 * n + 2, S:2 * S], bank.rearrange("p (b t) -> p b t", b=2),
                                         ACT.Copy).then_inc(misc_emptied_a, 1)
                    take(f"q3.{c}.{n}", QT3[:, c, 512 * n:512 * n + 512], scale=-float(DH3) ** -0.5)
            values("vl")
            attention(3)
            halves("ln9", xnT)
            router(2)
            for t in range(NT + 2):
                if t < NT:
                    bank = filled(act, f"uv.{t}")
                    if t >= 2:
                        act.wait_ge(s3_ready, t - 1)
                    nc.scalar.activation(sg[:, t % 2, 0:256], bank[:, 0:256], ACT.Silu).then_inc(silu3, 1)
                if 1 <= t <= NT:
                    bank = filled(act, f"sT.{t - 1}")
                    if t - 1 >= 2:
                        filled(act, f"y3.{t - 3}")
                    nc.scalar.activation(PT[:, (t - 1) % 2, 0:256], bank[:, 0:256], ACT.Copy).then_inc(misc_emptied_a, 1)

        @block.vector
        def _(dve):
            count = [0]

            def link(ins):
                count[0] += 1
                ins.then_inc(v_step, 1)
                dve.wait_ge(v_step, count[0])

            def norm_rows(n, src, k=None, ready=None):
                for t in range(NT):
                    if k is not None and k > 0:
                        dve.wait_ge(x_updated, NT * (k - 1) + t + 1)
                    nc.vector.bn_stats(st[:, t, :], src[:, t, :]).then_inc(stats_ready, 1)
                for t in range(NT):
                    dve.wait_ge(stats_ready, NT * n + t + 1)
                    nc.vector.bn_aggr(mv[:, t, :], st[:, t, :]).then_inc(moments_ready, 1)
                dve.wait_ge(moments_ready, NT * (n + 1))
                nc.vector.tensor_scalar(veps[:], mv[:, :, 1], EPS, None, ALU.add).then_inc(variance_ready, 1)
                dve.wait_ge(rstd_ready, n + 1)
                for t in range(NT):
                    nc.vector.tensor_scalar(xn[:, t, :], src[:, t, :], mv[:, t, 0:1], rstd[:, t:t + 1],
                                            ALU.subtract, ALU.mult).then_inc(rows_normed, 1)

            def take_rows(name, dst, add=None):
                bank = filled(dve, name)
                v = bank.rearrange("p (t e) -> p t e", t=4)
                if add is None:
                    nc.vector.tensor_copy(dst, v).then_inc(misc_emptied_v, 1)
                else:
                    nc.vector.tensor_tensor(dst, v, add, ALU.add).then_inc(misc_emptied_v, 1)

            def values8(name, bias):
                for n in range(2):
                    bank = filled(dve, f"{name}.{n}")
                    for k in range(4):
                        dst = V9[:, 4 * n + k, :, 0:DH]
                        v = bank[:, 128 * k:128 * k + 128].rearrange("p (h e) -> p h e", h=NH)
                        if bias is None:
                            ins = nc.vector.tensor_copy(dst, v)
                        else:
                            ins = nc.vector.tensor_tensor(dst, v, bias[:].rearrange("p (h e) -> p h e", h=NH), ALU.add)
                    ins.then_inc(misc_emptied_v, 1)

            def split_queries(name):
                for n in range(2):
                    emptied(dve, f"{name}.{n}")
                link(nc.vector.tensor_copy(qparts[:, 0, :], qf))
                link(nc.vector.tensor_tensor(qf, qf, qparts[:, 0, :], ALU.subtract))
                link(nc.vector.tensor_copy(qparts[:, 1, :], qf))
                nc.vector.tensor_tensor(qparts[:, 2, :], qf, qparts[:, 1, :], ALU.subtract).then_inc(qparts_ready, 1)

            def minima(layer, i):
                _, _, g, w = UNITS[layer][i]
                u = BASE[layer] + i
                dve.wait_ge(scores_ready, u + 1)
                if u >= 2:
                    dve.wait_ge(probs_ready, u - 1)
                if layer == 0:
                    dve.wait_ge(rel_masked, i + 1)
                    for k in range(g):
                        ins = nc.vector.tensor_tensor_reduce(
                            Sx[:, u % 2, k * w:(k + 1) * w], SC[u % 2][:, k * w:(k + 1) * w],
                            skewed[:, i % SKEW, k * w:(k + 1) * w], 1.0, 3e38, ALU.add, ALU.min,
                            smin[:, u % 2, k:k + 1])
                    ins.then_inc(min_ready, 1)
                else:
                    nc.vector.tensor_reduce(smin[:, u % 2, 0:g], SC[u % 2].rearrange("p (g w) -> p g w", w=w),
                                            AX.X, ALU.min).then_inc(min_ready, 1)

            def copy_probs(layer, i):
                u = BASE[layer] + i
                if COPIER[u] == "V":
                    dve.wait_ge(probsT_ready, u + 1)
                    if u >= 2:
                        dve.wait_ge(pv_done, u - 1)
                    nc.vector.tensor_copy(PT[:, u % 2, :], TP[u % 2]).then_inc(probsT_copied["V"], 1)

            def finish(layer, k):
                u = BASE[layer] + LAST[layer][k]
                g = GROUPS[layer] + k
                dve.wait_ge(pv_done, u + 1)
                if layer in (0, 2):
                    O = OB[g % 2][:, 0:NH * (DH + 1)].rearrange("p (h e) -> p h e", h=NH)
                    link(nc.vector.reciprocal(rsum[:], O[:, :, DH]))
                    y = xn[:, k, :]
                    link_to = nc.vector.tensor_tensor(y.rearrange("p (h e) -> p h e", h=NH), O[:, :, 0:DH],
                                                      bc(rsum[:], DH), ALU.mult)
                    link_to.then_inc(out_read, 1)
                    dve.wait_ge(out_read, g + 1)
                    if layer == 0:
                        nc.vector.scalar_tensor_tensor(x[:, k, :], y, tg[:, 0:1], x[:, k, :], ALU.mult, ALU.add) \
                            .then_inc(x_updated, 1)
                    else:
                        m = mean[:, k // 2, :, 0:DH]
                        yv = y.rearrange("p (h e) -> p h e", h=NH)
                        d = sg[:, 1, 0:D]
                        link(nc.vector.tensor_tensor(d.rearrange("p (h e) -> p h e", h=NH), m, yv, ALU.subtract))
                        nc.vector.scalar_tensor_tensor(y, d, mk2[:, k:k + 1], y, ALU.mult, ALU.add) \
                            .then_inc(heads_ready, 1)
                elif layer == 1:
                    O = OB[g % 2][:, 0:2 * (D + 1)].rearrange("p (t e) -> p t e", t=2)
                    link(nc.vector.reciprocal(rsum[:, 0:2], O[:, :, D]))
                    y = xn[:, 2 * k:2 * k + 2, :]
                    nc.vector.tensor_tensor(y, O[:, :, 0:D], bc(rsum[:, 0:2], D), ALU.mult).then_inc(out_read, 1)
                    dve.wait_ge(out_read, g + 1)
                    for t in (2 * k, 2 * k + 1):
                        nc.vector.scalar_tensor_tensor(x[:, t, :], xn[:, t, :], tg[:, 1:2], x[:, t, :],
                                                       ALU.mult, ALU.add).then_inc(x_updated, 1)
                else:
                    if k >= 1:
                        filled(dve, f"oT3.{k - 1}")
                    for n in range(2):
                        O = OB[n][:, 0:4 * (DH3 + 1)].rearrange("p (h e) -> p h e", h=4)
                        link(nc.vector.reciprocal(rsum[:, 4 * n:4 * n + 4], O[:, :, DH3]))
                        ins = nc.vector.tensor_tensor(stage3[:, 256 * n:256 * n + 256].rearrange("p (h e) -> p h e", h=4),
                                                      O[:, :, 0:DH3], bc(rsum[:, 4 * n:4 * n + 4], DH3), ALU.mult)
                    ins.then_inc(out_read, 1)

            def attention(layer):
                n = len(UNITS[layer])
                for i in range(n + 5):
                    if i < n:
                        minima(layer, i)
                    if 1 <= i <= n:
                        copy_probs(layer, i - 1)
                    if i - 2 in LAST[layer]:
                        finish(layer, LAST[layer].index(i - 2))
                    if layer == 3 and i - 4 in LAST[3]:
                        t = LAST[3].index(i - 4)
                        bank = filled(dve, f"wo3.{t}")
                        dve.wait_ge(x_updated, 6 * NT)
                        nc.vector.scalar_tensor_tensor(x[:, t, :], bank[:, 0:D], tg[:, 3:4], x[:, t, :],
                                                       ALU.mult, ALU.add).then_inc(misc_emptied_v, 1)
                        dve.wait_ge(misc_emptied_v, EMPTIED[AT[f"wo3.{t}"]])
                        nc.vector.tensor_copy(veps[:, t:t + 1], x[:, t, 0:1]).then_inc(x_updated, 1)

            def router(n, name, bias):
                bank = filled(dve, name)
                v = bank[:, 0:NT * E].rearrange("p (t e) -> p t e", t=NT)
                if bias is None:
                    nc.vector.tensor_copy(lg[:], v).then_inc(misc_emptied_v, 1)
                else:
                    nc.vector.tensor_tensor(lg[:], v, bias[:].unsqueeze(1).to_broadcast([P, NT, E]), ALU.add) \
                        .then_inc(misc_emptied_v, 1)
                dve.wait_ge(misc_emptied_v, EMPTIED[AT[name]])
                for t in range(NT):
                    ins = nc.vector.max(lmx[:, t, :], lg[:, t, :])
                link(ins)
                for t in range(NT):
                    ins = nc.vector.max_index(lix[:, t, :], lmx[:, t, :], lg[:, t, :])
                link(ins)
                if n == 1:
                    nc.vector.tensor_tensor(lg[:], lg[:], bc(lmx[:, :, 0], E), ALU.subtract).then_inc(router_in, 1)
                else:
                    nc.vector.tensor_tensor(rw[:, 0, :], lmx[:, :, 1], lmx[:, :, 0], ALU.subtract).then_inc(router_in, 1)
                link(nc.vector.tensor_copy(lixf[:], lix[:]))
                iot = iota[:].unsqueeze(1).to_broadcast([P, NT, E])
                nc.vector.tensor_tensor(oh[:, 0], iot, bc(lixf[:, :, 0], E), ALU.is_equal)
                if n != 1:
                    nc.vector.tensor_tensor(oh[:, 1], iot, bc(lixf[:, :, 1], E), ALU.is_equal)
                dve.wait_ge(router_exp, n + 1)
                if n == 1:
                    link(nc.vector.tensor_reduce(rw[:, 2, :], lg[:], AX.X, ALU.add))
                    link(nc.vector.reciprocal(rw[:, 3, :], rw[:, 2, :]))
                    nc.vector.tensor_tensor(cw[:], oh[:, 0], bc(rw[:, 3, :], E), ALU.mult).then_inc(cw_ready, 1)
                else:
                    link(nc.vector.tensor_scalar(rw[:, 2, :], rw[:, 1, :], 1.0, None, ALU.add))
                    link(nc.vector.reciprocal(rw[:, 3, :], rw[:, 2, :]))
                    link(nc.vector.tensor_tensor(rw[:, 2, :], rw[:, 3, :], rw[:, 1, :], ALU.mult))
                    nc.vector.tensor_tensor(oh[:, 0], oh[:, 0], bc(rw[:, 3, :], E), ALU.mult)
                    link(nc.vector.tensor_tensor(oh[:, 1], oh[:, 1], bc(rw[:, 2, :], E), ALU.mult))
                    nc.vector.tensor_tensor(cw[:], oh[:, 0], oh[:, 1], ALU.add).then_inc(cw_ready, 1)

            def output_bias(layer):
                for n in range(2):
                    bank = filled(dve, f"cwT{layer}.{n}")
                    nc.vector.tensor_copy(cwT[:, 512 * n:512 * n + 512], bank[0:E, :]).then_inc(misc_emptied_v, 1)
                for n in range(2):
                    take_rows(f"bias{layer}.{n}", xn[:, 4 * n:4 * n + 4, :])
                dve.wait_ge(misc_emptied_v, EMPTIED[AT[f"bias{layer}.1"]])

            def experts(layer, nch, gate):
                m = moe[layer]
                for e in range(E + 1):
                    if e < E and layer == 0:
                        for c in range(nch):
                            for n in range(2):
                                j = (e * nch + c) * 2 + n
                                dve.wait_ge(m["act"], j + 1)
                                dve.wait_ge(m["up"], j + 1)
                                if e >= 2:
                                    dve.wait_ge(m["down"], 2 * (e - 1))
                                nc.vector.scalar_tensor_tensor(hid[:, e % 2, c, 512 * n:512 * n + 512], TP[j % 2],
                                                               hb2[:, e, c:c + 1], sg[:, j % 2, :], ALU.add, ALU.mult) \
                                    .then_inc(m["hidden"], 1)
                    if e >= 1:
                        for n in range(2):
                            q = 2 * (e - 1) + n
                            dve.wait_ge(m["down"], q + 1)
                            if q >= 2:
                                dve.wait_ge(m["summed"], q - 1)
                            for k in range(4):
                                t = 4 * n + k
                                ins = nc.vector.scalar_tensor_tensor(xn[:, t, :], OB[n][:, 128 * k:128 * k + 128],
                                                                     cw[:, t, e - 1:e], xn[:, t, :], ALU.mult, ALU.add)
                            ins.then_inc(m["summed"], 1)
                dve.wait_ge(m["summed"], 2 * E)
                for t in range(NT):
                    nc.vector.scalar_tensor_tensor(x[:, t, :], xn[:, t, :], tg[:, gate:gate + 1], x[:, t, :],
                                                   ALU.mult, ALU.add).then_inc(x_updated, 1)

            def quantize_weight(w, scales, inverse, nchunk):
                if nchunk == 1:
                    link(nc.vector.tensor_reduce(scales, w, AX.X, ALU.max, apply_absolute_value=True))
                else:
                    link(nc.vector.tensor_reduce(scales, w, AX.X, ALU.max, apply_absolute_value=True))
                link(nc.vector.tensor_scalar(scales, scales, 1.0 / QMAX, None, ALU.mult))
                link(nc.vector.reciprocal(inverse, scales))
                for c in range(nchunk):
                    v = w if nchunk == 1 else w[:, c, :]
                    ins = nc.vector.tensor_scalar(v, v, inverse[:, c:c + 1], QMAX, ALU.mult, ALU.min)
                link(ins)
                link(nc.vector.tensor_scalar(w, w, -QMAX - 1.0, ROUND, ALU.max, ALU.add))
                return nc.vector.tensor_scalar(w, w, ROUND, None, ALU.subtract)

            dve.wait_ge(ld_er, 16)
            link(nc.vector.tensor_copy(erp[:, 0, :], erf[:]))
            link(nc.vector.tensor_tensor(erf[:], erf[:], erp[:, 0, :], ALU.subtract))
            link(nc.vector.tensor_copy(erp[:, 1, :], erf[:]))
            nc.vector.tensor_tensor(erp[:, 2, :], erf[:], erp[:, 1, :], ALU.subtract).then_inc(erparts_ready, 1)
            loaded(dve, "b0")
            nc.vector.tensor_scalar(nbq0, b0[:, 0:1], -SLICE8, None, ALU.mult).then_inc(nbq_ready, 1)
            dve.wait_ge(ld_x, 16)
            norm_rows(0, x)
            loaded(dve, "bv0")
            values8("v0", bv0)
            split_queries("q0")
            loaded(dve, "maskf", "ident", "b1")
            nc.vector.memset(maskb[:, 1, :], 0.0)
            link(nc.vector.tensor_copy(identb[:], ident[:]))
            nc.vector.tensor_copy(maskb[:, 0, :].rearrange("p (g w) -> p g w", g=4),
                                  maskf[:].unsqueeze(1).to_broadcast([P, 4, P]))
            nc.vector.tensor_copy(maskb[:, 1, :].rearrange("p (g w) -> p g w", g=2)[:, :, P:2 * P],
                                  maskf[:].unsqueeze(1).to_broadcast([P, 2, P])).then_inc(mask_ready, 1)
            nc.vector.tensor_scalar(nbq1, b1[:, 0:1], -SLICE8, None, ALU.mult).then_inc(nbq_ready, 1)
            dve.wait_ge(gates_ready, 1)
            attention(0)
            norm_rows(1, x, 1)
            loaded(dve, "br0", "iota", "hb2")
            router(0, "router0.0", br0)
            output_bias(0)
            experts(0, 4, 4)
            loaded(dve, "bv1")
            for n in range(2):
                take_rows(f"v1.{n}", VA[:, 4 * n:4 * n + 4, 0:D], bv1[:].unsqueeze(1).to_broadcast([P, 4, D]))
            dve.wait_ge(ld_mrow, 16)
            nc.vector.tensor_scalar(mrow[:], mrow[:], -10000.0, 10000.0, ALU.mult, ALU.add).then_inc(mask_ready, 1)
            norm_rows(2, x, 2)
            loaded(dve, "wg", "wu", "wd")
            quantize_weight(wg[:], wgs, iwg, NI).then_inc(weights_scaled, 1)
            quantize_weight(wu[:], wus, iwu, NI).then_inc(weights_scaled, 1)
            quantize_weight(wd[:], wds, iwd, 1).then_inc(weights_scaled, 1)
            nc.vector.tensor_scalar(diag[:], ident[:], wds, None, ALU.mult).then_inc(weights_scaled, 1)
            attention(1)
            for name, dst in (("wgT.0", wgT), ("wuT.0", wuT)):
                bank = filled(dve, name)
                nc.vector.tensor_copy(dst[:], bank[:, 0:NI * CI]).then_inc(misc_emptied_v, 1)
            bank = filled(dve, "wdT.0")
            nc.vector.tensor_copy(wdT[:], bank[0:CI, :].rearrange("p (c d) -> p c d", c=NI)).then_inc(misc_emptied_v, 1)
            bank = filled(dve, "wdrow.0")
            nc.vector.tensor_copy(wdrow[:], bank[:, 0:D]).then_inc(misc_emptied_v, 1)
            dve.wait_ge(sig_exp, 1)
            link(nc.vector.tensor_scalar(sg2, sg2, 1.0, None, ALU.add))
            link(nc.vector.reciprocal(sg2, sg2))
            norm_rows(3, x, 3)
            emptied(dve, "ln3.0")
            emptied(dve, "ln3.1")
            nc.vector.tensor_reduce(amx, xnT[:], AX.X, ALU.max, apply_absolute_value=True).then_inc(xmax_ready, 1)
            dve.wait_ge(xmax_all, 1)
            link(nc.vector.tensor_scalar(sx, amxg, sg2[:, 0:1], 1.0 / QMAX, ALU.mult, ALU.mult))
            nc.vector.tensor_scalar(fg, wgs, sx[0:CI, :], None, ALU.mult)
            nc.vector.tensor_scalar(fu, wus, sx[0:CI, :], None, ALU.mult)
            link(nc.vector.reciprocal(isx, sx))
            link(nc.vector.tensor_scalar(qf, xnT[:], isx, QMAX, ALU.mult, ALU.min))
            link(nc.vector.tensor_scalar(qf, qf, -QMAX - 1.0, ROUND, ALU.max, ALU.add))
            nc.vector.tensor_scalar(xq[:], qf, ROUND, None, ALU.subtract).then_inc(xq_ready, 1)
            for j in range(2 * NI):
                c, n = j // 2, j % 2
                dve.wait_ge(l1_silu, j + 1)
                dve.wait_ge(l1_up, j + 1)
                nc.vector.scalar_tensor_tensor(h1[0:CI, c, 512 * n:512 * n + 512], TP[j % 2][0:CI, :], fu[:, c:c + 1],
                                               sg[0:CI, j % 2, :], ALU.mult, ALU.mult).then_inc(l1_hidden, 1)
            dve.wait_ge(l1_hidden, 2 * NI)
            dve.wait_ge(pool_consts, 5)
            nc.vector.tensor_reduce(amh[0:CI, :], h1[0:CI], AX.XY, ALU.max, apply_absolute_value=True) \
                .then_inc(hmax_ready, 1)
            dve.wait_ge(hmax_all, 1)
            link(nc.vector.tensor_scalar(sh, amhg, sg2[:, 1:2], 1.0 / QMAX, ALU.mult, ALU.mult))
            nc.vector.tensor_scalar(fac, sh, tg[:, 5:6], None, ALU.mult)
            link(nc.vector.reciprocal(ish, sh))
            link(nc.vector.tensor_scalar(h1[0:CI], h1[0:CI], ish[0:CI, :], QMAX, ALU.mult, ALU.min))
            link(nc.vector.tensor_scalar(h1[0:CI], h1[0:CI], -QMAX - 1.0, ROUND, ALU.max, ALU.add))
            nc.vector.tensor_scalar(h1q[0:CI], h1[0:CI], ROUND, None, ALU.subtract).then_inc(hq_ready, 1)
            for n in range(2):
                dve.wait_ge(l1_down, n + 1)
                y = xn[:, 4 * n:4 * n + 4, :]
                link(nc.vector.tensor_tensor(y, OB[n].rearrange("p (t d) -> p t d", t=4),
                                             wdrow[:].unsqueeze(1).to_broadcast([P, 4, D]), ALU.mult))
                for t in range(4 * n, 4 * n + 4):
                    nc.vector.scalar_tensor_tensor(x[:, t, :], xn[:, t, :], fac, x[:, t, :],
                                                   ALU.mult, ALU.add).then_inc(x_updated, 1)
            loaded(dve, "maski")
            nc.vector.tensor_scalar(mk2[:], maski[:], 0.0, None, ALU.not_equal)
            values8("v2", None)
            for n in range(2):
                bank = filled(dve, f"mean.{n}")
                nc.vector.tensor_scalar(mean[:, 2 * n:2 * n + 2, :, :],
                                        bank[:, 0:2 * 144].rearrange("p (b h e) -> p b h e", b=2, h=NH),
                                        1.0 / S, None, ALU.mult).then_inc(misc_emptied_v, 1)
            norm_rows(4, x, 4)
            split_queries("q2")
            attention(2)
            for n in range(2):
                bank = filled(dve, f"wo2.{n}")
                for k in range(4):
                    t = 4 * n + k
                    ins = nc.vector.scalar_tensor_tensor(x[:, t, :], bank[:, 128 * k:128 * k + 128], tg[:, 2:3],
                                                         x[:, t, :], ALU.mult, ALU.add)
                    if k < 3:
                        ins.then_inc(x_updated, 1)
                    else:
                        ins.then_inc(misc_emptied_v, 1)
                        dve.wait_ge(misc_emptied_v, EMPTIED[AT[f"wo2.{n}"]])
                        nc.vector.tensor_copy(veps[:, 0:1], x[:, t, 0:1]).then_inc(x_updated, 1)
            norm_rows(5, x, 5)
            loaded(dve, "br2")
            router(1, "router2.0", br2)
            output_bias(2)
            experts(2, 2, 6)
            dve.wait_ge(ld_ctx, 16)
            norm_rows(6, ctxr)
            loaded(dve, "lnp", "cos", "sin")
            for n in range(2):
                bank = filled(dve, f"lnc.{n}")
                nc.vector.tensor_scalar(cnT[:, 512 * n:512 * n + 512], bank, lnp[:, 0:1], lnp[:, 1:2],
                                        ALU.mult, ALU.add).then_inc(misc_emptied_v, 1)
            for k in range(8):
                c, n = k // 2, k % 2
                if k >= 2:
                    dve.wait_ge(rope_done, k - 1)
                bank = filled(dve, f"kc.{c}.{n}")
                nc.vector.tensor_tensor(rope[:, 0, k % 2, :].rearrange("p (b t) -> p b t", b=2),
                                        bank.rearrange("p (b t) -> p b t", b=2),
                                        cos[:].unsqueeze(1).to_broadcast([P, 2, S]), ALU.mult).then_inc(misc_emptied_v, 1)
                bank = filled(dve, f"kr.{c}.{n}")
                nc.vector.tensor_tensor(rope[:, 1, k % 2, :].rearrange("p (b t) -> p b t", b=2),
                                        bank.rearrange("p (b t) -> p b t", b=2),
                                        sin[:].unsqueeze(1).to_broadcast([P, 2, S]), ALU.mult).then_inc(misc_emptied_v, 1)
                dve.wait_ge(misc_emptied_v, EMPTIED[AT[f"kr.{c}.{n}"]])
                nc.vector.tensor_copy(veps[:, 0:1], rope[:, 1, k % 2, 0:1]).then_inc(rope_in, 1)
            dve.wait_ge(vones, 1)

            def values(kind):
                for t in range(1, NT, 2):
                    k = 4 * (t // 2) + 2 * (kind == "vl") + 1
                    bank = filled(dve, f"{kind}.{t}")
                    nc.vector.tensor_copy(VX[:, k, :, 0:DH3], bank.rearrange("p (h e) -> p h e", h=NH3)) \
                        .then_inc(misc_emptied_v, 1)

            values("vc")
            norm_rows(7, x, 6)
            dve.wait_ge(rows_normed, 8 * NT)
            norm_rows(8, xn)
            for n in range(2):
                bank = filled(dve, f"ln8.{n}")
                nc.vector.tensor_scalar(xnT[:, 512 * n:512 * n + 512], bank, lnp[:, 2:3], lnp[:, 3:4],
                                        ALU.mult, ALU.add).then_inc(misc_emptied_v, 1)
            values("vl")
            attention(3)
            norm_rows(9, x, 7)
            router(2, "router3.0", None)
            dve.wait_ge(cw_ready, 3)
            for t in range(NT + 2):
                if t < NT:
                    bank = filled(dve, f"uv.{t}")
                    dve.wait_ge(silu3, t + 1)
                    if t >= 2:
                        filled(dve, f"sT.{t - 2}")
                    nc.vector.tensor_tensor(PR[:, t % 2, 256:512], bank[:, 256:512], sg[:, t % 2, 0:256],
                                            ALU.mult).then_inc(misc_emptied_v, 1)
                    dve.wait_ge(misc_emptied_v, EMPTIED[AT[f"uv.{t}"]])
                    nc.vector.tensor_tensor(PR[:, t % 2, 0:256].rearrange("p (e r) -> p e r", e=E),
                                            PR[:, t % 2, 256:512].rearrange("p (e r) -> p e r", e=E),
                                            bc(cw[:, t, :], 32), ALU.mult).then_inc(s3_ready, 1)
                if t >= 2:
                    bank = filled(dve, f"y3.{t - 2}")
                    nc.vector.scalar_tensor_tensor(x[:, t - 2, :], bank[:, 0:D], tg[:, 7:8], x[:, t - 2, :],
                                                   ALU.mult, ALU.add).then_inc(misc_emptied_v, 1)
                    dve.wait_ge(misc_emptied_v, EMPTIED[AT[f"y3.{t - 2}"]])
                    nc.vector.tensor_copy(veps[:, 0:1], x[:, t - 2, 0:1]).then_inc(x_updated, 1)

        @block.tensor
        def _(pe):
            def room(name):
                i = AT[name]
                if i >= 2:
                    emptied(pe, MISC[i - 2][0])
                return MB[i % 2]

            def halves(name, w, xT):
                for n in range(2):
                    bank = room(f"{name}.{n}")
                    nc.tensor.matmul(bank, w, xT[:, 512 * n:512 * n + 512], start=True, stop=True) \
                        .then_inc(misc_ready, 1)

            def rows(name, xT, w):
                for n in range(2):
                    bank = room(f"{name}.{n}")
                    for k in range(4):
                        t = 4 * n + k
                        ins = nc.tensor.matmul(bank[:, 128 * k:128 * k + 128], xT[:, 128 * t:128 * t + 128], w,
                                               start=True, stop=True)
                    ins.then_inc(misc_ready, 1)

            def turn_rows(n, name):
                for hf in range(2):
                    bank = room(f"{name}.{hf}")
                    for k in range(4):
                        t = 4 * hf + k
                        pe.wait_ge(rows_normed, NT * n + t + 1)
                        ins = nc.tensor.transpose(bank[:, 128 * k:128 * k + 128], xn[:, t, :], ident[:])
                    ins.then_inc(misc_ready, 1)

            def turned(name):
                for n in range(2):
                    emptied(pe, f"{name}.{n}")

            def rel(r):
                t, h, g, w = UNITS8[r]
                bank = room(f"qer.{r}")
                for k in range(g):
                    ins = nc.tensor.matmul(bank[:, k * w:(k + 1) * w], QS[:, h + k, t * P:(t + 1) * P], ES[:, S - w:S],
                                           start=True, stop=True)
                ins.then_inc(misc_ready, 1)

            def scores(layer, i):
                t, h, g, w = UNITS[layer][i]
                b, u = t // 2, BASE[layer] + i
                bank = SC[u % 2]
                if u >= 2:
                    pe.wait_ge(min_ready if layer == 0 else probs_ready, u - 1)
                if layer in (0, 2):
                    for k in range(g):
                        if layer == 2:
                            nc.tensor.matmul(bank[:, k * w:(k + 1) * w], identb[:],
                                             maskb[:, t % 2, k * w:(k + 1) * w], start=True, stop=False)
                        ins = nc.tensor.matmul(bank[:, k * w:(k + 1) * w], QS[:, h + k, t * P:(t + 1) * P],
                                               KS[:, h + k, b * S:b * S + w], start=(layer == 0),
                                               stop=True)
                elif layer == 1:
                    for k in range(2):
                        nc.tensor.matmul(bank[:, k * S:(k + 1) * S], ones[0:1, :], mrow[0:1, b * S:(b + 1) * S],
                                         start=True, stop=False)
                        ins = nc.tensor.matmul(bank[:, k * S:(k + 1) * S], qf[:, (t + k) * P:(t + k + 1) * P],
                                               kf[:, b * S:(b + 1) * S], start=False, stop=True)
                else:
                    r = DH3 * (h % 2)
                    ins = nc.tensor.matmul(bank, QT3[r:r + DH3, h // 2, t * P:(t + 1) * P], KT3[r:r + DH3, h // 2, b, :],
                                           start=True, stop=True)
                ins.then_inc(scores_ready, 1)

            def turn_probs(layer, i):
                u = BASE[layer] + i
                pe.wait_ge(probs_ready, u + 1)
                if u >= 2:
                    copied(pe, u - 2)
                for k in range(4):
                    ins = nc.tensor.transpose(TP[u % 2][:, P * k:P * k + P], PR[:, u % 2, P * k:P * k + P], ident[:])
                ins.then_inc(probsT_ready, 1)

            def weigh(layer, i):
                t, h, g, w = UNITS[layer][i]
                u = BASE[layer] + i
                k0 = sum(j < i for j in LAST[layer])
                grp = GROUPS[layer] + k0
                if i == 0 or i - 1 in LAST[layer]:
                    behind = grp if layer == 3 else grp - 1
                    if behind > 0:
                        pe.wait_ge(out_read, behind)
                copied(pe, u)
                for k in range(4):
                    pt = PT[:, u % 2, P * k:P * k + P]
                    if layer in (0, 2):
                        hh, jt, last = (h + k, 0, 0) if g == 4 else (h + k // 2, k % 2, 1)
                        ins = nc.tensor.matmul(OB[grp % 2][:, 9 * hh:9 * hh + 9], pt, V9[:, t - t % 2 + jt, hh, :],
                                               start=(jt == 0), stop=(jt == last))
                    elif layer == 1:
                        it, jt = k // 2, k % 2
                        ins = nc.tensor.matmul(OB[grp % 2][:, 129 * it:129 * it + 129], pt, VA[:, t + jt, :],
                                               start=(jt == 0), stop=(jt == 1))
                    else:
                        ins = nc.tensor.matmul(OB[h // 4][:, 65 * (h % 4):65 * (h % 4) + 65], pt,
                                               VX[:, 4 * (t // 2) + k, h, :], start=(k == 0), stop=(k == 3))
                ins.then_inc(pv_done, 1)

            def attention(layer):
                n = len(UNITS[layer])
                for i in range(n + 5):
                    if layer == 0 and i + LEAD < N8:
                        rel(i + LEAD)
                    if i < n:
                        scores(layer, i)
                    if 1 <= i <= n:
                        turn_probs(layer, i - 1)
                    if 2 <= i < n + 2:
                        weigh(layer, i - 2)
                    if layer == 3 and i - 3 in LAST[3]:
                        t = LAST[3].index(i - 3)
                        bank = room(f"oT3.{t}")
                        pe.wait_ge(out_read, GROUPS[3] + t + 1)
                        for k in range(4):
                            ins = nc.tensor.transpose(bank[:, P * k:P * k + P], stage3[:, P * k:P * k + P], ident[:])
                        ins.then_inc(misc_ready, 1)
                    if layer == 3 and i - 4 in LAST[3]:
                        t = LAST[3].index(i - 4)
                        bank = room(f"wo3.{t}")
                        emptied(pe, f"oT3.{t}")
                        for k in range(4):
                            ins = nc.tensor.matmul(bank[:, 0:D], sg[:, 0, P * k:P * k + P], wo3[:, k, :],
                                                   start=(k == 0), stop=(k == 3))
                        ins.then_inc(misc_ready, 1)

            def logits(name, w):
                bank = room(name)
                for t in range(NT):
                    ins = nc.tensor.matmul(bank[:, E * t:E * t + E], xnT[:, P * t:P * t + P], w[:], start=True, stop=True)
                ins.then_inc(misc_ready, 1)

            def output_bias(layer, n_cw, b):
                pe.wait_ge(cw_ready, n_cw)
                for n in range(2):
                    bank = room(f"cwT{layer}.{n}")
                    for k in range(4):
                        ins = nc.tensor.transpose(bank[0:E, P * k:P * k + P], cw[:, 4 * n + k, :], ident[:])
                    ins.then_inc(misc_ready, 1)
                for n in range(2):
                    bank = room(f"bias{layer}.{n}")
                    emptied(pe, f"cwT{layer}.{n}")
                    for k in range(4):
                        t = 4 * n + k
                        ins = nc.tensor.matmul(bank[:, P * k:P * k + P], cwT[:, P * t:P * t + P], b[:], start=True, stop=True)
                    ins.then_inc(misc_ready, 1)

            def experts(layer, nch, w1, w2, w3, ndma):
                m = moe[layer]
                for e in range(E + 1):
                    if e < E:
                        s = e % 2
                        pe.wait_ge(m[f"slot{s}"], 16 * ndma * (e // 2 + 1))
                        for c in range(nch):
                            for n in range(2):
                                j = (e * nch + c) * 2 + n
                                if j >= 2:
                                    pe.wait_ge(m["act"] if layer == 0 else m["hidden"], j - 1)
                                nc.tensor.matmul(SC[j % 2], w1[:, s, P * c:P * c + P], xnT[:, 512 * n:512 * n + 512],
                                                 start=True, stop=True).then_inc(m["gate"], 1)
                                if layer == 0:
                                    if j >= 2:
                                        pe.wait_ge(m["hidden"], j - 1)
                                    nc.tensor.matmul(TP[j % 2], w2[:, s, P * c:P * c + P], xnT[:, 512 * n:512 * n + 512],
                                                     start=True, stop=True).then_inc(m["up"], 1)
                    if e >= 1:
                        s = (e - 1) % 2
                        pe.wait_ge(m["hidden"], e * nch * 2)
                        for n in range(2):
                            q = 2 * (e - 1) + n
                            if q >= 2:
                                pe.wait_ge(m["summed"], q - 1)
                            for k in range(4):
                                t = 4 * n + k
                                for c in range(nch):
                                    ins = nc.tensor.matmul(OB[n][:, P * k:P * k + P], hid[:, s, c, P * t:P * t + P],
                                                           w3[:, s, c, :], start=(c == 0), stop=(c == nch - 1))
                            ins.then_inc(m["down"], 1)

            loaded(pe, "wk0")
            pe.wait_ge(ld_ctxT, 16)
            halves("k0", wk0[:], ctxT)
            loaded(pe, "wv0")
            rows("v0", ctxT, wv0[:])
            loaded(pe, "ident")
            turn_rows(0, "ln0")
            turned("ln0")
            loaded(pe, "wq0")
            halves("q0", wq0[:], xnT)
            pe.wait_ge(es_loaded, 16 * 9)
            pe.wait_ge(qs_loaded, 16 * 9)
            for r in range(LEAD):
                rel(r)
            pe.wait_ge(ks_loaded, 16 * 9)
            pe.wait_ge(pool_consts, 5)
            attention(0)
            turn_rows(1, "ln1")
            turned("ln1")
            loaded(pe, "wr0", "hb3")
            logits("router0.0", wr0)
            output_bias(0, 1, hb3)
            experts(0, 4, W1r, W2r, W3r, 3)
            loaded(pe, "wk1", "wv1", "wq1")
            halves("k1", wk1[:], ctxT)
            rows("v1", ctxT, wv1[:])
            turn_rows(2, "ln2")
            turned("ln2")
            halves("q1", wq1[:], xnT)
            for n in range(2):
                emptied(pe, f"q1.{n}")
            pe.wait_ge(mask_ready, 2)
            attention(1)
            for name, w, k in (("wgT.0", wg, 1), ("wuT.0", wu, 2)):
                bank = room(name)
                pe.wait_ge(weights_scaled, k)
                for c in range(NI):
                    ins = nc.tensor.transpose(bank[:, CI * c:CI * c + CI], w[:, c, :], ident[0:CI, 0:CI])
                ins.then_inc(misc_ready, 1)
            bank = room("wdT.0")
            pe.wait_ge(weights_scaled, 3)
            for c in range(NI):
                ins = nc.tensor.transpose(bank[0:CI, P * c:P * c + P], wd[:, CI * c:CI * c + CI], ident[:])
            ins.then_inc(misc_ready, 1)
            bank = room("wdrow.0")
            pe.wait_ge(weights_scaled, 4)
            nc.tensor.matmul(bank[:, 0:D], ones[:], diag[:], start=True, stop=True).then_inc(misc_ready, 1)
            turn_rows(3, "ln3")
            emptied(pe, "wdrow.0")
            pe.wait_ge(xq_ready, 1)
            for j in range(2 * NI):
                c, n = j // 2, j % 2
                if j >= 2:
                    pe.wait_ge(l1_silu, j - 1)
                nc.tensor.matmul(SC[j % 2][0:CI, :], wgT[:, CI * c:CI * c + CI], xq[:, 512 * n:512 * n + 512],
                                 start=True, stop=True).then_inc(l1_gate, 1)
                if j >= 2:
                    pe.wait_ge(l1_hidden, j - 1)
                nc.tensor.matmul(TP[j % 2][0:CI, :], wuT[:, CI * c:CI * c + CI], xq[:, 512 * n:512 * n + 512],
                                 start=True, stop=True).then_inc(l1_up, 1)
            pe.wait_ge(hq_ready, 1)
            for n in range(2):
                for k in range(4):
                    t = 4 * n + k
                    for c in range(NI):
                        ins = nc.tensor.matmul(OB[n][:, P * k:P * k + P], h1q[0:CI, c, P * t:P * t + P], wdT[:, c, :],
                                               start=(c == 0), stop=(c == NI - 1))
                ins.then_inc(l1_down, 1)
            loaded(pe, "wk2", "wv2", "wq2", "wo2")
            halves("k2", wk2[:], ctxT)
            rows("v2", ctxT, wv2[:])
            for n in range(2):
                emptied(pe, f"v2.{n}")
            for n in range(2):
                bank = room(f"mean.{n}")
                for k in range(2):
                    for jt in range(2):
                        t = 2 * (2 * n + k) + jt
                        ins = nc.tensor.matmul(bank[:, 144 * k:144 * k + 144], ones[:],
                                               V9[:, t].rearrange("p h e -> p (h e)"), start=(jt == 0), stop=(jt == 1))
                ins.then_inc(misc_ready, 1)
            turn_rows(4, "ln4")
            turned("ln4")
            halves("q2", wq2[:], xnT)
            pe.wait_ge(ks_loaded, 16 * 18)
            pe.wait_ge(qs_loaded, 16 * 18)
            attention(2)
            for n in range(2):
                bank = room(f"oT2.{n}")
                for k in range(4):
                    pe.wait_ge(heads_ready, 4 * n + k + 1)
                    ins = nc.tensor.transpose(bank[:, P * k:P * k + P], xn[:, 4 * n + k, :], ident[:])
                ins.then_inc(misc_ready, 1)
            turned("oT2")
            rows("wo2", xnT, wo2[:])
            turn_rows(5, "ln5")
            turned("ln5")
            loaded(pe, "wr2", "gb2")
            logits("router2.0", wr2)
            output_bias(2, 2, gb2)
            experts(2, 2, W1s, None, W2s, 2)
            turn_rows(6, "lnc")
            for n in range(2):
                emptied(pe, f"lnc.{n}")
            loaded(pe, "wkv3", "wkr3", "wq3", "wo3")
            for c in range(4):
                for n in range(2):
                    bank = room(f"kc.{c}.{n}")
                    nc.tensor.matmul(bank, wkv3[:, P * c:P * c + P], cnT[:, 512 * n:512 * n + 512], start=True, stop=True) \
                        .then_inc(misc_ready, 1)
                    bank = room(f"kr.{c}.{n}")
                    nc.tensor.matmul(bank, wkr3[:, P * c:P * c + P], cnT[:, 512 * n:512 * n + 512], start=True, stop=True) \
                        .then_inc(misc_ready, 1)
            for t in range(NT):
                bank = room(f"vc.{t}")
                nc.tensor.matmul(bank, cnT[:, P * t:P * t + P], wkv3[:, 512:1024], start=True, stop=True) \
                    .then_inc(misc_ready, 1)
            turn_rows(8, "ln8")
            for n in range(2):
                emptied(pe, f"ln8.{n}")
            for c in range(4):
                for n in range(2):
                    bank = room(f"kl.{c}.{n}")
                    nc.tensor.matmul(bank, wkv3[:, P * c:P * c + P], xnT[:, 512 * n:512 * n + 512], start=True, stop=True) \
                        .then_inc(misc_ready, 1)
                    bank = room(f"q3.{c}.{n}")
                    nc.tensor.matmul(bank, wq3[:, P * c:P * c + P], xnT[:, 512 * n:512 * n + 512], start=True, stop=True) \
                        .then_inc(misc_ready, 1)
            for t in range(NT):
                bank = room(f"vl.{t}")
                nc.tensor.matmul(bank, xnT[:, P * t:P * t + P], wkv3[:, 512:1024], start=True, stop=True) \
                    .then_inc(misc_ready, 1)
            pe.wait_ge(rope_done, 8)
            for n in ("q3.3.1", "vl.6", "vl.7"):
                emptied(pe, n)
            attention(3)
            turn_rows(9, "ln9")
            turned("ln9")
            loaded(pe, "wr3", "wuv", "wf3")
            logits("router3.0", wr3)
            for t in range(NT + 2):
                if t < NT:
                    bank = room(f"uv.{t}")
                    nc.tensor.matmul(bank, xnT[:, P * t:P * t + P], wuv[:], start=True, stop=True).then_inc(misc_ready, 1)
                if 1 <= t <= NT:
                    bank = room(f"sT.{t - 1}")
                    pe.wait_ge(s3_ready, t)
                    for k in range(2):
                        ins = nc.tensor.transpose(bank[:, P * k:P * k + P], PR[:, (t - 1) % 2, P * k:P * k + P], ident[:])
                    ins.then_inc(misc_ready, 1)
                if t >= 2:
                    bank = room(f"y3.{t - 2}")
                    emptied(pe, f"sT.{t - 2}")
                    for k in range(2):
                        ins = nc.tensor.matmul(bank[:, 0:D], PT[:, (t - 2) % 2, P * k:P * k + P], wf3[:, k, :],
                                               start=(k == 0), stop=(k == 1))
                    ins.then_inc(misc_ready, 1)


def _constants():
    half = DH3 // 2
    inv = (1.0 / np.float32(10000.0) ** (np.arange(0, DH3, 2, dtype=np.float32) / np.float32(DH3))).astype(np.float32)
    ang = (np.arange(S, dtype=np.float32)[None, :] * inv[:, None]).astype(np.float32)
    c, s = np.cos(ang).astype(np.float32), np.sin(ang).astype(np.float32)
    cos = np.concatenate([c] * 4, 0)
    sin = np.concatenate([-s, s, -s, s], 0)
    i, j = np.arange(P)[:, None], np.arange(P)[None, :]
    return {
        "ident": np.eye(P, dtype=np.float32),
        "maskf": np.where(j <= i, 0.0, BIG).astype(np.float32),
        "iota": np.tile(np.arange(E, dtype=np.float32), (P, 1)),
        "cos": np.ascontiguousarray(cos), "sin": np.ascontiguousarray(sin),
    }


def _lay_out(a):
    g = {k: np.asarray(v) for k, v in a.items()}
    ctx = g["ctx_1024"].reshape(TOK, D)
    wkv = g["L3_xattn_Wkv"]
    half = DH3 // 2
    swap = np.concatenate([np.concatenate([np.arange(half, DH3), np.arange(half)]) + DH3 * h for h in range(NH3)])
    lay = {
        "x": g["x"].reshape(TOK, D), "ctx": ctx, "ctxT": ctx.T,
        "erT": g["L0_xattn_Er"].T, "mrow": g["mask_BxS2_ff1"].reshape(1, TOK),
        "gates": np.concatenate([g["g_xattn"], g["g_ffn"]]),
        "clips": np.concatenate([g["L1_ffn_clip_x"], g["L1_ffn_clip_down"]]),
        "wq0": g["L0_xattn_Wq"].T, "wk0": g["L0_xattn_Wk"].T, "wv0": g["L0_xattn_Wv"].T,
        "b0": np.stack([g["L0_xattn_bq"], g["L0_xattn_bk"]], 1), "bv0": g["L0_xattn_bv"],
        "wq1": g["L1_xattn_Wq"], "wk1": g["L1_xattn_Wk"], "wv1": g["L1_xattn_Wv"],
        "b1": np.stack([g["L1_xattn_bq"], g["L1_xattn_bk"]], 1), "bv1": g["L1_xattn_bv"],
        "wq2": g["L2_xattn_WQ"], "wk2": g["L2_xattn_WK"], "wv2": g["L2_xattn_WV"], "wo2": g["L2_xattn_WO"],
        "maski": g["mask_BxS2_ik0"].reshape(NT, P).T,
        "wr0": g["L0_ffn_Wr"], "br0": g["L0_ffn_br"],
        "hb1": g["L0_ffn_b1"].reshape(E, 4, P).transpose(2, 0, 1),
        "hb2": g["L0_ffn_b2"].reshape(E, 4, P).transpose(2, 0, 1), "hb3": g["L0_ffn_b3"],
        "f1": g["L0_ffn_W1"], "f2": g["L0_ffn_W2"], "f3": g["L0_ffn_W3"],
        "wr2": g["L2_ffn_Wg"], "br2": g["L2_ffn_bg"],
        "gb1": g["L2_ffn_b1"].reshape(E, 2, P).transpose(2, 0, 1), "gb2": g["L2_ffn_b2"],
        "g1": g["L2_ffn_W1"], "g2": g["L2_ffn_W2"],
        "wg": g["L1_ffn_w_gate"].reshape(NI, CI, D).transpose(1, 0, 2),
        "wu": g["L1_ffn_w_up"].reshape(NI, CI, D).transpose(1, 0, 2), "wd": g["L1_ffn_w_down"],
        "lnp": np.stack([g["L3_xattn_gamma_x"], g["L3_xattn_beta_x"], g["L3_xattn_gamma_l"], g["L3_xattn_beta_l"]], 1),
        "wq3": g["L3_xattn_Wq"], "wkv3": wkv, "wkr3": wkv[:, 0:512][:, swap],
        "wo3": g["L3_xattn_Wo"].reshape(4, P, D).transpose(1, 0, 2).reshape(P, 512),
        "wr3": g["L3_ffn_gate_w"],
        "wuv": np.concatenate([g["L3_ffn_Wu"].transpose(1, 0, 2).reshape(D, 256),
                               g["L3_ffn_Wv"].transpose(1, 0, 2).reshape(D, 256)], 1),
        "wf3": g["L3_ffn_Wo"].reshape(2, P, D).transpose(1, 0, 2).reshape(P, 256),
    }
    return {k: np.ascontiguousarray(v) for k, v in lay.items()}


def kernel(**inputs):
    import concourse.bacc as bacc
    from concourse.bass_utils import run_bass_kernel_spmd

    arrays = {**_lay_out(inputs), **_constants()}
    nc = bacc.Bacc("TRN2", target_bir_lowering=False, num_devices=1)
    aps = {k: nc.dram_tensor("in_" + k + "_dram", v.shape, mybir.dt.from_np(v.dtype), kind="ExternalInput").ap()
           for k, v in arrays.items()}
    out = nc.dram_tensor("out_dram", (TOK, D), F32, kind="ExternalOutput").ap()
    build(nc, aps, out)
    r = run_bass_kernel_spmd(nc, [{"in_" + k + "_dram": v for k, v in arrays.items()}], core_ids=[0])
    return np.asarray(r.results[0]["out_dram"]).reshape(NB, S, D)
```

```python
from contextlib import ExitStack

import concourse.bass as bass
import numpy as np
from concourse import mybir

F32 = mybir.dt.float32
BF16 = mybir.dt.bfloat16
F32R = mybir.dt.float32r
U32 = mybir.dt.uint32
I32 = mybir.dt.int32
ALU = mybir.AluOpType
ACT = mybir.ActivationFunctionType
AX = mybir.AxisListType
RMAX = bass.bass_isa.ReduceOp.max

P = 128
NB, S, D = 4, 256, 128
NT = NB * S // P
TOK = NB * S
NH, DH = 16, 8
NPART = 3
STACK = NPART * NPART * DH
E = 8
NH3, DH3 = 8, 64
CI, NI = 88, 4
EPS = 1e-5
PIECE = 256
PIECES = {0: 6, 2: 2}
PIECE_AT = {0: [0, 1, 2, 3, 4, 5], 2: [0, 3]}
JOBS = {0: 8, 2: 4}
TURN, WEIGH = 2, 3
WIDE = 128
BIG = 1e30
ROUND = 1.5 * 2.0 ** 23
QMAX = 127.0
LEAD = 8
STAGE, SKEW = 4, 8
SLICE8 = float(DH) ** -0.5

UNITS8 = [(t, h, (4, 2)[t % 2], (128, 256)[t % 2]) for t in range(NT) for h in range(0, NH, (4, 2)[t % 2])]
UNITS1 = [(2 * b, 0, 2, 256) for b in range(NB)]
UNITS3 = [(t, h, 1, 512) for t in range(NT) for h in range(NH3)]
N8, N1, N3 = len(UNITS8), len(UNITS1), len(UNITS3)
BASE = {0: 0, 1: N8, 2: N8 + N1, 3: 2 * N8 + N1}
UNITS = {0: UNITS8, 1: UNITS1, 2: UNITS8, 3: UNITS3}
LAST = {k: [i for i, u in enumerate(v) if i + 1 == len(v) or v[i + 1][0] != u[0]] for k, v in UNITS.items()}
GROUPS = {0: 0, 1: 8, 2: 12, 3: 20}
COPIER = ["V"] * (2 * N8 + N1) + ["AV"[i % 2] for i in range(N3)]


def _plan_misc():
    m = []

    def add(name, n, who):
        m.extend((f"{name}.{i}", who) for i in range(n))

    add("k0", 2, "A"); add("v0", 2, "V")
    add("ln0", 2, "A"); add("q0", 2, "A"); add("qer", N8, "A")
    add("ln1", 2, "A"); add("router0", 1, "V"); add("cwT0", 2, "V"); add("yT0", 2, "V")
    add("k1", 2, "A"); add("v1", 2, "V"); add("ln2", 2, "A"); add("q1", 2, "A")
    add("wgT", 1, "V"); add("wuT", 1, "V"); add("wdT", 1, "V"); add("wdrow", 1, "V")
    add("ln3", 2, "A")
    add("k2", 2, "A"); add("v2", 2, "V"); add("mean", 2, "V"); add("ln4", 2, "A"); add("q2", 2, "A")
    add("oT2", 2, "A"); add("wo2", 2, "V")
    add("ln5", 2, "A"); add("router2", 1, "V"); add("cwT2", 2, "V"); add("yT2", 2, "V")
    add("lnc", 2, "V")
    for c in range(4):
        for n in range(2):
            m.append((f"kc.{c}.{n}", "V")); m.append((f"kr.{c}.{n}", "V"))
    for t in range(NT):
        m.append((f"vc.{t}", "AV"[t % 2]))
    add("ln8", 2, "V")
    for c in range(4):
        for n in range(2):
            m.append((f"kl.{c}.{n}", "A")); m.append((f"q3.{c}.{n}", "A"))
    for t in range(NT):
        m.append((f"vl.{t}", "AV"[t % 2]))
    for i in range(N3 + WEIGH + 3):
        if i - WEIGH - 1 in LAST[3]:
            m.append((f"oT3.{LAST[3].index(i - WEIGH - 1)}", "A"))
        if i - WEIGH - 2 in LAST[3]:
            m.append((f"wo3.{LAST[3].index(i - WEIGH - 2)}", "V"))
    add("ln9", 2, "A"); add("router3", 1, "V")
    for t in range(NT + 2):
        if t < NT:
            m.append((f"uv.{t}", "V"))
        if 1 <= t <= NT:
            m.append((f"sT.{t - 1}", "A"))
        if t >= 2:
            m.append((f"y3.{t - 2}", "V"))
    return m


MISC = _plan_misc()
AT = {name: i for i, (name, _) in enumerate(MISC)}
EMPTIED = [sum(w == who for _, w in MISC[:i + 1]) for i, (_, who) in enumerate(MISC)]


def build(nc, I, out):
    with ExitStack() as ctx:
        def sb(name, shape, dt=F32):
            return ctx.enter_context(nc.sbuf_tensor(name, shape, dt))

        def sem(name):
            return ctx.enter_context(nc.semaphore(name))

        def dram(name, shape, dt):
            return nc.dram_tensor(name, shape, dt, kind="Internal").ap()

        x = sb("x", [P, NT, D])
        ctxr = sb("ctxr", [P, NT, D])
        ctxT = sb("ctxT", [P, TOK])
        xn = sb("xn", [P, NT, D])
        xnT = sb("xnT", [P, TOK])
        cnT = sb("cnT", [P, TOK])
        arenaA = sb("arenaA", [P, 16384])
        QS = arenaA[0:STACK, 0:8192].bitcast(BF16).rearrange("p (h t) -> p h t", h=NH)
        KS = arenaA[0:STACK, 8192:16384].bitcast(BF16).rearrange("p (h t) -> p h t", h=NH)
        KT3 = arenaA[:, 0:8192].rearrange("p (c b k) -> p c b k", c=4, b=NB)
        QT3 = arenaA[:, 8192:8192 + 4096].rearrange("p (c t) -> p c t", c=4)
        arenaB = sb("arenaB", [P, 8320])
        stage = arenaB[:, 0:STAGE * 512].rearrange("p (n w) -> p n w", n=STAGE)
        skewed = arenaB[:, STAGE * 512:(STAGE + SKEW) * 512].rearrange("p (n w) -> p n w", n=SKEW)
        cwB = arenaA[:, 0:8192].rearrange("p (e t) -> p e t", e=E)
        at_b = nc.sbuf_base - 8320 * 4

        def place(name, at, shape):
            return nc.alloc_sbuf_tensor_at(name, shape, F32R, offset=at)

        wh = place("wh", at_b, [P, 2, 1536])
        wl = place("wl", at_b + 4 * 3072, [P, 2, 1536])
        hh = place("hh", at_b + 4 * 6144, [P, 2, 512])
        hl = place("hl", at_b + 4 * 7168, [P, 2, 512])
        h1 = arenaB[:, 0:4096].rearrange("p (c t) -> p c t", c=NI)
        h1q = arenaB[:, 4096:6144].bitcast(BF16).rearrange("p (c t) -> p c t", c=NI)
        VX = arenaB[:, 0:8320].rearrange("p (k h e) -> p k h e", k=16, h=NH3)
        ring = sb("ring", [P, 2, 1536])
        qparts = ring[:, 0, :].bitcast(BF16).rearrange("p (a t) -> p a t", a=NPART)
        kparts = ring[:, 1, :].bitcast(BF16).rearrange("p (a t) -> p a t", a=NPART)
        qkf = sb("qkf", [P, 2, TOK])
        at_q = nc.sbuf_base - 2 * TOK * 4
        xh, xl = place("xh", at_q, [P, TOK]), place("xl", at_q + 4 * TOK, [P, TOK])
        qf, kf = qkf[:, 0, :], qkf[:, 1, :]
        rope = qkf[:, :, :].rearrange("p a (n t) -> p a n t", n=2)
        v9 = sb("v9", [P, NT * NH * (DH + 1) + WIDE])
        V9 = v9[:, 0:NT * NH * (DH + 1)].rearrange("p (t h e) -> p t h e", t=NT, h=NH)
        VA = sb("VA", [P, NT, D + 1])
        Sx = sb("Sx", [P, 2, 512])
        PR = sb("PR", [P, 2, 512])
        PT = sb("PT", [P, 2, 512])
        sg = sb("sg", [P, 2, 512])
        stage3 = sb("stage3", [P, 512])
        xq = sb("xq", [P, TOK], BF16)
        ones = sb("ones", [P, P])
        identb = sb("identb", [P, P], BF16)
        maskb = sb("maskb", [P, 2, 512], BF16)
        erp = sb("erp", [DH, NPART, S], BF16)
        erf = sb("erf", [DH, S])
        ES = sb("ES", [STACK, S], BF16)
        mrow = sb("mrow", [1, TOK])
        mk2 = sb("mk2", [P, NT])
        mean = sb("mean", [P, NB, NH, DH + 1])
        cwT = sb("cwT", [E, TOK])
        tg = sb("tg", [P, 8])
        small = sb("small", [P, 64])
        nbq0, nbq1 = small[:, 0:1], small[:, 1:2]
        amx, sx, isx, gx = small[:, 2:3], small[:, 3:4], small[:, 4:5], small[:, 5:6]
        amh, sh, ish, fac = small[:, 6:7], small[:, 7:8], small[:, 8:9], small[:, 9:10]
        amxg, amhg = small[:, 10:11], small[:, 11:12]
        sg2 = small[:, 12:14]
        wgs, wus, wds = small[0:CI, 16:20], small[0:CI, 20:24], small[:, 24:25]
        iwg, iwu, iwd = small[0:CI, 28:32], small[0:CI, 32:36], small[:, 36:37]
        fg, fu = small[0:CI, 40:44], small[0:CI, 44:48]
        mhalf = sb("mhalf", [P, NT])
        st = sb("st", [P, NT, 6])
        mv = sb("mv", [P, NT, 2])
        veps = sb("veps", [P, NT])
        rstd = sb("rstd", [P, NT])
        smin = sb("smin", [P, 2, 4])
        rsum = sb("rsum", [P, NH])
        lg = sb("lg", [P, NT, E])
        lmx = sb("lmx", [P, NT, 8])
        lix = sb("lix", [P, NT, 8], U32)
        lixf = sb("lixf", [P, NT, 8])
        rw = sb("rw", [P, 4, NT])
        oh = sb("oh", [P, 2, NT, E])
        cw = sb("cw", [P, NT, E])
        wgT = sb("wgT", [P, NI * CI], BF16)
        wuT = sb("wuT", [P, NI * CI], BF16)
        wdT = sb("wdT", [CI, NI, D], BF16)
        wdrow = sb("wdrow", [P, D])
        diag = sb("diag", [P, P])
        loads = {}

        def load(name, shape, dt=F32):
            loads[name] = (sb("in_" + name, shape, dt), sem("ld_" + name))
            return loads[name][0]

        ident = load("ident", [P, P]); maskf = load("maskf", [P, P]); iota = load("iota", [P, E])
        cos = load("cos", [P, S]); sin = load("sin", [P, S])
        gates = load("gates", [P, 8]); clips = load("clips", [P, 2])
        wq0 = load("wq0", [D, D]); wk0 = load("wk0", [D, D]); wv0 = load("wv0", [D, D])
        b0 = load("b0", [D, 2]); bv0 = load("bv0", [P, D])
        wq1 = load("wq1", [D, D]); wk1 = load("wk1", [D, D]); wv1 = load("wv1", [D, D])
        b1 = load("b1", [D, 2]); bv1 = load("bv1", [P, D])
        wq2 = load("wq2", [D, D]); wk2 = load("wk2", [D, D]); wv2 = load("wv2", [D, D]); wo2 = load("wo2", [D, D])
        maski = load("maski", [P, NT], I32)
        wr0 = load("wr0", [D, E]); br0 = load("br0", [P, E])
        hb1 = load("hb1", [P, E, 4]); hb2 = load("hb2", [P, E, 4]); hb3 = load("hb3", [E, D])
        wr2 = load("wr2", [D, E]); br2 = load("br2", [P, E])
        gb1 = load("gb1", [P, E, 2]); gb2 = load("gb2", [E, D])
        wg = load("wg", [CI, NI, D]); wu = load("wu", [CI, NI, D]); wd = load("wd", [D, NI * CI])
        lnp = load("lnp", [D, 4])
        wr3 = load("wr3", [D, E])

        def load_late(name, at, n):
            loads[name] = (arenaA[:, 12288 + at:12288 + at + n], sem("ld_" + name))
            return loads[name][0]

        wq3, wkv3, wkr3 = load_late("wq3", 0, 512), load_late("wkv3", 512, 1024), load_late("wkr3", 1536, 512)
        wo3 = load_late("wo3", 2048, 512).rearrange("p (c d) -> p c d", c=4)
        wuv = load_late("wuv", 2560, 512)
        wf3 = load_late("wf3", 3072, 256).rearrange("p (c d) -> p c d", c=2)

        ps = ctx.enter_context(nc.psum_tensor("ps", [P, 8, 512], F32))
        SC = [ps[:, 0, :], ps[:, 1, :]]
        TP = [ps[:, 2, :], ps[:, 3, :]]
        OB = [ps[:, 4, :], ps[:, 5, :]]
        MB = [ps[:, 6, :], ps[:, 7, :]]

        relpos = dram("relpos", (N8, P, 512), F32)
        qpd = dram("qpd", (2, NPART, P, TOK), BF16)
        kpd = dram("kpd", (2, NPART, P, TOK), BF16)
        cwd = dram("cwd", (2, E, TOK), F32)

        ld_x, ld_ctx, ld_ctxT, ld_er, ld_mrow = (sem("ld_" + n) for n in ("x", "ctx", "ctxT", "er", "mrow"))
        stats_ready, moments_ready, variance_ready = sem("stats_ready"), sem("moments_ready"), sem("variance_ready")
        rstd_ready, rows_normed, x_updated = sem("rstd_ready"), sem("rows_normed"), sem("x_updated")
        misc_ready, misc_emptied_v, misc_emptied_a = sem("misc_ready"), sem("misc_emptied_v"), sem("misc_emptied_a")
        v_step, a_step, g_step = sem("v_step"), sem("a_step"), sem("g_step")
        constants_ready = sem("constants_ready")
        nbq_ready, gates_ready, sig_exp, pool_consts = sem("nbq_ready"), sem("gates_ready"), sem("sig_exp"), sem("pool_consts")
        kparts_ready, qparts_ready, erparts_ready = sem("kparts_ready"), sem("qparts_ready"), sem("erparts_ready")
        kp_stored, qp_stored = sem("kp_stored"), sem("qp_stored")
        ks_loaded, qs_loaded, es_loaded = sem("ks_loaded"), sem("qs_loaded"), sem("es_loaded")
        rel_stored = [sem(f"rel_stored{i}") for i in range(STAGE)]
        rel_loaded = [sem(f"rel_loaded{i}") for i in range(SKEW)]
        rel_masked = sem("rel_masked")
        scores_ready, min_ready, probs_ready = sem("scores_ready"), sem("min_ready"), sem("probs_ready")
        probsT_ready, pv_done, out_read = sem("probsT_ready"), sem("pv_done"), sem("out_read")
        probsT_copied = {"V": sem("probsT_copied_v"), "A": sem("probsT_copied_a")}
        mask_ready = sem("mask_ready")
        weights_scaled = sem("weights_scaled")
        xmax_ready, xmax_all, xq_ready = sem("xmax_ready"), sem("xmax_all"), sem("xq_ready")
        hmax_ready, hmax_all, hq_ready = sem("hmax_ready"), sem("hmax_all"), sem("hq_ready")
        l1_gate, l1_silu, l1_up, l1_hidden, l1_down = (sem("l1_" + n) for n in ("gate", "silu", "up", "hidden", "down"))
        router_in, router_exp, cw_ready = sem("router_in"), sem("router_exp"), sem("cw_ready")
        moe = {l: {n: sem(f"moe{l}_{n}") for n in ("gate", "act", "up", "mixed", "scaled", "hi", "lo", "down", "raw0",
                                                   "raw1", "w_hi", "w_lo", "x_hi", "x_lo", "summed")} for l in (0, 2)}
        cw_stored, cw_loaded = sem("cw_stored"), [sem(f"cw_loaded{e}") for e in range(E)]
        rope_in, rope_done, vones = sem("rope_in"), sem("rope_done"), sem("vones")
        heads_ready = sem("heads_ready")
        silu3, s3_ready, out_ready, out_stored = sem("silu3"), sem("s3_ready"), sem("out_ready"), sem("out_stored")

        block = ctx.enter_context(nc.Block())

        def loaded(eng, *names):
            for n in names:
                eng.wait_ge(loads[n][1], 16)

        def emptied(eng, name):
            i = AT[name]
            eng.wait_ge(misc_emptied_v if MISC[i][1] == "V" else misc_emptied_a, EMPTIED[i])

        def filled(eng, name):
            eng.wait_ge(misc_ready, AT[name] + 1)
            return MB[AT[name] % 2]

        def copied(eng, u):
            eng.wait_ge(probsT_copied[COPIER[u]], sum(c == COPIER[u] for c in COPIER[:u + 1]))

        def bc(ap, n):
            return ap.unsqueeze(2).to_broadcast([ap.shape[0], ap.shape[1], n])

        @block.sync
        def _(sp):
            def fetch(name, ap):
                sp.dma_start(loads[name][0][:], ap).then_inc(loads[name][1], 16)

            sp.dma_start(x[:], I["x"].rearrange("(t p) d -> p t d", p=P)).then_inc(ld_x, 16)
            sp.dma_start(ctxT[:], I["ctxT"]).then_inc(ld_ctxT, 16)
            for n in ("wk0", "b0", "ident", "wv0"):
                fetch(n, I[n])
            fetch("bv0", I["bv0"].partition_broadcast(P))
            sp.dma_start(erf[:], I["erT"]).then_inc(ld_er, 16)
            for n in ("wq0", "iota", "maskf"):
                fetch(n, I[n])
            fetch("gates", I["gates"].partition_broadcast(P))
            fetch("clips", I["clips"].partition_broadcast(P))
            for n in ("wq1", "wk1", "wv1", "b1", "wq2", "wk2", "wv2", "wo2", "maski", "wr0", "hb1", "hb2",
                      "hb3", "wr2", "gb1", "gb2", "wg", "wu", "wd"):
                fetch(n, I[n])
            for n in ("bv1", "br0", "br2"):
                fetch(n, I[n].partition_broadcast(P))
            sp.dma_start(mrow[:], I["mrow"]).then_inc(ld_mrow, 16)

            def restack(parts_ready, parts, store, stored, stack, stack_loaded, n, key):
                sp.wait_ge(parts_ready, n + 1)
                sp.dma_start(store[n].rearrange("a p t -> p a t"), parts).then_inc(stored, 16)
                sp.wait_ge(stored, 16 * (n + 1))
                for c in range(NPART * NPART):
                    a = c % NPART if key else c // NPART
                    sp.dma_start(stack[c * DH:(c + 1) * DH],
                                 store[n, a].rearrange("(h d) t -> d h t", d=DH)).then_inc(stack_loaded, 16)

            def experts(layer, e):
                m, s = moe[layer], e % 2
                if e >= 2:
                    sp.wait_ge(m["w_lo"], PIECES[layer] * (e - 1))
                if layer == 0:
                    sp.dma_start(ring[:, s, 0:512], I["f1"][e]).then_inc(m[f"raw{s}"], 16)
                    sp.dma_start(ring[:, s, 512:1024], I["f2"][e]).then_inc(m[f"raw{s}"], 16)
                    sp.dma_start(ring[:, s, 1024:1536].rearrange("p (c d) -> p c d", c=4),
                                 I["f3"][e].rearrange("(c p) d -> p c d", p=P)).then_inc(m[f"raw{s}"], 16)
                else:
                    sp.dma_start(ring[:, s, 0:256], I["g1"][e]).then_inc(m[f"raw{s}"], 16)
                    sp.dma_start(ring[:, s, 256:512].rearrange("p (c d) -> p c d", c=2),
                                 I["g2"][e].rearrange("(c p) d -> p c d", p=P)).then_inc(m[f"raw{s}"], 16)

            def spread_coefficients(i, layer):
                emptied(sp, f"cwT{layer}.1")
                sp.dma_start(cwd[i], cwT[:]).then_inc(cw_stored, 16)
                sp.wait_ge(cw_stored, 16 * (i + 1))
                for e in range(E):
                    sp.dma_start(cwB[:, e, :], cwd[i, e].partition_broadcast(P)).then_inc(cw_loaded[e], 16)

            sp.wait_ge(erparts_ready, 1)
            for c in range(NPART * NPART):
                sp.dma_start(ES[c * DH:(c + 1) * DH, :], erp[:, c % NPART, :]).then_inc(es_loaded, 16)
            restack(kparts_ready, kparts, kpd, kp_stored, KS, ks_loaded, 0, True)
            restack(qparts_ready, qparts, qpd, qp_stored, QS, qs_loaded, 0, False)

            def store_rel(r):
                emptied(sp, f"qer.{r}")
                sp.dma_start(relpos[r], stage[:, r % STAGE, :]).then_inc(rel_stored[r % STAGE], 16)

            def load_rel(r):
                w = UNITS8[r][3]
                sp.wait_ge(rel_stored[r % STAGE], 16 * (r // STAGE + 1))
                if r >= SKEW:
                    sp.wait_ge(min_ready, r - SKEW + 1)
                src = bass.AP(relpos.tensor, relpos[r].offset + P - 1, [[512 - 1, P], [w, 512 // w], [1, w]])
                sp.dma_start(skewed[:, r % SKEW, :].rearrange("p (g w) -> p g w", w=w), src) \
                    .then_inc(rel_loaded[r % SKEW], 16)

            for r in range(N8 + 1):
                if r < N8:
                    store_rel(r)
                if r >= 1:
                    load_rel(r - 1)
                if r == 4:
                    sp.wait_ge(qs_loaded, 16 * 9)
                    sp.wait_ge(ks_loaded, 16 * 9)
                    experts(0, 0)
                    experts(0, 1)
            sp.dma_start(ctxr[:], I["ctx"].rearrange("(t p) d -> p t d", p=P)).then_inc(ld_ctx, 16)
            for n in ("cos", "sin", "lnp", "wr3"):
                fetch(n, I[n])
            spread_coefficients(0, 0)
            for e in range(2, E):
                experts(0, e)
            restack(kparts_ready, kparts, kpd, kp_stored, KS, ks_loaded, 1, True)
            restack(qparts_ready, qparts, qpd, qp_stored, QS, qs_loaded, 1, False)
            sp.wait_ge(ks_loaded, 16 * 18)
            sp.wait_ge(qs_loaded, 16 * 18)
            experts(2, 0)
            experts(2, 1)
            sp.wait_ge(scores_ready, BASE[3])
            for n in ("wq3", "wkv3", "wkr3", "wo3", "wuv", "wf3"):
                fetch(n, I[n])
            spread_coefficients(1, 2)
            for e in range(2, E):
                experts(2, e)
            for t in range(NT):
                sp.wait_ge(x_updated, 8 * NT - NT + t + 1)
                sp.dma_start(out[t * P:(t + 1) * P, :], x[:, t, :]).then_inc(out_stored, 16)
            sp.wait_ge(out_stored, 16 * NT)

        @block.gpsimd
        def _(pool):
            nc.gpsimd.memset(ones[:], 1.0).then_inc(pool_consts, 1)
            nc.gpsimd.memset(mhalf[:], -0.5).then_inc(pool_consts, 1)
            nc.gpsimd.memset(V9[:, :, :, DH:DH + 1], 1.0).then_inc(pool_consts, 1)
            nc.gpsimd.memset(v9[:, NT * NH * (DH + 1):], 0.0).then_inc(pool_consts, 1)
            nc.gpsimd.memset(VA[:, :, D:D + 1], 1.0).then_inc(pool_consts, 1)
            nc.gpsimd.memset(amh, 0.0).then_inc(pool_consts, 1)

            count = [0]

            def link(ins):
                count[0] += 1
                ins.then_inc(g_step, 1)
                pool.wait_ge(g_step, count[0])

            def rsqrt(n):
                if n == 0:
                    pool.wait_ge(pool_consts, 2)
                pool.wait_ge(variance_ready, n + 1)
                nc.gpsimd.tensor_tensor(rstd[:], veps[:], mhalf[:], ALU.pow).then_inc(rstd_ready, 1)

            def split_keys(n, names):
                for name in names:
                    emptied(pool, name)
                link(nc.gpsimd.tensor_copy(kparts[:, 0, :], kf))
                link(nc.gpsimd.tensor_tensor(kf, kf, kparts[:, 0, :], ALU.subtract))
                link(nc.gpsimd.tensor_copy(kparts[:, 1, :], kf))
                nc.gpsimd.tensor_tensor(kparts[:, 2, :], kf, kparts[:, 1, :], ALU.subtract).then_inc(kparts_ready, 1)

            rsqrt(0)
            split_keys(0, ("k0.0", "k0.1"))
            for r in range(N8):
                w = UNITS8[r][3]
                pool.wait_ge(rel_loaded[r % SKEW], 16 * (r // SKEW + 1))
                v = skewed[:, r % SKEW, :].rearrange("p (g w) -> p g w", w=w)[:, :, w - P:w]
                nc.gpsimd.affine_select(out=v, in_=v, pattern=[[0, 512 // w], [-1, P]], compare_op=ALU.is_ge,
                                        fill=BIG, base=0, channel_multiplier=1).then_inc(rel_masked, 1)
            def split_piece(e, k):
                m, s, a = moe[0], e % 2, PIECE * k
                pool.wait_ge(m["w_hi"], PIECES[0] * e + k + 1)
                nc.gpsimd.tensor_tensor(wl[:, s, a:a + PIECE], ring[:, s, a:a + PIECE],
                                        wh[:, s, a:a + PIECE].bitcast(F32), ALU.subtract).then_inc(m["w_lo"], 1)

            rsqrt(1)
            for k in range(PIECES[0]):
                split_piece(0, k)
            m = moe[0]
            for j in range(E * 8):
                e, n = j // 8, j % 2
                if j % 8 == 0:
                    pool.wait_ge(cw_loaded[e], 16)
                pool.wait_ge(m["mixed"], j + 1)
                if j >= 2:
                    pool.wait_ge(m["lo"], j - 1)
                nc.gpsimd.tensor_tensor(PT[:, j % 2, :], PR[:, j % 2, :], cwB[:, e, 512 * n:512 * n + 512],
                                        ALU.mult).then_inc(m["scaled"], 1)
                if e + 1 < E and j % 8 in PIECE_AT[0]:
                    split_piece(e + 1, PIECE_AT[0].index(j % 8))
            for n in (2, 3):
                rsqrt(n)
            pool.wait_ge(xmax_ready, 1)
            nc.gpsimd.partition_all_reduce(amxg, amx, P, RMAX).then_inc(xmax_all, 1)
            pool.wait_ge(hmax_ready, 1)
            nc.gpsimd.partition_all_reduce(amhg, amh, P, RMAX).then_inc(hmax_all, 1)
            split_keys(1, ("k2.0", "k2.1"))
            rsqrt(4)
            rsqrt(5)
            m = moe[2]
            for j in range(E * 4):
                pool.wait_ge(m["hi"], j + 1)
                if j >= 2:
                    pool.wait_ge(m["down"], j - 1)
                nc.gpsimd.tensor_tensor(hl[:, j % 2, :], PT[:, j % 2, :], hh[:, j % 2, :].bitcast(F32),
                                        ALU.subtract).then_inc(m["lo"], 1)
            rsqrt(6)
            pool.wait_ge(m["down"], E * 4)
            nc.gpsimd.memset(VX[:, :, :, DH3:DH3 + 1], 1.0).then_inc(vones, 1)
            for k in range(8):
                c, n = k // 2, k % 2
                pool.wait_ge(rope_in, k + 1)
                nc.gpsimd.tensor_tensor(KT3[:, c, 2 * n:2 * n + 2, 0:S],
                                        rope[:, 0, k % 2, :].rearrange("p (b t) -> p b t", b=2),
                                        rope[:, 1, k % 2, :].rearrange("p (b t) -> p b t", b=2),
                                        ALU.add).then_inc(rope_done, 1)
            rsqrt(7)
            rsqrt(8)
            rsqrt(9)

        @block.scalar
        def _(act):
            loaded(act, "gates", "clips")
            nc.scalar.activation(tg[:], gates[:], ACT.Tanh).then_inc(gates_ready, 1)
            nc.scalar.activation(sg2, clips[:], ACT.Exp, scale=-1.0).then_inc(sig_exp, 1)

            def take(name, dst, func=ACT.Copy, **kw):
                bank = filled(act, name)
                nc.scalar.activation(dst, bank, func, **kw).then_inc(misc_emptied_a, 1)

            def halves(name, dst, func=ACT.Copy, **kw):
                for n in range(2):
                    take(f"{name}.{n}", dst[:, 512 * n:512 * n + 512], func, **kw)

            def rel(r):
                if r >= STAGE:
                    act.wait_ge(rel_stored[r % STAGE], 16 * (r // STAGE))
                take(f"qer.{r}", stage[:, r % STAGE, :])

            def exps(layer, i):
                _, _, g, w = UNITS[layer][i]
                u = BASE[layer] + i
                act.wait_ge(min_ready, u + 1)
                if u >= 2:
                    act.wait_ge(probsT_ready, u - 1)
                src = Sx[:, u % 2, :] if layer == 0 else SC[u % 2]
                for k in range(g):
                    ins = nc.scalar.activation(PR[:, u % 2, k * w:(k + 1) * w], src[:, k * w:(k + 1) * w], ACT.Exp,
                                               bias=smin[:, u % 2, k:k + 1], scale=-1.0)
                ins.then_inc(probs_ready, 1)

            def copy_probs(layer, i):
                u = BASE[layer] + i
                if COPIER[u] == "A":
                    act.wait_ge(probsT_ready, u + 1)
                    if u >= 2:
                        act.wait_ge(pv_done, u - 1)
                    nc.scalar.activation(PT[:, u % 2, :], TP[u % 2], ACT.Copy).then_inc(probsT_copied["A"], 1)

            def attention(layer):
                for i in range(len(UNITS[layer]) + WEIGH + 2):
                    if layer == 0 and i + LEAD < N8:
                        rel(i + LEAD)
                    if i < len(UNITS[layer]):
                        exps(layer, i)
                    if 0 <= i - TURN < len(UNITS[layer]):
                        copy_probs(layer, i - TURN)
                    if layer == 3 and i - WEIGH - 1 in LAST[3]:
                        t = LAST[3].index(i - WEIGH - 1)
                        if t >= 1:
                            emptied(act, f"wo3.{t - 1}")
                        take(f"oT3.{t}", sg[:, 0, :])

            def round_piece(layer, e, k):
                m, s, a = moe[layer], e % 2, PIECE * k
                if k == 0:
                    act.wait_ge(m[f"raw{s}"], (48 if layer == 0 else 32) * (e // 2 + 1))
                    if e >= 2:
                        act.wait_ge(m["up" if layer == 0 else "gate"], JOBS[layer] * (e - 1))
                if e >= 2 and a >= (1024 if layer == 0 else 256):
                    act.wait_ge(m["down"], JOBS[layer] * (e - 1))
                nc.scalar.activation(wh[:, s, a:a + PIECE], ring[:, s, a:a + PIECE], ACT.Copy).then_inc(m["w_hi"], 1)

            def next_piece(layer, j):
                e, k = j // JOBS[layer], j % JOBS[layer]
                if e + 1 < E and k in PIECE_AT[layer]:
                    round_piece(layer, e + 1, PIECE_AT[layer].index(k))

            def round_rows(layer):
                emptied(act, f"ln{5 if layer else 1}.1")
                nc.scalar.activation(xh[:], xnT[:], ACT.Copy).then_inc(moe[layer]["x_hi"], 1)

            def experts0():
                m = moe[0]
                for j in range(E * 8 + 1):
                    if j < E * 8:
                        e, c = j // 8, j // 2 % 4
                        act.wait_ge(m["gate"], j + 1)
                        if j >= 2:
                            act.wait_ge(m["mixed"], j - 1)
                        nc.scalar.activation(sg[:, j % 2, :], SC[j % 2], ACT.Silu, bias=hb1[:, e, c:c + 1]) \
                            .then_inc(m["act"], 1)
                    if j >= 1:
                        act.wait_ge(m["scaled"], j)
                        if j >= 3:
                            act.wait_ge(m["down"], j - 2)
                        nc.scalar.activation(hh[:, (j - 1) % 2, :], PT[:, (j - 1) % 2, :], ACT.Copy) \
                            .then_inc(m["hi"], 1)
                    next_piece(0, j)

            def experts2():
                m = moe[2]
                for j in range(E * 4):
                    e, c = j // 4, j // 2 % 2
                    act.wait_ge(m["gate"], j + 1)
                    if j >= 2:
                        act.wait_ge(m["scaled"], j - 1)
                    nc.scalar.activation(sg[:, j % 2, :], SC[j % 2], ACT.Gelu, bias=gb1[:, e, c:c + 1]) \
                        .then_inc(m["act"], 1)
                    next_piece(2, j)

            def take_sums(layer):
                for n in range(2):
                    act.wait_ge(moe[layer]["down"], E * (8 if layer == 0 else 4) - 1 + n)
                    nc.scalar.activation(xnT[:, 512 * n:512 * n + 512], OB[n], ACT.Copy).then_inc(moe[layer]["summed"], 1)

            def router(n):
                act.wait_ge(router_in, n + 1)
                if n == 1:
                    nc.scalar.activation(lg[:], lg[:], ACT.Exp).then_inc(router_exp, 1)
                else:
                    nc.scalar.activation(rw[:, 1, :], rw[:, 0, :], ACT.Exp).then_inc(router_exp, 1)

            loaded(act, "b0")
            halves("k0", kf, ACT.Identity, bias=b0[:, 1:2])
            halves("ln0", xnT)
            act.wait_ge(nbq_ready, 1)
            halves("q0", qf, ACT.Identity, bias=nbq0, scale=-SLICE8)
            for r in range(LEAD):
                rel(r)
            attention(0)
            for k in range(PIECES[0]):
                round_piece(0, 0, k)
            halves("ln1", xnT)
            round_rows(0)
            router(0)
            loaded(act, "hb1")
            experts0()
            take_sums(0)
            loaded(act, "b1")
            halves("k1", kf, ACT.Identity, bias=b1[:, 1:2])
            halves("ln2", xnT)
            act.wait_ge(nbq_ready, 2)
            halves("q1", qf, ACT.Identity, bias=nbq1, scale=-SLICE8)
            attention(1)
            halves("ln3", xnT)
            for j in range(2 * NI):
                act.wait_ge(l1_gate, j + 1)
                if j >= 2:
                    act.wait_ge(l1_hidden, j - 1)
                if j == 0:
                    act.wait_ge(xq_ready, 1)
                nc.scalar.activation(sg[0:CI, j % 2, :], SC[j % 2][0:CI, :], ACT.Silu,
                                     scale=fg[:, j // 2:j // 2 + 1]).then_inc(l1_silu, 1)
            halves("k2", kf)
            halves("ln4", xnT)
            halves("q2", qf, scale=-SLICE8)
            attention(2)
            halves("oT2", xnT)
            for k in range(PIECES[2]):
                round_piece(2, 0, k)
            halves("ln5", xnT)
            round_rows(2)
            router(1)
            loaded(act, "gb1")
            experts2()
            take_sums(2)
            act.wait_ge(vones, 1)

            def values(kind):
                for t in range(0, NT, 2):
                    k = 4 * (t // 2) + 2 * (kind == "vl")
                    bank = filled(act, f"{kind}.{t}")
                    nc.scalar.activation(VX[:, k, :, 0:DH3], bank.rearrange("p (h e) -> p h e", h=NH3),
                                         ACT.Copy).then_inc(misc_emptied_a, 1)

            values("vc")
            for c in range(4):
                for n in range(2):
                    bank = filled(act, f"kl.{c}.{n}")
                    nc.scalar.activation(KT3[:, c, 2 * n:2 * n + 2, S:2 * S], bank.rearrange("p (b t) -> p b t", b=2),
                                         ACT.Copy).then_inc(misc_emptied_a, 1)
                    take(f"q3.{c}.{n}", QT3[:, c, 512 * n:512 * n + 512], scale=-float(DH3) ** -0.5)
            values("vl")
            attention(3)
            halves("ln9", xnT)
            router(2)
            for t in range(NT + 2):
                if t < NT:
                    bank = filled(act, f"uv.{t}")
                    if t >= 2:
                        act.wait_ge(s3_ready, t - 1)
                    nc.scalar.activation(sg[:, t % 2, 0:256], bank[:, 0:256], ACT.Silu).then_inc(silu3, 1)
                if 1 <= t <= NT:
                    bank = filled(act, f"sT.{t - 1}")
                    if t - 1 >= 2:
                        filled(act, f"y3.{t - 3}")
                    nc.scalar.activation(PT[:, (t - 1) % 2, 0:256], bank[:, 0:256], ACT.Copy).then_inc(misc_emptied_a, 1)

        @block.vector
        def _(dve):
            count = [0]

            def link(ins):
                count[0] += 1
                ins.then_inc(v_step, 1)
                dve.wait_ge(v_step, count[0])

            def norm_rows(n, src, k=None, ready=None):
                for t in range(NT):
                    if k is not None and k > 0:
                        dve.wait_ge(x_updated, NT * (k - 1) + t + 1)
                    nc.vector.bn_stats(st[:, t, :], src[:, t, :]).then_inc(stats_ready, 1)
                for t in range(NT):
                    dve.wait_ge(stats_ready, NT * n + t + 1)
                    nc.vector.bn_aggr(mv[:, t, :], st[:, t, :]).then_inc(moments_ready, 1)
                dve.wait_ge(moments_ready, NT * (n + 1))
                nc.vector.tensor_scalar(veps[:], mv[:, :, 1], EPS, None, ALU.add).then_inc(variance_ready, 1)
                dve.wait_ge(rstd_ready, n + 1)
                for t in range(NT):
                    nc.vector.tensor_scalar(xn[:, t, :], src[:, t, :], mv[:, t, 0:1], rstd[:, t:t + 1],
                                            ALU.subtract, ALU.mult).then_inc(rows_normed, 1)

            def take_rows(name, dst, add=None):
                bank = filled(dve, name)
                v = bank.rearrange("p (t e) -> p t e", t=4)
                if add is None:
                    nc.vector.tensor_copy(dst, v).then_inc(misc_emptied_v, 1)
                else:
                    nc.vector.tensor_tensor(dst, v, add, ALU.add).then_inc(misc_emptied_v, 1)

            def values8(name, bias):
                for n in range(2):
                    bank = filled(dve, f"{name}.{n}")
                    for k in range(4):
                        dst = V9[:, 4 * n + k, :, 0:DH]
                        v = bank[:, 128 * k:128 * k + 128].rearrange("p (h e) -> p h e", h=NH)
                        if bias is None:
                            ins = nc.vector.tensor_copy(dst, v)
                        else:
                            ins = nc.vector.tensor_tensor(dst, v, bias[:].rearrange("p (h e) -> p h e", h=NH), ALU.add)
                    ins.then_inc(misc_emptied_v, 1)

            def split_queries(name):
                for n in range(2):
                    emptied(dve, f"{name}.{n}")
                link(nc.vector.tensor_copy(qparts[:, 0, :], qf))
                link(nc.vector.tensor_tensor(qf, qf, qparts[:, 0, :], ALU.subtract))
                link(nc.vector.tensor_copy(qparts[:, 1, :], qf))
                nc.vector.tensor_tensor(qparts[:, 2, :], qf, qparts[:, 1, :], ALU.subtract).then_inc(qparts_ready, 1)

            def minima(layer, i):
                _, _, g, w = UNITS[layer][i]
                u = BASE[layer] + i
                dve.wait_ge(scores_ready, u + 1)
                if u >= 2:
                    dve.wait_ge(probs_ready, u - 1)
                if layer == 0:
                    dve.wait_ge(rel_masked, i + 1)
                    for k in range(g):
                        ins = nc.vector.tensor_tensor_reduce(
                            Sx[:, u % 2, k * w:(k + 1) * w], SC[u % 2][:, k * w:(k + 1) * w],
                            skewed[:, i % SKEW, k * w:(k + 1) * w], 1.0, 3e38, ALU.add, ALU.min,
                            smin[:, u % 2, k:k + 1])
                    ins.then_inc(min_ready, 1)
                else:
                    nc.vector.tensor_reduce(smin[:, u % 2, 0:g], SC[u % 2].rearrange("p (g w) -> p g w", w=w),
                                            AX.X, ALU.min).then_inc(min_ready, 1)

            def copy_probs(layer, i):
                u = BASE[layer] + i
                if COPIER[u] == "V":
                    dve.wait_ge(probsT_ready, u + 1)
                    if u >= 2:
                        dve.wait_ge(pv_done, u - 1)
                    nc.vector.tensor_copy(PT[:, u % 2, :], TP[u % 2]).then_inc(probsT_copied["V"], 1)

            def finish(layer, k):
                u = BASE[layer] + LAST[layer][k]
                g = GROUPS[layer] + k
                dve.wait_ge(pv_done, u + 1)
                if layer in (0, 2):
                    O = OB[g % 2][:, 0:NH * (DH + 1)].rearrange("p (h e) -> p h e", h=NH)
                    link(nc.vector.reciprocal(rsum[:], O[:, :, DH]))
                    y = xn[:, k, :]
                    link_to = nc.vector.tensor_tensor(y.rearrange("p (h e) -> p h e", h=NH), O[:, :, 0:DH],
                                                      bc(rsum[:], DH), ALU.mult)
                    link_to.then_inc(out_read, 1)
                    dve.wait_ge(out_read, g + 1)
                    if layer == 0:
                        nc.vector.scalar_tensor_tensor(x[:, k, :], y, tg[:, 0:1], x[:, k, :], ALU.mult, ALU.add) \
                            .then_inc(x_updated, 1)
                    else:
                        m = mean[:, k // 2, :, 0:DH]
                        yv = y.rearrange("p (h e) -> p h e", h=NH)
                        d = sg[:, 1, 0:D]
                        link(nc.vector.tensor_tensor(d.rearrange("p (h e) -> p h e", h=NH), m, yv, ALU.subtract))
                        nc.vector.scalar_tensor_tensor(y, d, mk2[:, k:k + 1], y, ALU.mult, ALU.add) \
                            .then_inc(heads_ready, 1)
                elif layer == 1:
                    O = OB[g % 2][:, 0:2 * (D + 1)].rearrange("p (t e) -> p t e", t=2)
                    link(nc.vector.reciprocal(rsum[:, 0:2], O[:, :, D]))
                    y = xn[:, 2 * k:2 * k + 2, :]
                    nc.vector.tensor_tensor(y, O[:, :, 0:D], bc(rsum[:, 0:2], D), ALU.mult).then_inc(out_read, 1)
                    dve.wait_ge(out_read, g + 1)
                    for t in (2 * k, 2 * k + 1):
                        nc.vector.scalar_tensor_tensor(x[:, t, :], xn[:, t, :], tg[:, 1:2], x[:, t, :],
                                                       ALU.mult, ALU.add).then_inc(x_updated, 1)
                else:
                    if k >= 1:
                        filled(dve, f"oT3.{k - 1}")
                    for n in range(2):
                        O = OB[n][:, 0:4 * (DH3 + 1)].rearrange("p (h e) -> p h e", h=4)
                        link(nc.vector.reciprocal(rsum[:, 4 * n:4 * n + 4], O[:, :, DH3]))
                        ins = nc.vector.tensor_tensor(stage3[:, 256 * n:256 * n + 256].rearrange("p (h e) -> p h e", h=4),
                                                      O[:, :, 0:DH3], bc(rsum[:, 4 * n:4 * n + 4], DH3), ALU.mult)
                    ins.then_inc(out_read, 1)

            def attention(layer):
                n = len(UNITS[layer])
                for i in range(n + WEIGH + 2):
                    if i < n:
                        minima(layer, i)
                    if 0 <= i - TURN < n:
                        copy_probs(layer, i - TURN)
                    if i - WEIGH in LAST[layer]:
                        finish(layer, LAST[layer].index(i - WEIGH))
                    if layer == 3 and i - WEIGH - 2 in LAST[3]:
                        t = LAST[3].index(i - WEIGH - 2)
                        bank = filled(dve, f"wo3.{t}")
                        dve.wait_ge(x_updated, 6 * NT)
                        nc.vector.scalar_tensor_tensor(x[:, t, :], bank[:, 0:D], tg[:, 3:4], x[:, t, :],
                                                       ALU.mult, ALU.add).then_inc(misc_emptied_v, 1)
                        dve.wait_ge(misc_emptied_v, EMPTIED[AT[f"wo3.{t}"]])
                        nc.vector.tensor_copy(veps[:, t:t + 1], x[:, t, 0:1]).then_inc(x_updated, 1)

            def router(n, name, bias):
                bank = filled(dve, name)
                v = bank[:, 0:NT * E].rearrange("p (t e) -> p t e", t=NT)
                if bias is None:
                    nc.vector.tensor_copy(lg[:], v).then_inc(misc_emptied_v, 1)
                else:
                    nc.vector.tensor_tensor(lg[:], v, bias[:].unsqueeze(1).to_broadcast([P, NT, E]), ALU.add) \
                        .then_inc(misc_emptied_v, 1)
                dve.wait_ge(misc_emptied_v, EMPTIED[AT[name]])
                for t in range(NT):
                    ins = nc.vector.max(lmx[:, t, :], lg[:, t, :])
                link(ins)
                for t in range(NT):
                    ins = nc.vector.max_index(lix[:, t, :], lmx[:, t, :], lg[:, t, :])
                link(ins)
                if n == 1:
                    nc.vector.tensor_tensor(lg[:], lg[:], bc(lmx[:, :, 0], E), ALU.subtract).then_inc(router_in, 1)
                else:
                    nc.vector.tensor_tensor(rw[:, 0, :], lmx[:, :, 1], lmx[:, :, 0], ALU.subtract).then_inc(router_in, 1)
                link(nc.vector.tensor_copy(lixf[:], lix[:]))
                iot = iota[:].unsqueeze(1).to_broadcast([P, NT, E])
                nc.vector.tensor_tensor(oh[:, 0], iot, bc(lixf[:, :, 0], E), ALU.is_equal)
                if n != 1:
                    nc.vector.tensor_tensor(oh[:, 1], iot, bc(lixf[:, :, 1], E), ALU.is_equal)
                dve.wait_ge(router_exp, n + 1)
                if n == 1:
                    link(nc.vector.tensor_reduce(rw[:, 2, :], lg[:], AX.X, ALU.add))
                    link(nc.vector.reciprocal(rw[:, 3, :], rw[:, 2, :]))
                    nc.vector.tensor_tensor(cw[:], oh[:, 0], bc(rw[:, 3, :], E), ALU.mult).then_inc(cw_ready, 1)
                else:
                    link(nc.vector.tensor_scalar(rw[:, 2, :], rw[:, 1, :], 1.0, None, ALU.add))
                    link(nc.vector.reciprocal(rw[:, 3, :], rw[:, 2, :]))
                    link(nc.vector.tensor_tensor(rw[:, 2, :], rw[:, 3, :], rw[:, 1, :], ALU.mult))
                    nc.vector.tensor_tensor(oh[:, 0], oh[:, 0], bc(rw[:, 3, :], E), ALU.mult)
                    link(nc.vector.tensor_tensor(oh[:, 1], oh[:, 1], bc(rw[:, 2, :], E), ALU.mult))
                    nc.vector.tensor_tensor(cw[:], oh[:, 0], oh[:, 1], ALU.add).then_inc(cw_ready, 1)

            def split_rows(layer):
                dve.wait_ge(moe[layer]["x_hi"], 1)
                nc.vector.tensor_tensor(xl[:], xnT[:], xh[:].bitcast(F32), ALU.subtract).then_inc(moe[layer]["x_lo"], 1)

            def take_coefficients(layer):
                for n in range(2):
                    bank = filled(dve, f"cwT{layer}.{n}")
                    nc.vector.tensor_copy(cwT[:, 512 * n:512 * n + 512], bank[0:E, :]).then_inc(misc_emptied_v, 1)

            def experts0():
                m = moe[0]
                for j in range(E * 8 + 1):
                    if j < E * 8:
                        e, c = j // 8, j // 2 % 4
                        dve.wait_ge(m["act"], j + 1)
                        dve.wait_ge(m["up"], j + 1)
                        if j >= 2:
                            dve.wait_ge(m["scaled"], j - 1)
                        nc.vector.scalar_tensor_tensor(PR[:, j % 2, :], TP[j % 2], hb2[:, e, c:c + 1], sg[:, j % 2, :],
                                                       ALU.add, ALU.mult).then_inc(m["mixed"], 1)
                    if j >= 1:
                        dve.wait_ge(m["hi"], j)
                        if j >= 3:
                            dve.wait_ge(m["down"], j - 2)
                        k = (j - 1) % 2
                        nc.vector.tensor_tensor(hl[:, k, :], PT[:, k, :], hh[:, k, :].bitcast(F32), ALU.subtract) \
                            .then_inc(m["lo"], 1)

            def split_piece(e, k):
                m, s, a = moe[2], e % 2, PIECE * k
                dve.wait_ge(m["w_hi"], PIECES[2] * e + k + 1)
                nc.vector.tensor_tensor(wl[:, s, a:a + PIECE], ring[:, s, a:a + PIECE],
                                        wh[:, s, a:a + PIECE].bitcast(F32), ALU.subtract).then_inc(m["w_lo"], 1)

            def experts2():
                m = moe[2]
                for j in range(E * 4):
                    e, n = j // 4, j % 2
                    if j % 4 == 0:
                        dve.wait_ge(cw_loaded[e], 32)
                    dve.wait_ge(m["act"], j + 1)
                    if j >= 2:
                        dve.wait_ge(m["lo"], j - 1)
                    nc.vector.tensor_tensor(PT[:, j % 2, :], sg[:, j % 2, :], cwB[:, e, 512 * n:512 * n + 512],
                                            ALU.mult).then_inc(m["scaled"], 1)
                    if e + 1 < E and j % 4 in PIECE_AT[2]:
                        split_piece(e + 1, PIECE_AT[2].index(j % 4))
                    dve.wait_ge(m["scaled"], j + 1)
                    if j >= 2:
                        dve.wait_ge(m["down"], j - 1)
                    nc.vector.tensor_copy(hh[:, j % 2, :], PT[:, j % 2, :]).then_inc(m["hi"], 1)

            def add_experts(layer, gate):
                for n in range(2):
                    bank = filled(dve, f"yT{layer}.{n}")
                    for k in range(4):
                        t = 4 * n + k
                        ins = nc.vector.scalar_tensor_tensor(x[:, t, :], bank[:, 128 * k:128 * k + 128],
                                                             tg[:, gate:gate + 1], x[:, t, :], ALU.mult, ALU.add)
                        if k < 3:
                            ins.then_inc(x_updated, 1)
                    ins.then_inc(misc_emptied_v, 1)
                    dve.wait_ge(misc_emptied_v, EMPTIED[AT[f"yT{layer}.{n}"]])
                    nc.vector.tensor_copy(veps[:, 0:1], x[:, t, 0:1]).then_inc(x_updated, 1)

            def quantize_weight(w, scales, inverse, nchunk):
                if nchunk == 1:
                    link(nc.vector.tensor_reduce(scales, w, AX.X, ALU.max, apply_absolute_value=True))
                else:
                    link(nc.vector.tensor_reduce(scales, w, AX.X, ALU.max, apply_absolute_value=True))
                link(nc.vector.tensor_scalar(scales, scales, 1.0 / QMAX, None, ALU.mult))
                link(nc.vector.reciprocal(inverse, scales))
                for c in range(nchunk):
                    v = w if nchunk == 1 else w[:, c, :]
                    ins = nc.vector.tensor_scalar(v, v, inverse[:, c:c + 1], QMAX, ALU.mult, ALU.min)
                link(ins)
                link(nc.vector.tensor_scalar(w, w, -QMAX - 1.0, ROUND, ALU.max, ALU.add))
                return nc.vector.tensor_scalar(w, w, ROUND, None, ALU.subtract)

            dve.wait_ge(ld_er, 16)
            link(nc.vector.tensor_copy(erp[:, 0, :], erf[:]))
            link(nc.vector.tensor_tensor(erf[:], erf[:], erp[:, 0, :], ALU.subtract))
            link(nc.vector.tensor_copy(erp[:, 1, :], erf[:]))
            nc.vector.tensor_tensor(erp[:, 2, :], erf[:], erp[:, 1, :], ALU.subtract).then_inc(erparts_ready, 1)
            loaded(dve, "b0")
            nc.vector.tensor_scalar(nbq0, b0[:, 0:1], -SLICE8, None, ALU.mult).then_inc(nbq_ready, 1)
            dve.wait_ge(ld_x, 16)
            norm_rows(0, x)
            loaded(dve, "bv0")
            values8("v0", bv0)
            split_queries("q0")
            loaded(dve, "maskf", "ident", "b1")
            nc.vector.memset(maskb[:, 1, :], 0.0)
            link(nc.vector.tensor_copy(identb[:], ident[:]))
            nc.vector.tensor_copy(maskb[:, 0, :].rearrange("p (g w) -> p g w", g=4),
                                  maskf[:].unsqueeze(1).to_broadcast([P, 4, P]))
            nc.vector.tensor_copy(maskb[:, 1, :].rearrange("p (g w) -> p g w", g=2)[:, :, P:2 * P],
                                  maskf[:].unsqueeze(1).to_broadcast([P, 2, P])).then_inc(mask_ready, 1)
            nc.vector.tensor_scalar(nbq1, b1[:, 0:1], -SLICE8, None, ALU.mult).then_inc(nbq_ready, 1)
            dve.wait_ge(gates_ready, 1)
            attention(0)
            norm_rows(1, x, 1)
            loaded(dve, "br0", "iota", "hb2")
            split_rows(0)
            router(0, "router0.0", br0)
            take_coefficients(0)
            experts0()
            add_experts(0, 4)
            loaded(dve, "bv1")
            for n in range(2):
                take_rows(f"v1.{n}", VA[:, 4 * n:4 * n + 4, 0:D], bv1[:].unsqueeze(1).to_broadcast([P, 4, D]))
            dve.wait_ge(ld_mrow, 16)
            nc.vector.tensor_scalar(mrow[:], mrow[:], -10000.0, 10000.0, ALU.mult, ALU.add).then_inc(mask_ready, 1)
            norm_rows(2, x, 2)
            loaded(dve, "wg", "wu", "wd")
            quantize_weight(wg[:], wgs, iwg, NI).then_inc(weights_scaled, 1)
            quantize_weight(wu[:], wus, iwu, NI).then_inc(weights_scaled, 1)
            quantize_weight(wd[:], wds, iwd, 1).then_inc(weights_scaled, 1)
            nc.vector.tensor_scalar(diag[:], ident[:], wds, None, ALU.mult).then_inc(weights_scaled, 1)
            attention(1)
            for name, dst in (("wgT.0", wgT), ("wuT.0", wuT)):
                bank = filled(dve, name)
                nc.vector.tensor_copy(dst[:], bank[:, 0:NI * CI]).then_inc(misc_emptied_v, 1)
            bank = filled(dve, "wdT.0")
            nc.vector.tensor_copy(wdT[:], bank[0:CI, :].rearrange("p (c d) -> p c d", c=NI)).then_inc(misc_emptied_v, 1)
            bank = filled(dve, "wdrow.0")
            nc.vector.tensor_copy(wdrow[:], bank[:, 0:D]).then_inc(misc_emptied_v, 1)
            dve.wait_ge(sig_exp, 1)
            link(nc.vector.tensor_scalar(sg2, sg2, 1.0, None, ALU.add))
            link(nc.vector.reciprocal(sg2, sg2))
            norm_rows(3, x, 3)
            emptied(dve, "ln3.0")
            emptied(dve, "ln3.1")
            nc.vector.tensor_reduce(amx, xnT[:], AX.X, ALU.max, apply_absolute_value=True).then_inc(xmax_ready, 1)
            dve.wait_ge(xmax_all, 1)
            link(nc.vector.tensor_scalar(sx, amxg, sg2[:, 0:1], 1.0 / QMAX, ALU.mult, ALU.mult))
            nc.vector.tensor_scalar(fg, wgs, sx[0:CI, :], None, ALU.mult)
            nc.vector.tensor_scalar(fu, wus, sx[0:CI, :], None, ALU.mult)
            link(nc.vector.reciprocal(isx, sx))
            link(nc.vector.tensor_scalar(qf, xnT[:], isx, QMAX, ALU.mult, ALU.min))
            link(nc.vector.tensor_scalar(qf, qf, -QMAX - 1.0, ROUND, ALU.max, ALU.add))
            nc.vector.tensor_scalar(xq[:], qf, ROUND, None, ALU.subtract).then_inc(xq_ready, 1)
            for j in range(2 * NI):
                c, n = j // 2, j % 2
                dve.wait_ge(l1_silu, j + 1)
                dve.wait_ge(l1_up, j + 1)
                nc.vector.scalar_tensor_tensor(h1[0:CI, c, 512 * n:512 * n + 512], TP[j % 2][0:CI, :], fu[:, c:c + 1],
                                               sg[0:CI, j % 2, :], ALU.mult, ALU.mult).then_inc(l1_hidden, 1)
            dve.wait_ge(l1_hidden, 2 * NI)
            dve.wait_ge(pool_consts, 6)
            nc.vector.tensor_reduce(amh[0:CI, :], h1[0:CI], AX.XY, ALU.max, apply_absolute_value=True) \
                .then_inc(hmax_ready, 1)
            dve.wait_ge(hmax_all, 1)
            link(nc.vector.tensor_scalar(sh, amhg, sg2[:, 1:2], 1.0 / QMAX, ALU.mult, ALU.mult))
            nc.vector.tensor_scalar(fac, sh, tg[:, 5:6], None, ALU.mult)
            link(nc.vector.reciprocal(ish, sh))
            link(nc.vector.tensor_scalar(h1[0:CI], h1[0:CI], ish[0:CI, :], QMAX, ALU.mult, ALU.min))
            link(nc.vector.tensor_scalar(h1[0:CI], h1[0:CI], -QMAX - 1.0, ROUND, ALU.max, ALU.add))
            nc.vector.tensor_scalar(h1q[0:CI], h1[0:CI], ROUND, None, ALU.subtract).then_inc(hq_ready, 1)
            for n in range(2):
                dve.wait_ge(l1_down, n + 1)
                y = xn[:, 4 * n:4 * n + 4, :]
                link(nc.vector.tensor_tensor(y, OB[n].rearrange("p (t d) -> p t d", t=4),
                                             wdrow[:].unsqueeze(1).to_broadcast([P, 4, D]), ALU.mult))
                for t in range(4 * n, 4 * n + 4):
                    nc.vector.scalar_tensor_tensor(x[:, t, :], xn[:, t, :], fac, x[:, t, :],
                                                   ALU.mult, ALU.add).then_inc(x_updated, 1)
            loaded(dve, "maski")
            nc.vector.tensor_scalar(mk2[:], maski[:], 0.0, None, ALU.not_equal)
            values8("v2", None)
            for n in range(2):
                bank = filled(dve, f"mean.{n}")
                nc.vector.tensor_scalar(mean[:, 2 * n:2 * n + 2, :, :],
                                        bank[:, 0:2 * 144].rearrange("p (b h e) -> p b h e", b=2, h=NH),
                                        1.0 / S, None, ALU.mult).then_inc(misc_emptied_v, 1)
            norm_rows(4, x, 4)
            split_queries("q2")
            attention(2)
            for n in range(2):
                bank = filled(dve, f"wo2.{n}")
                for k in range(4):
                    t = 4 * n + k
                    ins = nc.vector.scalar_tensor_tensor(x[:, t, :], bank[:, 128 * k:128 * k + 128], tg[:, 2:3],
                                                         x[:, t, :], ALU.mult, ALU.add)
                    if k < 3:
                        ins.then_inc(x_updated, 1)
                    else:
                        ins.then_inc(misc_emptied_v, 1)
                        dve.wait_ge(misc_emptied_v, EMPTIED[AT[f"wo2.{n}"]])
                        nc.vector.tensor_copy(veps[:, 0:1], x[:, t, 0:1]).then_inc(x_updated, 1)
            norm_rows(5, x, 5)
            loaded(dve, "br2")
            split_rows(2)
            for k in range(PIECES[2]):
                split_piece(0, k)
            router(1, "router2.0", br2)
            take_coefficients(2)
            experts2()
            add_experts(2, 6)
            dve.wait_ge(ld_ctx, 16)
            norm_rows(6, ctxr)
            loaded(dve, "lnp", "cos", "sin")
            for n in range(2):
                bank = filled(dve, f"lnc.{n}")
                nc.vector.tensor_scalar(cnT[:, 512 * n:512 * n + 512], bank, lnp[:, 0:1], lnp[:, 1:2],
                                        ALU.mult, ALU.add).then_inc(misc_emptied_v, 1)
            for k in range(8):
                c, n = k // 2, k % 2
                if k >= 2:
                    dve.wait_ge(rope_done, k - 1)
                bank = filled(dve, f"kc.{c}.{n}")
                nc.vector.tensor_tensor(rope[:, 0, k % 2, :].rearrange("p (b t) -> p b t", b=2),
                                        bank.rearrange("p (b t) -> p b t", b=2),
                                        cos[:].unsqueeze(1).to_broadcast([P, 2, S]), ALU.mult).then_inc(misc_emptied_v, 1)
                bank = filled(dve, f"kr.{c}.{n}")
                nc.vector.tensor_tensor(rope[:, 1, k % 2, :].rearrange("p (b t) -> p b t", b=2),
                                        bank.rearrange("p (b t) -> p b t", b=2),
                                        sin[:].unsqueeze(1).to_broadcast([P, 2, S]), ALU.mult).then_inc(misc_emptied_v, 1)
                dve.wait_ge(misc_emptied_v, EMPTIED[AT[f"kr.{c}.{n}"]])
                nc.vector.tensor_copy(veps[:, 0:1], rope[:, 1, k % 2, 0:1]).then_inc(rope_in, 1)
            dve.wait_ge(vones, 1)

            def values(kind):
                for t in range(1, NT, 2):
                    k = 4 * (t // 2) + 2 * (kind == "vl") + 1
                    bank = filled(dve, f"{kind}.{t}")
                    nc.vector.tensor_copy(VX[:, k, :, 0:DH3], bank.rearrange("p (h e) -> p h e", h=NH3)) \
                        .then_inc(misc_emptied_v, 1)

            values("vc")
            norm_rows(7, x, 6)
            dve.wait_ge(rows_normed, 8 * NT)
            norm_rows(8, xn)
            for n in range(2):
                bank = filled(dve, f"ln8.{n}")
                nc.vector.tensor_scalar(xnT[:, 512 * n:512 * n + 512], bank, lnp[:, 2:3], lnp[:, 3:4],
                                        ALU.mult, ALU.add).then_inc(misc_emptied_v, 1)
            values("vl")
            attention(3)
            norm_rows(9, x, 7)
            router(2, "router3.0", None)
            dve.wait_ge(cw_ready, 3)
            for t in range(NT + 2):
                if t < NT:
                    bank = filled(dve, f"uv.{t}")
                    dve.wait_ge(silu3, t + 1)
                    if t >= 2:
                        filled(dve, f"sT.{t - 2}")
                    nc.vector.tensor_tensor(PR[:, t % 2, 256:512], bank[:, 256:512], sg[:, t % 2, 0:256],
                                            ALU.mult).then_inc(misc_emptied_v, 1)
                    dve.wait_ge(misc_emptied_v, EMPTIED[AT[f"uv.{t}"]])
                    nc.vector.tensor_tensor(PR[:, t % 2, 0:256].rearrange("p (e r) -> p e r", e=E),
                                            PR[:, t % 2, 256:512].rearrange("p (e r) -> p e r", e=E),
                                            bc(cw[:, t, :], 32), ALU.mult).then_inc(s3_ready, 1)
                if t >= 2:
                    bank = filled(dve, f"y3.{t - 2}")
                    nc.vector.scalar_tensor_tensor(x[:, t - 2, :], bank[:, 0:D], tg[:, 7:8], x[:, t - 2, :],
                                                   ALU.mult, ALU.add).then_inc(misc_emptied_v, 1)
                    dve.wait_ge(misc_emptied_v, EMPTIED[AT[f"y3.{t - 2}"]])
                    nc.vector.tensor_copy(veps[:, 0:1], x[:, t - 2, 0:1]).then_inc(x_updated, 1)

        @block.tensor
        def _(pe):
            def room(name):
                i = AT[name]
                if i >= 2:
                    emptied(pe, MISC[i - 2][0])
                return MB[i % 2]

            def halves(name, w, xT):
                for n in range(2):
                    bank = room(f"{name}.{n}")
                    nc.tensor.matmul(bank, w, xT[:, 512 * n:512 * n + 512], start=True, stop=True) \
                        .then_inc(misc_ready, 1)

            def rows(name, xT, w):
                for n in range(2):
                    bank = room(f"{name}.{n}")
                    for k in range(4):
                        t = 4 * n + k
                        ins = nc.tensor.matmul(bank[:, 128 * k:128 * k + 128], xT[:, 128 * t:128 * t + 128], w,
                                               start=True, stop=True)
                    ins.then_inc(misc_ready, 1)

            def turn_rows(n, name):
                for hf in range(2):
                    bank = room(f"{name}.{hf}")
                    for k in range(4):
                        t = 4 * hf + k
                        pe.wait_ge(rows_normed, NT * n + t + 1)
                        ins = nc.tensor.transpose(bank[:, 128 * k:128 * k + 128], xn[:, t, :], ident[:])
                    ins.then_inc(misc_ready, 1)

            def turned(name):
                for n in range(2):
                    emptied(pe, f"{name}.{n}")

            def rel(r):
                t, h, g, w = UNITS8[r]
                bank = room(f"qer.{r}")
                for k in range(g):
                    ins = nc.tensor.matmul(bank[:, k * w:(k + 1) * w], QS[:, h + k, t * P:(t + 1) * P], ES[:, S - w:S],
                                           start=True, stop=True)
                ins.then_inc(misc_ready, 1)

            def scores(layer, i):
                t, h, g, w = UNITS[layer][i]
                b, u = t // 2, BASE[layer] + i
                bank = SC[u % 2]
                if u >= 2:
                    pe.wait_ge(min_ready if layer == 0 else probs_ready, u - 1)
                if layer in (0, 2):
                    for k in range(g):
                        if layer == 2:
                            nc.tensor.matmul(bank[:, k * w:(k + 1) * w], identb[:],
                                             maskb[:, t % 2, k * w:(k + 1) * w], start=True, stop=False)
                        ins = nc.tensor.matmul(bank[:, k * w:(k + 1) * w], QS[:, h + k, t * P:(t + 1) * P],
                                               KS[:, h + k, b * S:b * S + w], start=(layer == 0),
                                               stop=True)
                elif layer == 1:
                    for k in range(2):
                        nc.tensor.matmul(bank[:, k * S:(k + 1) * S], ones[0:1, :], mrow[0:1, b * S:(b + 1) * S],
                                         start=True, stop=False)
                        ins = nc.tensor.matmul(bank[:, k * S:(k + 1) * S], qf[:, (t + k) * P:(t + k + 1) * P],
                                               kf[:, b * S:(b + 1) * S], start=False, stop=True)
                else:
                    r = DH3 * (h % 2)
                    ins = nc.tensor.matmul(bank, QT3[r:r + DH3, h // 2, t * P:(t + 1) * P], KT3[r:r + DH3, h // 2, b, :],
                                           start=True, stop=True)
                ins.then_inc(scores_ready, 1)

            def turn_probs(layer, i):
                u = BASE[layer] + i
                pe.wait_ge(probs_ready, u + 1)
                if u >= 2:
                    copied(pe, u - 2)
                for k in range(4):
                    ins = nc.tensor.transpose(TP[u % 2][:, P * k:P * k + P], PR[:, u % 2, P * k:P * k + P], ident[:])
                ins.then_inc(probsT_ready, 1)

            def weigh(layer, i):
                t, h, g, w = UNITS[layer][i]
                u = BASE[layer] + i
                k0 = sum(j < i for j in LAST[layer])
                grp = GROUPS[layer] + k0
                if i == 0 or i - 1 in LAST[layer]:
                    behind = grp if layer == 3 else grp - 1
                    if behind > 0:
                        pe.wait_ge(out_read, behind)
                copied(pe, u)
                for k in range(4):
                    pt = PT[:, u % 2, P * k:P * k + P]
                    if layer in (0, 2):
                        hh, jt, last = (h + k, 0, 0) if g == 4 else (h + k // 2, k % 2, 1)
                        a = (DH + 1) * (NH * (t - t % 2 + jt) + hh)
                        ins = nc.tensor.matmul(OB[grp % 2][:, 9 * hh:9 * hh + WIDE], pt, v9[:, a:a + WIDE],
                                               start=(jt == 0), stop=(jt == last))
                    elif layer == 1:
                        it, jt = k // 2, k % 2
                        ins = nc.tensor.matmul(OB[grp % 2][:, 129 * it:129 * it + 129], pt, VA[:, t + jt, :],
                                               start=(jt == 0), stop=(jt == 1))
                    else:
                        ins = nc.tensor.matmul(OB[h // 4][:, 65 * (h % 4):65 * (h % 4) + 65], pt,
                                               VX[:, 4 * (t // 2) + k, h, :], start=(k == 0), stop=(k == 3))
                ins.then_inc(pv_done, 1)

            def attention(layer):
                n = len(UNITS[layer])
                for i in range(n + WEIGH + 2):
                    if layer == 0 and i + LEAD < N8:
                        rel(i + LEAD)
                    if i < n:
                        scores(layer, i)
                    if 0 <= i - TURN < n:
                        turn_probs(layer, i - TURN)
                    if 0 <= i - WEIGH < n:
                        weigh(layer, i - WEIGH)
                    if layer == 3 and i - WEIGH - 1 in LAST[3]:
                        t = LAST[3].index(i - WEIGH - 1)
                        bank = room(f"oT3.{t}")
                        pe.wait_ge(out_read, GROUPS[3] + t + 1)
                        for k in range(4):
                            ins = nc.tensor.transpose(bank[:, P * k:P * k + P], stage3[:, P * k:P * k + P], ident[:])
                        ins.then_inc(misc_ready, 1)
                    if layer == 3 and i - WEIGH - 2 in LAST[3]:
                        t = LAST[3].index(i - WEIGH - 2)
                        bank = room(f"wo3.{t}")
                        emptied(pe, f"oT3.{t}")
                        for k in range(4):
                            ins = nc.tensor.matmul(bank[:, 0:D], sg[:, 0, P * k:P * k + P], wo3[:, k, :],
                                                   start=(k == 0), stop=(k == 3))
                        ins.then_inc(misc_ready, 1)

            def logits(name, w):
                bank = room(name)
                for t in range(NT):
                    ins = nc.tensor.matmul(bank[:, E * t:E * t + E], xnT[:, P * t:P * t + P], w[:], start=True, stop=True)
                ins.then_inc(misc_ready, 1)

            def turn_coefficients(layer, n_cw):
                pe.wait_ge(cw_ready, n_cw)
                for n in range(2):
                    bank = room(f"cwT{layer}.{n}")
                    for k in range(4):
                        ins = nc.tensor.transpose(bank[0:E, P * k:P * k + P], cw[:, 4 * n + k, :], ident[:])
                    ins.then_inc(misc_ready, 1)

            def three(out, w, at, xs_hi, xs_lo, start, stop):
                nc.tensor.matmul(out, wh[:, w, at:at + P], xs_hi, start=start, stop=False)
                nc.tensor.matmul(out, wh[:, w, at:at + P], xs_lo, start=False, stop=False)
                return nc.tensor.matmul(out, wl[:, w, at:at + P], xs_hi, start=False, stop=stop)

            def experts(layer, nch, b):
                m, per = moe[layer], 2 * nch
                nj, down_at = E * per, {0: 1024, 2: 256}[layer]
                pe.wait_ge(m["x_lo"], 1)
                for j in range(nj + 3):
                    if j < nj:
                        e, c, n = j // per, j // 2 % nch, j % 2
                        if j % per == 0:
                            pe.wait_ge(m["w_lo"], PIECES[layer] * e + {0: 4, 2: 1}[layer])
                        x_hi, x_lo = xh[:, 512 * n:512 * n + 512], xl[:, 512 * n:512 * n + 512]
                        if j >= 2:
                            pe.wait_ge(m["act"], j - 1)
                        three(SC[j % 2], e % 2, P * c, x_hi, x_lo, True, True).then_inc(m["gate"], 1)
                        if layer == 0:
                            if j >= 2:
                                pe.wait_ge(m["mixed"], j - 1)
                            three(TP[j % 2], e % 2, 512 + P * c, x_hi, x_lo, True, True).then_inc(m["up"], 1)
                    if j == 1:
                        turn_coefficients(layer, 1 + layer // 2)
                        emptied(pe, f"cwT{layer}.1")
                        for n in range(2):
                            nc.tensor.matmul(OB[n], b[:], cwT[:, 512 * n:512 * n + 512], start=True, stop=False)
                    if j >= 3:
                        i = j - 3
                        e, c, n = i // per, i // 2 % nch, i % 2
                        if i % per == 0:
                            pe.wait_ge(m["w_lo"], PIECES[layer] * (e + 1))
                        pe.wait_ge(m["lo"], i + 1)
                        three(OB[n], e % 2, down_at + P * c, hh[:, i % 2, :], hl[:, i % 2, :],
                              False, i >= nj - 2).then_inc(m["down"], 1)
                for n in range(2):
                    pe.wait_ge(m["summed"], n + 1)
                    bank = room(f"yT{layer}.{n}")
                    for k in range(4):
                        t = 4 * n + k
                        ins = nc.tensor.transpose(bank[:, P * k:P * k + P], xnT[:, P * t:P * t + P], ident[:])
                    ins.then_inc(misc_ready, 1)

            loaded(pe, "wk0")
            pe.wait_ge(ld_ctxT, 16)
            halves("k0", wk0[:], ctxT)
            loaded(pe, "wv0")
            rows("v0", ctxT, wv0[:])
            loaded(pe, "ident")
            turn_rows(0, "ln0")
            turned("ln0")
            loaded(pe, "wq0")
            halves("q0", wq0[:], xnT)
            pe.wait_ge(es_loaded, 16 * 9)
            pe.wait_ge(qs_loaded, 16 * 9)
            for r in range(LEAD):
                rel(r)
            pe.wait_ge(ks_loaded, 16 * 9)
            pe.wait_ge(pool_consts, 6)
            attention(0)
            turn_rows(1, "ln1")
            turned("ln1")
            loaded(pe, "wr0", "hb3")
            logits("router0.0", wr0)
            experts(0, 4, hb3)
            loaded(pe, "wk1", "wv1", "wq1")
            halves("k1", wk1[:], ctxT)
            rows("v1", ctxT, wv1[:])
            turn_rows(2, "ln2")
            turned("ln2")
            halves("q1", wq1[:], xnT)
            for n in range(2):
                emptied(pe, f"q1.{n}")
            pe.wait_ge(mask_ready, 2)
            attention(1)
            for name, w, k in (("wgT.0", wg, 1), ("wuT.0", wu, 2)):
                bank = room(name)
                pe.wait_ge(weights_scaled, k)
                for c in range(NI):
                    ins = nc.tensor.transpose(bank[:, CI * c:CI * c + CI], w[:, c, :], ident[0:CI, 0:CI])
                ins.then_inc(misc_ready, 1)
            bank = room("wdT.0")
            pe.wait_ge(weights_scaled, 3)
            for c in range(NI):
                ins = nc.tensor.transpose(bank[0:CI, P * c:P * c + P], wd[:, CI * c:CI * c + CI], ident[:])
            ins.then_inc(misc_ready, 1)
            bank = room("wdrow.0")
            pe.wait_ge(weights_scaled, 4)
            nc.tensor.matmul(bank[:, 0:D], ones[:], diag[:], start=True, stop=True).then_inc(misc_ready, 1)
            turn_rows(3, "ln3")
            emptied(pe, "wdrow.0")
            pe.wait_ge(xq_ready, 1)
            for j in range(2 * NI):
                c, n = j // 2, j % 2
                if j >= 2:
                    pe.wait_ge(l1_silu, j - 1)
                nc.tensor.matmul(SC[j % 2][0:CI, :], wgT[:, CI * c:CI * c + CI], xq[:, 512 * n:512 * n + 512],
                                 start=True, stop=True).then_inc(l1_gate, 1)
                if j >= 2:
                    pe.wait_ge(l1_hidden, j - 1)
                nc.tensor.matmul(TP[j % 2][0:CI, :], wuT[:, CI * c:CI * c + CI], xq[:, 512 * n:512 * n + 512],
                                 start=True, stop=True).then_inc(l1_up, 1)
            pe.wait_ge(hq_ready, 1)
            for n in range(2):
                for k in range(4):
                    t = 4 * n + k
                    for c in range(NI):
                        ins = nc.tensor.matmul(OB[n][:, P * k:P * k + P], h1q[0:CI, c, P * t:P * t + P], wdT[:, c, :],
                                               start=(c == 0), stop=(c == NI - 1))
                ins.then_inc(l1_down, 1)
            loaded(pe, "wk2", "wv2", "wq2", "wo2")
            halves("k2", wk2[:], ctxT)
            rows("v2", ctxT, wv2[:])
            for n in range(2):
                emptied(pe, f"v2.{n}")
            for n in range(2):
                bank = room(f"mean.{n}")
                for k in range(2):
                    for jt in range(2):
                        t = 2 * (2 * n + k) + jt
                        ins = nc.tensor.matmul(bank[:, 144 * k:144 * k + 144], ones[:],
                                               V9[:, t].rearrange("p h e -> p (h e)"), start=(jt == 0), stop=(jt == 1))
                ins.then_inc(misc_ready, 1)
            turn_rows(4, "ln4")
            turned("ln4")
            halves("q2", wq2[:], xnT)
            pe.wait_ge(ks_loaded, 16 * 18)
            pe.wait_ge(qs_loaded, 16 * 18)
            attention(2)
            for n in range(2):
                bank = room(f"oT2.{n}")
                for k in range(4):
                    pe.wait_ge(heads_ready, 4 * n + k + 1)
                    ins = nc.tensor.transpose(bank[:, P * k:P * k + P], xn[:, 4 * n + k, :], ident[:])
                ins.then_inc(misc_ready, 1)
            turned("oT2")
            rows("wo2", xnT, wo2[:])
            turn_rows(5, "ln5")
            turned("ln5")
            loaded(pe, "wr2", "gb2")
            logits("router2.0", wr2)
            experts(2, 2, gb2)
            turn_rows(6, "lnc")
            for n in range(2):
                emptied(pe, f"lnc.{n}")
            loaded(pe, "wkv3", "wkr3", "wq3", "wo3")
            for c in range(4):
                for n in range(2):
                    bank = room(f"kc.{c}.{n}")
                    nc.tensor.matmul(bank, wkv3[:, P * c:P * c + P], cnT[:, 512 * n:512 * n + 512], start=True, stop=True) \
                        .then_inc(misc_ready, 1)
                    bank = room(f"kr.{c}.{n}")
                    nc.tensor.matmul(bank, wkr3[:, P * c:P * c + P], cnT[:, 512 * n:512 * n + 512], start=True, stop=True) \
                        .then_inc(misc_ready, 1)
            for t in range(NT):
                bank = room(f"vc.{t}")
                nc.tensor.matmul(bank, cnT[:, P * t:P * t + P], wkv3[:, 512:1024], start=True, stop=True) \
                    .then_inc(misc_ready, 1)
            turn_rows(8, "ln8")
            for n in range(2):
                emptied(pe, f"ln8.{n}")
            for c in range(4):
                for n in range(2):
                    bank = room(f"kl.{c}.{n}")
                    nc.tensor.matmul(bank, wkv3[:, P * c:P * c + P], xnT[:, 512 * n:512 * n + 512], start=True, stop=True) \
                        .then_inc(misc_ready, 1)
                    bank = room(f"q3.{c}.{n}")
                    nc.tensor.matmul(bank, wq3[:, P * c:P * c + P], xnT[:, 512 * n:512 * n + 512], start=True, stop=True) \
                        .then_inc(misc_ready, 1)
            for t in range(NT):
                bank = room(f"vl.{t}")
                nc.tensor.matmul(bank, xnT[:, P * t:P * t + P], wkv3[:, 512:1024], start=True, stop=True) \
                    .then_inc(misc_ready, 1)
            pe.wait_ge(rope_done, 8)
            for n in ("q3.3.1", "vl.6", "vl.7"):
                emptied(pe, n)
            attention(3)
            turn_rows(9, "ln9")
            turned("ln9")
            loaded(pe, "wr3", "wuv", "wf3")
            logits("router3.0", wr3)
            for t in range(NT + 2):
                if t < NT:
                    bank = room(f"uv.{t}")
                    nc.tensor.matmul(bank, xnT[:, P * t:P * t + P], wuv[:], start=True, stop=True).then_inc(misc_ready, 1)
                if 1 <= t <= NT:
                    bank = room(f"sT.{t - 1}")
                    pe.wait_ge(s3_ready, t)
                    for k in range(2):
                        ins = nc.tensor.transpose(bank[:, P * k:P * k + P], PR[:, (t - 1) % 2, P * k:P * k + P], ident[:])
                    ins.then_inc(misc_ready, 1)
                if t >= 2:
                    bank = room(f"y3.{t - 2}")
                    emptied(pe, f"sT.{t - 2}")
                    for k in range(2):
                        ins = nc.tensor.matmul(bank[:, 0:D], PT[:, (t - 2) % 2, P * k:P * k + P], wf3[:, k, :],
                                               start=(k == 0), stop=(k == 1))
                    ins.then_inc(misc_ready, 1)


def _constants():
    half = DH3 // 2
    inv = (1.0 / np.float32(10000.0) ** (np.arange(0, DH3, 2, dtype=np.float32) / np.float32(DH3))).astype(np.float32)
    ang = (np.arange(S, dtype=np.float32)[None, :] * inv[:, None]).astype(np.float32)
    c, s = np.cos(ang).astype(np.float32), np.sin(ang).astype(np.float32)
    cos = np.concatenate([c] * 4, 0)
    sin = np.concatenate([-s, s, -s, s], 0)
    i, j = np.arange(P)[:, None], np.arange(P)[None, :]
    return {
        "ident": np.eye(P, dtype=np.float32),
        "maskf": np.where(j <= i, 0.0, BIG).astype(np.float32),
        "iota": np.tile(np.arange(E, dtype=np.float32), (P, 1)),
        "cos": np.ascontiguousarray(cos), "sin": np.ascontiguousarray(sin),
    }


def _lay_out(a):
    g = {k: np.asarray(v) for k, v in a.items()}
    ctx = g["ctx_1024"].reshape(TOK, D)
    wkv = g["L3_xattn_Wkv"]
    half = DH3 // 2
    swap = np.concatenate([np.concatenate([np.arange(half, DH3), np.arange(half)]) + DH3 * h for h in range(NH3)])
    lay = {
        "x": g["x"].reshape(TOK, D), "ctx": ctx, "ctxT": ctx.T,
        "erT": g["L0_xattn_Er"].T, "mrow": g["mask_BxS2_ff1"].reshape(1, TOK),
        "gates": np.concatenate([g["g_xattn"], g["g_ffn"]]),
        "clips": np.concatenate([g["L1_ffn_clip_x"], g["L1_ffn_clip_down"]]),
        "wq0": g["L0_xattn_Wq"].T, "wk0": g["L0_xattn_Wk"].T, "wv0": g["L0_xattn_Wv"].T,
        "b0": np.stack([g["L0_xattn_bq"], g["L0_xattn_bk"]], 1), "bv0": g["L0_xattn_bv"],
        "wq1": g["L1_xattn_Wq"], "wk1": g["L1_xattn_Wk"], "wv1": g["L1_xattn_Wv"],
        "b1": np.stack([g["L1_xattn_bq"], g["L1_xattn_bk"]], 1), "bv1": g["L1_xattn_bv"],
        "wq2": g["L2_xattn_WQ"], "wk2": g["L2_xattn_WK"], "wv2": g["L2_xattn_WV"], "wo2": g["L2_xattn_WO"],
        "maski": g["mask_BxS2_ik0"].reshape(NT, P).T,
        "wr0": g["L0_ffn_Wr"], "br0": g["L0_ffn_br"],
        "hb1": g["L0_ffn_b1"].reshape(E, 4, P).transpose(2, 0, 1),
        "hb2": g["L0_ffn_b2"].reshape(E, 4, P).transpose(2, 0, 1), "hb3": g["L0_ffn_b3"],
        "f1": g["L0_ffn_W1"], "f2": g["L0_ffn_W2"], "f3": g["L0_ffn_W3"],
        "wr2": g["L2_ffn_Wg"], "br2": g["L2_ffn_bg"],
        "gb1": g["L2_ffn_b1"].reshape(E, 2, P).transpose(2, 0, 1), "gb2": g["L2_ffn_b2"],
        "g1": g["L2_ffn_W1"], "g2": g["L2_ffn_W2"],
        "wg": g["L1_ffn_w_gate"].reshape(NI, CI, D).transpose(1, 0, 2),
        "wu": g["L1_ffn_w_up"].reshape(NI, CI, D).transpose(1, 0, 2), "wd": g["L1_ffn_w_down"],
        "lnp": np.stack([g["L3_xattn_gamma_x"], g["L3_xattn_beta_x"], g["L3_xattn_gamma_l"], g["L3_xattn_beta_l"]], 1),
        "wq3": g["L3_xattn_Wq"], "wkv3": wkv, "wkr3": wkv[:, 0:512][:, swap],
        "wo3": g["L3_xattn_Wo"].reshape(4, P, D).transpose(1, 0, 2).reshape(P, 512),
        "wr3": g["L3_ffn_gate_w"],
        "wuv": np.concatenate([g["L3_ffn_Wu"].transpose(1, 0, 2).reshape(D, 256),
                               g["L3_ffn_Wv"].transpose(1, 0, 2).reshape(D, 256)], 1),
        "wf3": g["L3_ffn_Wo"].reshape(2, P, D).transpose(1, 0, 2).reshape(P, 256),
    }
    return {k: np.ascontiguousarray(v) for k, v in lay.items()}


def kernel(**inputs):
    import concourse.bacc as bacc
    from concourse.bass_utils import run_bass_kernel_spmd

    arrays = {**_lay_out(inputs), **_constants()}
    nc = bacc.Bacc("TRN2", target_bir_lowering=False, num_devices=1)
    aps = {k: nc.dram_tensor("in_" + k + "_dram", v.shape, mybir.dt.from_np(v.dtype), kind="ExternalInput").ap()
           for k, v in arrays.items()}
    out = nc.dram_tensor("out_dram", (TOK, D), F32, kind="ExternalOutput").ap()
    build(nc, aps, out)
    r = run_bass_kernel_spmd(nc, [{"in_" + k + "_dram": v for k, v in arrays.items()}], core_ids=[0])
    return np.asarray(r.results[0]["out_dram"]).reshape(NB, S, D)
```

```python
from contextlib import ExitStack

import concourse.bass as bass
import numpy as np
from concourse import mybir

F32 = mybir.dt.float32
BF16 = mybir.dt.bfloat16
F32R = mybir.dt.float32r
U32 = mybir.dt.uint32
I32 = mybir.dt.int32
ALU = mybir.AluOpType
ACT = mybir.ActivationFunctionType
AX = mybir.AxisListType
RMAX = bass.bass_isa.ReduceOp.max

P = 128
NB, S, D = 4, 256, 128
NT = NB * S // P
TOK = NB * S
NH, DH = 16, 8
NPART = 3
STACK = NPART * NPART * DH
E = 8
NH3, DH3 = 8, 64
CI, NI = 88, 4
EPS = 1e-5
PIECE = 256
PIECES = {0: 6, 2: 2}
PIECE_AT = {0: [0, 1, 2, 3, 4, 5], 2: [0, 3]}
JOBS = {0: 8, 2: 4}
TURN, WEIGH = 2, 3
WIDE = 96
NB8 = 16 * NH3 * (DH3 + 1) + WIDE - (DH3 + 1)
BIG = 1e30
ROUND = 1.5 * 2.0 ** 23
QMAX = 127.0
LEAD = 7
STAGE, SKEW = 4, 8
SLICE8 = float(DH) ** -0.5

UNITS8 = [(t, h, (4, 2)[t % 2], (128, 256)[t % 2]) for t in range(NT) for h in range(0, NH, (4, 2)[t % 2])]
UNITS1 = [(2 * b, 0, 2, 256) for b in range(NB)]
UNITS3 = [(t, h, 1, 512) for t in range(NT) for h in range(NH3)]
N8, N1, N3 = len(UNITS8), len(UNITS1), len(UNITS3)
BASE = {0: 0, 1: N8, 2: N8 + N1, 3: 2 * N8 + N1}
UNITS = {0: UNITS8, 1: UNITS1, 2: UNITS8, 3: UNITS3}
LAST = {k: [i for i, u in enumerate(v) if i + 1 == len(v) or v[i + 1][0] != u[0]] for k, v in UNITS.items()}
GROUPS = {0: 0, 1: 8, 2: 12, 3: 20}
COPIER = ["V"] * (2 * N8 + N1) + ["AV"[i % 2] for i in range(N3)]


STEPS3 = [(1, "oT3", "A"), (2, "wo3", "V"), (4, "ln9", "A"), (5, "router3", "V"), (5, "uv", "V"), (11, "sT", "A"),
          (12, "y3", "V")]


def _tile3(i, behind):
    return LAST[3].index(i - WEIGH - behind) if i - WEIGH - behind in LAST[3] else None


def _plan_misc():
    m = []

    def add(name, n, who):
        m.extend((f"{name}.{i}", who) for i in range(n))

    add("k0", 2, "A"); add("ln0", 2, "A"); add("q0", 2, "A"); add("v0", 2, "V")
    add("k2", 2, "A"); add("qer", STAGE, "A")
    add("wgT", 1, "V"); add("wuT", 1, "V"); add("wdT", 1, "V"); add("wdrow", 1, "V")
    add("k1", 2, "A"); add("v1", 2, "V")
    m.extend((f"qer.{r}", "A") for r in range(STAGE, N8))
    add("ln1", 2, "A"); add("router0", 1, "V"); add("cwB0", 2, "A"); add("cwT0", 2, "V"); add("yT0", 2, "V")
    add("v2", 2, "A"); add("ln2", 2, "A"); add("q1", 2, "A"); add("mean", 2, "A"); add("ln3", 2, "A")
    add("ln4", 2, "A"); add("q2", 2, "A"); add("lnc", 2, "V")
    add("oT2", 2, "A"); add("wo2", 2, "V")
    add("ln5", 2, "A"); add("router2", 1, "V"); add("cwB2", 2, "A"); add("cwT2", 2, "V"); add("yT2", 2, "V")
    m.extend((f"kc.{c}.{n}", "A") for c in range(4) for n in range(2))
    add("vc", NT, "A")
    add("ln8", 2, "V")
    for c in range(4):
        for n in range(2):
            m.append((f"kl.{c}.{n}", "A")); m.append((f"q3.{c}.{n}", "A"))
    for t in range(NT):
        m.append((f"vl.{t}", "AV"[t % 2]))
    for i in range(N3 + WEIGH + 13):
        m.extend((f"{name}.{_tile3(i, behind)}", who) for behind, name, who in STEPS3 if _tile3(i, behind) is not None)
    return m


MISC = _plan_misc()
AT = {name: i for i, (name, _) in enumerate(MISC)}
EMPTIED = [sum(w == who for _, w in MISC[:i + 1]) for i, (_, who) in enumerate(MISC)]


def build(nc, I, out):
    with ExitStack() as ctx:
        def sb(name, shape, dt=F32):
            return ctx.enter_context(nc.sbuf_tensor(name, shape, dt))

        def sem(name):
            return ctx.enter_context(nc.semaphore(name))

        def dram(name, shape, dt):
            return nc.dram_tensor(name, shape, dt, kind="Internal").ap()

        x = sb("x", [P, NT, D])
        ctxr = sb("ctxr", [P, NT, D])
        ctxT = sb("ctxT", [P, TOK])
        xn = sb("xn", [P, NT, D])
        xnT = sb("xnT", [P, TOK])
        cnT = sb("cnT", [P, TOK])
        arenaA = sb("arenaA", [P, 16384])
        QS = arenaA[0:STACK, 0:8192].bitcast(BF16).rearrange("p (f h t) -> p f h t", f=2, h=NH)
        KS = arenaA[0:STACK, 8192:16384].bitcast(BF16).rearrange("p (f h t) -> p f h t", f=2, h=NH)
        KT3 = arenaA[:, 0:8192].rearrange("p (c b k) -> p c b k", c=4, b=NB)
        QT3 = arenaA[:, 8192:8192 + 4096].rearrange("p (c t) -> p c t", c=4)
        arenaB = sb("arenaB", [P, NB8])
        stage = arenaB[:, 0:STAGE * 512].rearrange("p (n w) -> p n w", n=STAGE)
        skewed = arenaB[:, STAGE * 512:(STAGE + SKEW) * 512].rearrange("p (n w) -> p n w", n=SKEW)
        cwB = arenaA[:, 0:8192].rearrange("p (e t) -> p e t", e=E)
        at_b = nc.sbuf_base - NB8 * 4

        def place(name, at, shape):
            return nc.alloc_sbuf_tensor_at(name, shape, F32R, offset=at)

        wh = place("wh", at_b, [P, 2, 1536])
        wl = place("wl", at_b + 4 * 3072, [P, 2, 1536])
        hh = place("hh", at_b + 4 * 6144, [P, 2, 512])
        hl = place("hl", at_b + 4 * 7168, [P, 2, 512])
        k2f = ctxr[:].rearrange("p t d -> p (t d)")
        k2parts = arenaB[:, 6144:7680].bitcast(BF16).rearrange("p (a t) -> p a t", a=NPART)
        k1f = cnT
        hh_more, hl_more = place("hh_more", at_b + 4 * 512, [P, 2, 512]), place("hl_more", at_b + 4 * 2048, [P, 2, 512])
        h1 = arenaB[:, 0:4096].rearrange("p (c t) -> p c t", c=NI)
        h1q = arenaB[:, 4096:6144].bitcast(BF16).rearrange("p (c t) -> p c t", c=NI)
        VX = arenaB[:, 0:8320].rearrange("p (k h e) -> p k h e", k=16, h=NH3)
        ring = sb("ring", [P, 2, 1536])
        at_r = nc.sbuf_base - 3072 * 4
        kh3, kl3 = place("kh3", at_r, [P, 2, 512]), place("kl3", at_r + 4 * 1024, [P, 2, 512])
        qh3, ql3 = place("qh3", at_r + 4 * 2048, [P, 2, P]), place("ql3", at_r + 4 * 2304, [P, 2, P])
        qparts = ring[:, 0, :].bitcast(BF16).rearrange("p (a t) -> p a t", a=NPART)
        kparts = ring[:, 1, :].bitcast(BF16).rearrange("p (a t) -> p a t", a=NPART)
        qkf = sb("qkf", [P, 2, TOK])
        at_q = nc.sbuf_base - 2 * TOK * 4
        xh, xl = place("xh", at_q, [P, TOK]), place("xl", at_q + 4 * TOK, [P, TOK])
        qf, kf = qkf[:, 0, :], qkf[:, 1, :]
        closed = kf

        def k_swapped(c):
            flat = ring[:].rearrange("p s w -> p (s w)")[:, TOK * c:TOK * c + TOK] if c < 3 else qkf[:, 0, :]
            return flat.rearrange("p (b t) -> p b t", b=NB)

        v9 = sb("v9", [P, NT * NH * (DH + 1) + WIDE])
        V9 = v9[:, 0:NT * NH * (DH + 1)].rearrange("p (t h e) -> p t h e", t=NT, h=NH)
        VA = sb("VA", [P, NT, D + 1])
        Sx = sb("Sx", [P, 2, 512])
        PR = sb("PR", [P, 2, 512])
        PT = sb("PT", [P, 2, 512])
        sg = sb("sg", [P, 2, 512])
        stage3 = sb("stage3", [P, 512])
        xq = sb("xq", [P, TOK], BF16)
        ones = sb("ones", [P, P])
        erp = sb("erp", [DH, NPART, S], BF16)
        erf = sb("erf", [DH, S])
        ES = sb("ES", [STACK, S], BF16)
        mk2 = sb("mk2", [P, NT])
        mean = sb("mean", [P, NB, NH, DH + 1])
        cwT = sb("cwT", [E, TOK])
        tg = sb("tg", [P, 8])
        small = sb("small", [P, 64])
        nbq0, nbq1 = small[:, 0:1], small[:, 1:2]
        amx, sx, isx, gx = small[:, 2:3], small[:, 3:4], small[:, 4:5], small[:, 5:6]
        amh, sh, ish, fac = small[:, 6:7], small[:, 7:8], small[:, 8:9], small[:, 9:10]
        amxg, amhg = small[:, 10:11], small[:, 11:12]
        sg2 = small[:, 12:14]
        wgs, wus, wds = small[0:CI, 16:20], small[0:CI, 20:24], small[:, 24:25]
        iwg, iwu, iwd = small[0:CI, 28:32], small[0:CI, 32:36], small[:, 36:37]
        fg, fu = small[0:CI, 40:44], small[0:CI, 44:48]
        minus_round = small[:, 61:62]
        mhalf = sb("mhalf", [P, NT])
        st = sb("st", [P, NT, 6])
        mv = sb("mv", [P, NT, 2])
        veps = sb("veps", [P, NT])
        rstd = sb("rstd", [P, NT])
        smin = sb("smin", [P, 2, 4])
        rsum = sb("rsum", [P, NH])
        lg = sb("lg", [P, NT, E])
        lmx = sb("lmx", [P, NT, 8])
        lix = sb("lix", [P, NT, 8], U32)
        lixf = sb("lixf", [P, NT, 8])
        rw = sb("rw", [P, 4, NT])
        oh = sb("oh", [P, 2, NT, E])
        cw = sb("cw", [P, NT, E])
        wgT = sb("wgT", [P, NI * CI], BF16)
        wuT = sb("wuT", [P, NI * CI], BF16)
        wdT = sb("wdT", [CI, NI, D], BF16)
        wdrow = sb("wdrow", [P, D])
        diag = sb("diag", [P, P])
        loads, group_size, group_sem = {}, {}, {}

        def arrives(name, tile, group):
            group = group or name
            if group not in group_sem:
                group_sem[group] = sem("ld_" + group)
            group_size[group] = group_size.get(group, 0) + 1
            loads[name] = (tile, group_sem[group], group)
            return tile

        def load(name, shape, dt=F32, group=None):
            return arrives(name, sb("in_" + name, shape, dt), group)

        ident = load("ident", [P, P]); maskf = load("maskf", [P, S]); iota = load("iota", [P, E])
        cos = load("cos", [P, S], group="rope"); sin = load("sin", [P, S], group="rope")
        gates = load("gates", [P, 8], group="gates"); clips = load("clips", [P, 2], group="gates")
        wq0 = load("wq0", [D, D]); wk0 = load("wk0", [D, D]); wv0 = load("wv0", [D, D])
        b0 = load("b0", [D, 2]); bv0 = load("bv0", [P, D])
        wq1 = load("wq1", [D, D]); wk1 = load("wk1", [D, D], group="attention1")
        wv1 = load("wv1", [D, D], group="attention1")
        b1 = load("b1", [D, 2], group="attention1"); bv1 = load("bv1", [P, D], group="attention1")
        wq2 = load("wq2", [D, D], group="attention2"); wk2 = load("wk2", [D, D])
        wv2 = load("wv2", [D, D], group="attention2"); wo2 = load("wo2", [D, D], group="attention2")
        maski = load("maski", [P, NT], I32, group="attention2")
        wr0 = load("wr0", [D, E], group="experts0"); br0 = load("br0", [P, E], group="experts0")
        hb1 = load("hb1", [P, E, 4], group="experts0"); hb2 = load("hb2", [P, E, 4], group="experts0")
        hb3 = load("hb3", [E, D], group="experts0")
        wr2 = load("wr2", [D, E], group="experts2"); br2 = load("br2", [P, E], group="experts2")
        gb1 = load("gb1", [P, E, 2], group="experts2"); gb2 = load("gb2", [E, D], group="experts2")
        wg = load("wg", [CI, NI, D], group="ffn1"); wu = load("wu", [CI, NI, D], group="ffn1")
        wd = load("wd", [D, NI * CI], group="ffn1")
        lnp = load("lnp", [D, 4], group="layer3small")
        wr3 = load("wr3", [D, E], group="layer3small")

        def load_late(name, at, n):
            return arrives(name, arenaA[:, 12288 + at:12288 + at + n], "layer3")

        wq3, wkv3 = load_late("wq3", 0, 512), load_late("wkv3", 512, 1024)
        wo3 = load_late("wo3", 2048, 512).rearrange("p (c d) -> p c d", c=4)
        wuv = load_late("wuv", 2560, 512)
        wf3 = load_late("wf3", 3072, 256).rearrange("p (c d) -> p c d", c=2)

        ps = ctx.enter_context(nc.psum_tensor("ps", [P, 8, 512], F32))
        SC = [ps[:, 0, :], ps[:, 1, :]]
        TP = [ps[:, 2, :], ps[:, 3, :]]
        OB = [ps[:, 4, :], ps[:, 5, :]]
        MB = [ps[:, 6, :], ps[:, 7, :]]

        relpos = dram("relpos", (N8, P, 512), F32)
        qpd = dram("qpd", (2, 2, NPART, DH, NH, 512), BF16)
        kpd = dram("kpd", (2, 2, NPART, DH, NH, 512), BF16)
        cwd = dram("cwd", (2, E, TOK), F32)

        ld_x, ld_ctx, ld_ctxT, ld_er, ld_mrow = (sem("ld_" + n) for n in ("x", "ctx", "ctxT", "er", "mrow"))
        stats_ready, moments_ready, variance_ready = sem("stats_ready"), sem("moments_ready"), sem("variance_ready")
        rstd_ready, rows_normed, x_updated = sem("rstd_ready"), sem("rows_normed"), sem("x_updated")
        misc_ready, misc_emptied_v, misc_emptied_a = sem("misc_ready"), sem("misc_emptied_v"), sem("misc_emptied_a")
        v_step, g_step = sem("v_step"), sem("g_step")
        nbq_ready, gates_ready = sem("nbq_ready"), sem("gates_ready")
        sig_exp, pool_consts = sem("sig_exp"), sem("pool_consts")
        kparts_ready, qparts_ready, erparts_ready = sem("kparts_ready"), sem("qparts_ready"), sem("erparts_ready")
        keys_rounded, keys_left, es_loaded = sem("keys_rounded"), sem("keys_left"), sem("es_loaded")
        kp_stored, qp_stored, ks_loaded, qs_loaded = ([sem(f"{n}{f}") for f in range(2)] for n in
                                                      ("kp_stored", "qp_stored", "ks_loaded", "qs_loaded"))
        rel_stored = [sem(f"rel_stored{i}") for i in range(STAGE)]
        rel_loaded = [sem(f"rel_loaded{i}") for i in range(SKEW)]
        rel_masked = sem("rel_masked")
        scores_ready, min_ready, probs_ready = sem("scores_ready"), sem("min_ready"), sem("probs_ready")
        probsT_ready, pv_done, out_read = sem("probsT_ready"), sem("pv_done"), sem("out_read")
        probsT_copied = {"V": sem("probsT_copied_v"), "A": sem("probsT_copied_a")}
        weights_scaled = sem("weights_scaled")
        xmax_ready, xmax_all, xq_ready = sem("xmax_ready"), sem("xmax_all"), sem("xq_ready")
        hmax_ready, hmax_all = sem("hmax_ready"), sem("hmax_all")
        hscale_ready, hscaled, hclipped = sem("hscale_ready"), sem("hscaled"), sem("hclipped")
        hq_ready0, hq_ready1 = sem("hq_ready0"), sem("hq_ready1")
        l1_gate, l1_silu, l1_up, l1_hidden, l1_down = (sem("l1_" + n) for n in ("gate", "silu", "up", "hidden", "down"))
        router_in, router_exp, cw_ready = sem("router_in"), sem("router_exp"), sem("cw_ready")
        moe = {l: {n: sem(f"moe{l}_{n}") for n in ("gate", "act", "up", "mixed", "scaled", "hi", "lo", "down", "raw0",
                                                   "raw1", "w_hi", "w_lo", "x_hi", "x_lo", "summed")} for l in (0, 2)}
        cw_stored, cw_loaded = sem("cw_stored"), [sem(f"cw_loaded{e}") for e in range(E)]
        rope_in, rope_done, vones = sem("rope_in"), sem("rope_done"), sem("vones")
        swapped = [sem(f"swapped{c}") for c in range(4)]
        heads_ready, pair_hi, pair_lo = sem("heads_ready"), sem("pair_hi"), sem("pair_lo")
        silu3, s3_ready, out_stored = sem("silu3"), sem("s3_ready"), sem("out_stored")

        block = ctx.enter_context(nc.Block())

        def loaded(eng, *names):
            for n in names:
                eng.wait_ge(loads[n][1], 16 * group_size[loads[n][2]])

        def emptied(eng, name):
            i = AT[name]
            eng.wait_ge(misc_emptied_v if MISC[i][1] == "V" else misc_emptied_a, EMPTIED[i])

        def filled(eng, name):
            eng.wait_ge(misc_ready, AT[name] + 1)
            return MB[AT[name] % 2]

        def copied(eng, u):
            eng.wait_ge(probsT_copied[COPIER[u]], sum(c == COPIER[u] for c in COPIER[:u + 1]))

        def store_parts(eng, parts_ready, parts, store, stored, n, f):
            for a in range(NPART):
                if parts_ready is qparts_ready:
                    eng.wait_ge(qparts_ready, NPART * (2 * n + f) + a + 1)
                elif a == 0:
                    eng.wait_ge(kparts_ready, 2 * n + f + 1)
                eng.dma_start(store[n, f, a].rearrange("d h t -> h d t"),
                             parts[:, a, 512 * f:512 * f + 512]).then_inc(stored[f], 16)

        def stack_keys(eng, n, f):
            eng.wait_ge(kp_stored[f], 16 * NPART * (n + 1))
            src = bass.AP(kpd.tensor, kpd[n, f].offset, [[0, NPART], [NH * 512, NPART * DH], [1, NH * 512]])
            eng.dma_start(KS[:, f].rearrange("p h t -> p (h t)"), src).then_inc(ks_loaded[f], 16)

        def hidden2(j):
            k = j % 2
            if j % 4 < 2:
                return hh[:, k, :], hl[:, k, :], PT[:, k, :]
            return hh_more[:, k, :], hl_more[:, k, :], PR[:, k, :]

        def rest_done(eng, j):
            eng.wait_ge(moe[2]["lo"], j + 1)

        def pair(g):
            t, c, s = g // 4, g % 4, g % 2
            return ((kh3[:, s, :], kl3[:, s, :], KT3[:, c, t // 2, :]),
                    (qh3[:, s, :], ql3[:, s, :], QT3[:, c, t * P:(t + 1) * P]))

        def bc(ap, n):
            return ap.unsqueeze(2).to_broadcast([ap.shape[0], ap.shape[1], n])

        @block.sync
        def _(sp):
            def fetch(name, ap):
                sp.dma_start(loads[name][0][:], ap).then_inc(loads[name][1], 16)

            sp.dma_start(x[:], I["x"].rearrange("(t p) d -> p t d", p=P)).then_inc(ld_x, 16)
            sp.dma_start(ctxT[:], I["ctxT"]).then_inc(ld_ctxT, 16)
            for n in ("wk0", "b0", "ident", "wq0"):
                fetch(n, I[n])
            sp.dma_start(erf[:], I["erT"]).then_inc(ld_er, 16)
            for n in ("wv0", "wk2", "wk1", "wv1", "b1", "wg", "wu", "wd", "maskf"):
                fetch(n, I[n])
            for n in ("bv0", "bv1", "gates", "clips"):
                fetch(n, I[n].partition_broadcast(P))

            def stack_queries(n, f):
                sp.wait_ge(qp_stored[f], 16 * NPART * (n + 1))
                for a in range(NPART):
                    src = bass.AP(qpd.tensor, qpd[n, f, a].offset, [[0, NPART], [NH * 512, DH], [1, NH * 512]])
                    sp.dma_start(QS[NPART * DH * a:NPART * DH * (a + 1), f].rearrange("p h t -> p (h t)"), src) \
                        .then_inc(qs_loaded[f], 16)

            def experts(layer, e):
                m, s = moe[layer], e % 2
                if e >= 2:
                    sp.wait_ge(m["w_lo"], PIECES[layer] * (e - 1))
                if layer == 0:
                    sp.dma_start(ring[:, s, 0:512], I["f1"][e]).then_inc(m[f"raw{s}"], 16)
                    sp.dma_start(ring[:, s, 512:1024], I["f2"][e]).then_inc(m[f"raw{s}"], 16)
                    sp.dma_start(ring[:, s, 1024:1536].rearrange("p (c d) -> p c d", c=4),
                                 I["f3"][e].rearrange("(c p) d -> p c d", p=P)).then_inc(m[f"raw{s}"], 16)
                else:
                    sp.dma_start(ring[:, s, 0:256], I["g1"][e]).then_inc(m[f"raw{s}"], 16)
                    sp.dma_start(ring[:, s, 256:512].rearrange("p (c d) -> p c d", c=2),
                                 I["g2"][e].rearrange("(c p) d -> p c d", p=P)).then_inc(m[f"raw{s}"], 16)

            def store_coefficients(i, layer):
                emptied(sp, f"cwT{layer}.1")
                sp.dma_start(cwd[i], cwT[:]).then_inc(cw_stored, 16)
                sp.wait_ge(cw_stored, 16 * (i + 1))

            def spread_coefficients(i, e):
                if e < E:
                    sp.dma_start(cwB[:, e, :], cwd[i, e].partition_broadcast(P)).then_inc(cw_loaded[e], 16)

            sp.wait_ge(erparts_ready, 1)
            for c in range(NPART * NPART):
                sp.dma_start(ES[c * DH:(c + 1) * DH, :], erp[:, c % NPART, :]).then_inc(es_loaded, 16)
            store_parts(sp, kparts_ready, kparts, kpd, kp_stored, 0, 0)
            store_parts(sp, qparts_ready, qparts, qpd, qp_stored, 0, 0)
            store_parts(sp, kparts_ready, kparts, kpd, kp_stored, 0, 1)
            stack_queries(0, 0)
            stack_keys(sp, 0, 0)
            store_parts(sp, qparts_ready, qparts, qpd, qp_stored, 0, 1)

            def store_rel(r):
                emptied(sp, f"qer.{r}")
                sp.dma_start(relpos[r], stage[:, r % STAGE, :]).then_inc(rel_stored[r % STAGE], 16)

            def load_rel(r):
                w = UNITS8[r][3]
                sp.wait_ge(rel_stored[r % STAGE], 16 * (r // STAGE + 1))
                if r >= SKEW:
                    sp.wait_ge(min_ready, r - SKEW + 1)
                src = bass.AP(relpos.tensor, relpos[r].offset + P - 1, [[512 - 1, P], [w, 512 // w], [1, w]])
                sp.dma_start(skewed[:, r % SKEW, :].rearrange("p (g w) -> p g w", w=w), src) \
                    .then_inc(rel_loaded[r % SKEW], 16)

            for r in range(N8 + 1):
                if r < N8:
                    store_rel(r)
                if r >= 1:
                    load_rel(r - 1)
                if r == 3:
                    stack_keys(sp, 0, 1)
                if r == 12:
                    stack_queries(0, 1)
                if r == N8:
                    experts(0, 0)
            for n in ("iota", "wr0", "hb1", "hb2", "hb3"):
                fetch(n, I[n])
            for n in ("br0", "br2"):
                fetch(n, I[n].partition_broadcast(P))
            experts(0, 1)
            for f in range(2):
                store_parts(sp, kparts_ready, k2parts, kpd, kp_stored, 1, f)
            for n in ("wq1", "wq2", "wv2", "wo2", "maski", "wr2", "gb1", "gb2"):
                fetch(n, I[n])
            sp.dma_start(ctxr[:], I["ctx"].rearrange("(t p) d -> p t d", p=P)).then_inc(ld_ctx, 16)
            for n in ("cos", "sin", "lnp", "wr3"):
                fetch(n, I[n])
            store_coefficients(0, 0)
            spread_coefficients(0, 1)
            for e in range(2, E):
                spread_coefficients(0, e)
                experts(0, e)
                if e < 4:
                    sp.wait_ge(scores_ready, N8)
                    stack_keys(sp, 1, e - 2)
            sp.wait_ge(moe[0]["up"], JOBS[0] * E)
            sp.dma_start(closed, I["mrow"].partition_broadcast(P)).then_inc(ld_mrow, 16)
            for f in range(2):
                store_parts(sp, qparts_ready, qparts, qpd, qp_stored, 1, f)
                stack_queries(1, f)
            experts(2, 0)
            experts(2, 1)
            sp.wait_ge(scores_ready, BASE[3])
            for n in ("wq3", "wkv3", "wo3", "wuv", "wf3"):
                fetch(n, I[n])
            experts(2, 2)
            store_coefficients(1, 2)
            for e in range(1, 4):
                spread_coefficients(1, e)
            for e in range(3, E):
                spread_coefficients(1, e + 1)
                experts(2, e)
            HALF = DH3 // 2
            for c in range(4):
                emptied(sp, f"kc.{c}.1")
                for p in range(0, P, HALF):
                    q = p + HALF if p % DH3 == 0 else p - HALF
                    sp.dma_start(k_swapped(c)[p:p + HALF], KT3[q:q + HALF, c, :, 0:S]).then_inc(swapped[c], 16)
            for t in range(NT):
                emptied(sp, f"y3.{t}")
                sp.dma_start(out[t * P:(t + 1) * P, :], x[:, t, :]).then_inc(out_stored, 16)
            sp.wait_ge(out_stored, 16 * NT)

        @block.gpsimd
        def _(pool):
            nc.gpsimd.memset(ones[:], 1.0).then_inc(pool_consts, 1)
            nc.gpsimd.memset(mhalf[:], -0.5).then_inc(pool_consts, 1)
            nc.gpsimd.memset(V9[:, :, :, DH:DH + 1], 1.0).then_inc(pool_consts, 1)
            nc.gpsimd.memset(v9[:, NT * NH * (DH + 1):], 0.0).then_inc(pool_consts, 1)
            nc.gpsimd.memset(VA[:, :, D:D + 1], 1.0).then_inc(pool_consts, 1)
            nc.gpsimd.memset(amh, 0.0).then_inc(pool_consts, 1)
            nc.gpsimd.memset(minus_round, -ROUND).then_inc(pool_consts, 1)

            count = [0]

            def link(ins):
                count[0] += 1
                ins.then_inc(g_step, 1)
                pool.wait_ge(g_step, count[0])

            def rsqrt(n):
                for f in range(2):
                    s = slice(4 * f, 4 * f + 4)
                    pool.wait_ge(variance_ready, 2 * n + f + 1)
                    nc.gpsimd.tensor_tensor(rstd[:, s], veps[:, s], mhalf[:, s], ALU.pow).then_inc(rstd_ready, 1)

            def split_keys(name, k, parts, i):
                s = slice(512 * (i % 2), 512 * (i % 2) + 512)
                emptied(pool, f"{name}.{i % 2}")
                pool.wait_ge(keys_rounded, (1, 2, 5, 6)[i])
                nc.gpsimd.tensor_tensor(k[:, s], k[:, s], parts[:, 0, s], ALU.subtract).then_inc(keys_left, 1)
                pool.wait_ge(keys_rounded, (3, 4, 7, 8)[i])
                nc.gpsimd.tensor_tensor(parts[:, 2, s], k[:, s], parts[:, 1, s], ALU.subtract).then_inc(kparts_ready, 1)

            pool.wait_ge(pool_consts, 2)
            rsqrt(0)
            split_keys("k0", kf, kparts, 0)
            split_keys("k0", kf, kparts, 1)
            for i in (2, 3):
                split_keys("k2", k2f, k2parts, i)
            for r in range(N8):
                w = UNITS8[r][3]
                pool.wait_ge(rel_loaded[r % SKEW], 16 * (r // SKEW + 1))
                v = skewed[:, r % SKEW, :].rearrange("p (g w) -> p g w", w=w)[:, :, w - P:w]
                nc.gpsimd.affine_select(out=v, in_=v, pattern=[[0, 512 // w], [-1, P]], compare_op=ALU.is_ge,
                                        fill=BIG, base=0, channel_multiplier=1).then_inc(rel_masked, 1)
            def split_piece(e, k):
                m, s, a = moe[0], e % 2, PIECE * k
                pool.wait_ge(m["w_hi"], PIECES[0] * e + k + 1)
                nc.gpsimd.tensor_tensor(wl[:, s, a:a + PIECE], ring[:, s, a:a + PIECE],
                                        wh[:, s, a:a + PIECE].bitcast(F32), ALU.subtract).then_inc(m["w_lo"], 1)

            rsqrt(1)
            for k in range(PIECES[0]):
                split_piece(0, k)
            m = moe[0]
            for j in range(E * 8):
                e, n = j // 8, j % 2
                if j < 2:
                    emptied(pool, f"cwB0.{n}")
                elif e >= 1 and j % 8 == 0:
                    pool.wait_ge(cw_loaded[e], 16)
                pool.wait_ge(m["mixed"], j + 1)
                if j >= 2:
                    pool.wait_ge(m["lo"], j - 1)
                nc.gpsimd.tensor_tensor(PT[:, j % 2, :], PR[:, j % 2, :], cwB[:, e, 512 * n:512 * n + 512],
                                        ALU.mult).then_inc(m["scaled"], 1)
                if e + 1 < E and j % 8 in PIECE_AT[0]:
                    split_piece(e + 1, PIECE_AT[0].index(j % 8))
            for n in (2, 3):
                rsqrt(n)
            pool.wait_ge(xmax_ready, 1)
            nc.gpsimd.partition_all_reduce(amxg, amx, P, RMAX).then_inc(xmax_all, 1)
            pool.wait_ge(hmax_ready, 1)
            nc.gpsimd.partition_all_reduce(amhg, amh, P, RMAX).then_inc(hmax_all, 1)
            pool.wait_ge(hscale_ready, 1)
            v = h1[0:CI, :, 512:1024]
            nc.gpsimd.tensor_scalar(v, v, ish[0:CI, :], ROUND, ALU.mult, ALU.add).then_inc(hscaled, 1)
            for n in (4, 5, 6):
                rsqrt(n)
            m = moe[2]
            for j in range(E * 4):
                pool.wait_ge(m["hi"], j + 1)
                if j >= 4:
                    pool.wait_ge(m["down"], j - 3)
                hi, lo, rows = hidden2(j)
                nc.gpsimd.tensor_tensor(lo, rows, hi.bitcast(F32), ALU.subtract).then_inc(m["lo"], 1)
            pool.wait_ge(m["down"], E * 4)
            nc.gpsimd.memset(VX[:, :, :, DH3:DH3 + 1], 1.0).then_inc(vones, 1)
            nc.gpsimd.memset(arenaB[:, 16 * NH3 * (DH3 + 1):], 0.0).then_inc(vones, 1)
            rsqrt(7)
            rsqrt(8)
            for c in range(4):
                pool.wait_ge(rope_in, 2 * c + 2)
                nc.gpsimd.tensor_tensor(KT3[:, c, :, 0:S], KT3[:, c, :, 0:S], k_swapped(c), ALU.add) \
                    .then_inc(rope_done, 1)
            def root(t):
                pool.wait_ge(variance_ready, 2 * 9 + t + 1)
                nc.gpsimd.tensor_tensor(rstd[:, t:t + 1], veps[:, t:t + 1], mhalf[:, t:t + 1], ALU.pow) \
                    .then_inc(rstd_ready, 1)

            def silu_denominator(t):
                pool.wait_ge(silu3, 4 * t + 1)
                nc.gpsimd.tensor_scalar(sg[:, 1, 0:256], sg[:, 1, 0:256], 1.0, None, ALU.add).then_inc(silu3, 1)

            def expert_rows(t):
                pool.wait_ge(cw_ready, 2 + t + 1)
                emptied(pool, f"uv.{t}")
                pool.wait_ge(silu3, 4 * t + 4)
                w = Sx[:, 1, 256:512]
                link(nc.gpsimd.tensor_tensor(w, w, sg[:, 1, 0:256], ALU.mult))
                if t >= 1:
                    filled(pool, f"sT.{t - 1}")
                nc.gpsimd.tensor_tensor(Sx[:, 0, 0:256].rearrange("p (e r) -> p e r", e=E),
                                        w.rearrange("p (e r) -> p e r", e=E),
                                        bc(cw[:, t, :], 32), ALU.mult).then_inc(s3_ready, 1)

            def rest_of_pair(g):
                for k, (hi, lo, raw) in enumerate(pair(g)):
                    pool.wait_ge(pair_hi, 2 * g + k + 1)
                    nc.gpsimd.tensor_tensor(lo, raw, hi.bitcast(F32), ALU.subtract).then_inc(pair_lo, 1)

            rest_of_pair(0)
            for i in range(N3 + WEIGH + 10):
                if i % 2 == 0 and i // 2 + 1 < N3 // 2:
                    rest_of_pair(i // 2 + 1)
                for behind, work in ((2, root), (6, silu_denominator), (9, expert_rows)):
                    if _tile3(i, behind) is not None:
                        work(_tile3(i, behind))

        @block.scalar
        def _(act):
            def take(name, dst, func=ACT.Copy, **kw):
                bank = filled(act, name)
                nc.scalar.activation(dst, bank, func, **kw).then_inc(misc_emptied_a, 1)

            def load_table(func):
                nc.scalar.activation(small[:, 60:61], ones[:, 0:1], func)

            def halves(name, dst, func=ACT.Copy, **kw):
                for n in range(2):
                    take(f"{name}.{n}", dst[:, 512 * n:512 * n + 512], func, **kw)

            def rel(r):
                if r >= STAGE:
                    act.wait_ge(rel_stored[r % STAGE], 16 * (r // STAGE))
                take(f"qer.{r}", stage[:, r % STAGE, :])

            def exps(layer, i):
                _, _, g, w = UNITS[layer][i]
                u = BASE[layer] + i
                act.wait_ge(min_ready, u + 1)
                if u >= 2:
                    act.wait_ge(probsT_ready, u - 1)
                src = Sx[:, u % 2, :] if layer < 3 else SC[u % 2]
                for k in range(g):
                    ins = nc.scalar.activation(PR[:, u % 2, k * w:(k + 1) * w], src[:, k * w:(k + 1) * w], ACT.Exp,
                                               bias=smin[:, u % 2, k:k + 1], scale=-1.0)
                ins.then_inc(probs_ready, 1)

            def copy_probs(layer, i):
                u = BASE[layer] + i
                if COPIER[u] == "A":
                    act.wait_ge(probsT_ready, u + 1)
                    if u >= 2:
                        act.wait_ge(pv_done, u - 1)
                    nc.scalar.activation(PT[:, u % 2, :], TP[u % 2], ACT.Copy).then_inc(probsT_copied["A"], 1)

            def round_pair(g):
                if g >= 2:
                    act.wait_ge(scores_ready, BASE[3] + 2 * (g - 1))
                for hi, _, raw in pair(g):
                    nc.scalar.activation(hi, raw, ACT.Copy).then_inc(pair_hi, 1)

            def finished_tile(i):
                t = _tile3(i, 1)
                if t is not None:
                    if t >= 1:
                        emptied(act, f"wo3.{t - 1}")
                    take(f"oT3.{t}", sg[:, 0, :])
                t = _tile3(i, 4)
                if t is not None:
                    bank = filled(act, f"ln9.{t}")
                    nc.scalar.activation(xnT[:, P * t:P * t + P], bank[:, 0:P], ACT.Copy).then_inc(misc_emptied_a, 1)
                t = _tile3(i, 6)
                if t is not None:
                    if t >= 1:
                        act.wait_ge(s3_ready, t)
                    bank = filled(act, f"uv.{t}")
                    nc.scalar.activation(sg[:, 1, 0:256], bank[:, 0:256], ACT.Exp, scale=-1.0).then_inc(silu3, 1)
                    act.wait_ge(router_in, 2 + t + 1)
                    nc.scalar.activation(rw[:, 1, t:t + 1], rw[:, 0, t:t + 1], ACT.Exp).then_inc(router_exp, 1)
                t = _tile3(i, 11)
                if t is not None:
                    if t >= 1:
                        filled(act, f"y3.{t - 1}")
                    bank = filled(act, f"sT.{t}")
                    nc.scalar.activation(Sx[:, 1, 0:256], bank[:, 0:256], ACT.Copy).then_inc(misc_emptied_a, 1)

            def attention(layer):
                for i in range(len(UNITS[layer]) + WEIGH + (13 if layer == 3 else 2)):
                    if layer == 0 and i + LEAD < N8:
                        rel(i + LEAD)
                    if layer == 3 and i % 2 == 0 and i // 2 + 1 < N3 // 2:
                        round_pair(i // 2 + 1)
                    if i < len(UNITS[layer]):
                        exps(layer, i)
                    if 0 <= i - TURN < len(UNITS[layer]):
                        copy_probs(layer, i - TURN)
                    if layer == 3:
                        finished_tile(i)

            def round_piece(layer, e, k):
                m, s, a = moe[layer], e % 2, PIECE * k
                if k == 0:
                    act.wait_ge(m[f"raw{s}"], (48 if layer == 0 else 32) * (e // 2 + 1))
                    if e >= 2:
                        act.wait_ge(m["up" if layer == 0 else "gate"], JOBS[layer] * (e - 1))
                if e >= 2 and a >= (1024 if layer == 0 else 256):
                    act.wait_ge(m["down"], JOBS[layer] * (e - 1))
                nc.scalar.activation(wh[:, s, a:a + PIECE], ring[:, s, a:a + PIECE], ACT.Copy).then_inc(m["w_hi"], 1)

            def next_piece(layer, j):
                e, k = j // JOBS[layer], j % JOBS[layer]
                if e + 1 < E and k in PIECE_AT[layer]:
                    round_piece(layer, e + 1, PIECE_AT[layer].index(k))

            def round_rows(layer):
                emptied(act, f"ln{5 if layer else 1}.1")
                nc.scalar.activation(xh[:], xnT[:], ACT.Copy).then_inc(moe[layer]["x_hi"], 1)

            def first_coefficients(layer):
                for n in range(2):
                    take(f"cwB{layer}.{n}", cwB[:, 0, 512 * n:512 * n + 512])

            def experts0():
                m = moe[0]
                for j in range(E * 8 + 1):
                    if j < E * 8:
                        e, c = j // 8, j // 2 % 4
                        act.wait_ge(m["gate"], j + 1)
                        if j >= 2:
                            act.wait_ge(m["mixed"], j - 1)
                        nc.scalar.activation(sg[:, j % 2, :], SC[j % 2], ACT.Silu, bias=hb1[:, e, c:c + 1]) \
                            .then_inc(m["act"], 1)
                    if j == 1:
                        first_coefficients(0)
                        for f in range(2):
                            act.wait_ge(kp_stored[f], 16 * NPART * 2)
                    if j >= 1:
                        act.wait_ge(m["scaled"], j)
                        if j >= 3:
                            act.wait_ge(m["down"], j - 2)
                        nc.scalar.activation(hh[:, (j - 1) % 2, :], PT[:, (j - 1) % 2, :], ACT.Copy) \
                            .then_inc(m["hi"], 1)
                    next_piece(0, j)

            def experts2():
                m = moe[2]
                for j in range(E * 4):
                    e, c = j // 4, j // 2 % 2
                    act.wait_ge(m["gate"], j + 1)
                    if j >= 2:
                        act.wait_ge(m["scaled"], j - 1)
                    nc.scalar.activation(sg[:, j % 2, :], SC[j % 2], ACT.Gelu, bias=gb1[:, e, c:c + 1]) \
                        .then_inc(m["act"], 1)
                    if j == 1:
                        first_coefficients(2)
                    next_piece(2, j)

            def take_sums(layer):
                for n in range(2):
                    act.wait_ge(moe[layer]["down"], E * (8 if layer == 0 else 4) - 1 + n)
                    nc.scalar.activation(xnT[:, 512 * n:512 * n + 512], OB[n], ACT.Copy) \
                        .then_inc(moe[layer]["summed"], 1)

            def router(n):
                act.wait_ge(router_in, n + 1)
                if n == 1:
                    nc.scalar.activation(lg[:], lg[:], ACT.Exp).then_inc(router_exp, 1)
                else:
                    nc.scalar.activation(rw[:, 1, :], rw[:, 0, :], ACT.Exp).then_inc(router_exp, 1)

            def keys(name, k, parts, i, **kw):
                s = slice(512 * (i % 2), 512 * (i % 2) + 512)
                bank = filled(act, f"{name}.{i % 2}")
                nc.scalar.activation(parts[:, 0, s], bank, ACT.Identity, **kw).then_inc(keys_rounded, 1)
                nc.scalar.activation(k[:, s], bank, ACT.Identity, **kw).then_inc(misc_emptied_a, 1)

            def keys_part1(k, parts, i):
                s = slice(512 * (i % 2), 512 * (i % 2) + 512)
                act.wait_ge(keys_left, i + 1)
                nc.scalar.activation(parts[:, 1, s], k[:, s], ACT.Identity).then_inc(keys_rounded, 1)

            act.wait_ge(pool_consts, 7)
            loaded(act, "b0")
            for i in range(2):
                keys("k0", kf, kparts, i, bias=b0[:, 1:2])
            halves("ln0", xnT)
            for i in range(2):
                keys_part1(kf, kparts, i)
            act.wait_ge(nbq_ready, 1)
            halves("q0", qf, ACT.Identity, bias=nbq0, scale=-SLICE8)
            loaded(act, "gates", "clips")
            nc.scalar.activation(tg[:], gates[:], ACT.Tanh).then_inc(gates_ready, 1)
            nc.scalar.activation(sg2, clips[:], ACT.Exp, scale=-1.0).then_inc(sig_exp, 1)
            for i in (2, 3):
                keys("k2", k2f, k2parts, i)
            keys_part1(k2f, k2parts, 2)
            for r in range(STAGE):
                rel(r)
            keys_part1(k2f, k2parts, 3)
            loaded(act, "b1")
            halves("k1", k1f, ACT.Identity, bias=b1[:, 1:2])
            for r in range(STAGE, LEAD):
                rel(r)
            attention(0)
            for k in range(PIECES[0]):
                round_piece(0, 0, k)
            halves("ln1", xnT)
            round_rows(0)
            router(0)
            loaded(act, "hb1")
            experts0()
            take_sums(0)
            for n in range(2):
                bank = filled(act, f"v2.{n}")
                for k in range(4):
                    ins = nc.scalar.activation(V9[:, 4 * n + k, :, 0:DH],
                                               bank[:, 128 * k:128 * k + 128].rearrange("p (h e) -> p h e", h=NH),
                                               ACT.Copy)
                ins.then_inc(misc_emptied_a, 1)
            load_table(ACT.Exp)
            halves("ln2", xnT)
            act.wait_ge(nbq_ready, 2)
            halves("q1", qf, ACT.Identity, bias=nbq1, scale=-SLICE8)
            attention(1)
            for n in range(2):
                bank = filled(act, f"mean.{n}")
                nc.scalar.activation(mean[:, 2 * n:2 * n + 2, :, :],
                                     bank[:, 0:2 * 144].rearrange("p (b h e) -> p b h e", b=2, h=NH), ACT.Copy,
                                     scale=1.0 / S).then_inc(misc_emptied_a, 1)
            load_table(ACT.Silu)
            halves("ln3", xnT)
            for j in range(2 * NI):
                act.wait_ge(l1_gate, j + 1)
                if j >= 2:
                    act.wait_ge(l1_hidden, j - 1)
                if j == 0:
                    act.wait_ge(xq_ready, 1)
                nc.scalar.activation(sg[0:CI, j % 2, :], SC[j % 2][0:CI, :], ACT.Silu,
                                     scale=fg[:, j // 2:j // 2 + 1]).then_inc(l1_silu, 1)
            act.wait_ge(hclipped, 1)
            nc.scalar.activation(h1q[0:CI, :, 0:512], h1[0:CI, :, 0:512], ACT.Identity, bias=minus_round[0:CI, :]) \
                .then_inc(hq_ready0, 1)
            halves("ln4", xnT)
            halves("q2", qf, scale=-SLICE8)
            attention(2)
            halves("oT2", xnT)
            for k in range(PIECES[2]):
                round_piece(2, 0, k)
            halves("ln5", xnT)
            round_rows(2)
            router(1)
            loaded(act, "gb1")
            experts2()
            take_sums(2)
            for c in range(4):
                for n in range(2):
                    bank = filled(act, f"kc.{c}.{n}")
                    nc.scalar.activation(KT3[:, c, 2 * n:2 * n + 2, 0:S], bank.rearrange("p (b t) -> p b t", b=2),
                                         ACT.Copy).then_inc(misc_emptied_a, 1)
            act.wait_ge(vones, 2)

            def values(kind):
                for t in range(0, NT, 1 if kind == "vc" else 2):
                    k = 4 * (t // 2) + 2 * (kind == "vl") + t % 2
                    bank = filled(act, f"{kind}.{t}")
                    nc.scalar.activation(VX[:, k, :, 0:DH3], bank.rearrange("p (h e) -> p h e", h=NH3),
                                         ACT.Copy).then_inc(misc_emptied_a, 1)

            values("vc")
            for c in range(4):
                for n in range(2):
                    bank = filled(act, f"kl.{c}.{n}")
                    nc.scalar.activation(KT3[:, c, 2 * n:2 * n + 2, S:2 * S], bank.rearrange("p (b t) -> p b t", b=2),
                                         ACT.Copy).then_inc(misc_emptied_a, 1)
                    take(f"q3.{c}.{n}", QT3[:, c, 512 * n:512 * n + 512], scale=-float(DH3) ** -0.5)
            load_table(ACT.Exp)
            values("vl")
            act.wait_ge(rope_done, 4)
            emptied(act, "q3.3.1")
            round_pair(0)
            attention(3)

        @block.vector
        def _(dve):
            count = [0]

            def link(ins):
                count[0] += 1
                ins.then_inc(v_step, 1)
                dve.wait_ge(v_step, count[0])

            def moments(n, src, tiles, k=None):
                for t in tiles:
                    if k is not None and k > 0:
                        dve.wait_ge(x_updated, NT * (k - 1) + t + 1)
                    nc.vector.bn_stats(st[:, t, :], src[:, t, :]).then_inc(stats_ready, 1)
                for t in tiles:
                    dve.wait_ge(stats_ready, NT * n + t + 1)
                    nc.vector.bn_aggr(mv[:, t, :], st[:, t, :]).then_inc(moments_ready, 1)
                if t % 4 == 3:
                    dve.wait_ge(moments_ready, NT * n + t + 1)
                    nc.vector.tensor_scalar(veps[:, t - 3:t + 1], mv[:, t - 3:t + 1, 1], EPS, None, ALU.add) \
                        .then_inc(variance_ready, 1)

            def norm_rows(n, src, k=None, dst=None):
                for f in range(2):
                    moments(n, src, range(4 * f, 4 * f + 4), k)
                for t in range(NT):
                    if t % 4 == 0:
                        dve.wait_ge(rstd_ready, 2 * n + t // 4 + 1)
                    nc.vector.tensor_scalar((dst or xn)[:, t, :], src[:, t, :], mv[:, t, 0:1], rstd[:, t:t + 1],
                                            ALU.subtract, ALU.mult).then_inc(rows_normed, 1)

            def take_rows(name, dst, add):
                bank = filled(dve, name)
                v = bank.rearrange("p (t e) -> p t e", t=4)
                nc.vector.tensor_tensor(dst, v, add, ALU.add).then_inc(misc_emptied_v, 1)

            def values8(name, bias):
                for n in range(2):
                    bank = filled(dve, f"{name}.{n}")
                    for k in range(4):
                        dst = V9[:, 4 * n + k, :, 0:DH]
                        v = bank[:, 128 * k:128 * k + 128].rearrange("p (h e) -> p h e", h=NH)
                        if bias is None:
                            ins = nc.vector.tensor_copy(dst, v)
                        else:
                            ins = nc.vector.tensor_tensor(dst, v, bias[:].rearrange("p (h e) -> p h e", h=NH), ALU.add)
                    ins.then_inc(misc_emptied_v, 1)

            def split_queries(name):
                def part(ins):
                    ins.then_inc(qparts_ready, 1)
                    qp[0] += 1

                for f in range(2):
                    emptied(dve, f"{name}.{f}")
                    q, s = qf[:, 512 * f:512 * f + 512], slice(512 * f, 512 * f + 512)
                    part(nc.vector.tensor_copy(qparts[:, 0, s], q))
                    dve.wait_ge(qparts_ready, qp[0])
                    link(nc.vector.tensor_tensor(q, q, qparts[:, 0, s], ALU.subtract))
                    part(nc.vector.tensor_copy(qparts[:, 1, s], q))
                    dve.wait_ge(qparts_ready, qp[0])
                    part(nc.vector.tensor_tensor(qparts[:, 2, s], q, qparts[:, 1, s], ALU.subtract))

            qp = [0]

            def minima(layer, i):
                t, _, g, w = UNITS[layer][i]
                u = BASE[layer] + i
                dve.wait_ge(scores_ready, u + 1)
                if u >= 2:
                    dve.wait_ge(probs_ready, u - 1)
                if layer < 3:
                    if layer == 0:
                        dve.wait_ge(rel_masked, i + 1)
                    for k in range(g):
                        if layer == 0:
                            added = skewed[:, i % SKEW, k * w:(k + 1) * w]
                        else:
                            added = closed[:, i * S:(i + 1) * S] if layer == 1 else maskf[:, S - w:S]
                        ins = nc.vector.tensor_tensor_reduce(
                            Sx[:, u % 2, k * w:(k + 1) * w], SC[u % 2][:, k * w:(k + 1) * w], added,
                            1.0, 3e38, ALU.add, ALU.min,
                            smin[:, u % 2, k:k + 1])
                    ins.then_inc(min_ready, 1)
                else:
                    nc.vector.tensor_reduce(smin[:, u % 2, 0:g], SC[u % 2].rearrange("p (g w) -> p g w", w=w),
                                            AX.X, ALU.min).then_inc(min_ready, 1)

            def copy_probs(layer, i):
                u = BASE[layer] + i
                if COPIER[u] == "V":
                    dve.wait_ge(probsT_ready, u + 1)
                    if u >= 2:
                        dve.wait_ge(pv_done, u - 1)
                    nc.vector.tensor_copy(PT[:, u % 2, :], TP[u % 2]).then_inc(probsT_copied["V"], 1)

            def finish(layer, k):
                u = BASE[layer] + LAST[layer][k]
                g = GROUPS[layer] + k
                dve.wait_ge(pv_done, u + 1)
                if layer in (0, 2):
                    O = OB[g % 2][:, 0:NH * (DH + 1)].rearrange("p (h e) -> p h e", h=NH)
                    link(nc.vector.reciprocal(rsum[:], O[:, :, DH]))
                    y = xn[:, k, :]
                    link_to = nc.vector.tensor_tensor(y.rearrange("p (h e) -> p h e", h=NH), O[:, :, 0:DH],
                                                      bc(rsum[:], DH), ALU.mult)
                    link_to.then_inc(out_read, 1)
                    dve.wait_ge(out_read, g + 1)
                    if layer == 0:
                        nc.vector.scalar_tensor_tensor(x[:, k, :], y, tg[:, 0:1], x[:, k, :], ALU.mult, ALU.add) \
                            .then_inc(x_updated, 1)
                    else:
                        m = mean[:, k // 2, :, 0:DH]
                        yv = y.rearrange("p (h e) -> p h e", h=NH)
                        d = sg[:, 1, 0:D]
                        link(nc.vector.tensor_tensor(d.rearrange("p (h e) -> p h e", h=NH), m, yv, ALU.subtract))
                        nc.vector.scalar_tensor_tensor(y, d, mk2[:, k:k + 1], y, ALU.mult, ALU.add) \
                            .then_inc(heads_ready, 1)
                elif layer == 1:
                    O = OB[g % 2][:, 0:2 * (D + 1)].rearrange("p (t e) -> p t e", t=2)
                    link(nc.vector.reciprocal(rsum[:, 0:2], O[:, :, D]))
                    y = xn[:, 2 * k:2 * k + 2, :]
                    nc.vector.tensor_tensor(y, O[:, :, 0:D], bc(rsum[:, 0:2], D), ALU.mult).then_inc(out_read, 1)
                    dve.wait_ge(out_read, g + 1)
                    for t in (2 * k, 2 * k + 1):
                        nc.vector.scalar_tensor_tensor(x[:, t, :], xn[:, t, :], tg[:, 1:2], x[:, t, :],
                                                       ALU.mult, ALU.add).then_inc(x_updated, 1)
                else:
                    if k >= 1:
                        filled(dve, f"oT3.{k - 1}")
                    for n in range(2):
                        O = OB[n][:, 0:4 * (DH3 + 1)].rearrange("p (h e) -> p h e", h=4)
                        link(nc.vector.reciprocal(rsum[:, 4 * n:4 * n + 4], O[:, :, DH3]))
                        heads = stage3[:, 256 * n:256 * n + 256].rearrange("p (h e) -> p h e", h=4)
                        ins = nc.vector.tensor_tensor(heads, O[:, :, 0:DH3], bc(rsum[:, 4 * n:4 * n + 4], DH3),
                                                      ALU.mult)
                    ins.then_inc(out_read, 1)

            def attention(layer):
                n = len(UNITS[layer])
                for i in range(n + WEIGH + (14 if layer == 3 else 2)):
                    if i < n:
                        minima(layer, i)
                    if 0 <= i - TURN < n:
                        copy_probs(layer, i - TURN)
                    if i - WEIGH in LAST[layer]:
                        finish(layer, LAST[layer].index(i - WEIGH))
                    if layer == 3:
                        finished_tile(i)

            def finished_tile(i):
                t = _tile3(i, 2)
                if t is not None:
                    bank = filled(dve, f"wo3.{t}")
                    nc.vector.scalar_tensor_tensor(x[:, t, :], bank[:, 0:D], tg[:, 3:4], x[:, t, :],
                                                   ALU.mult, ALU.add).then_inc(misc_emptied_v, 1)
                    emptied(dve, f"wo3.{t}")
                    nc.vector.bn_stats(st[:, t, :], x[:, t, :]).then_inc(stats_ready, 1)
                    dve.wait_ge(stats_ready, NT * 9 + t + 1)
                    nc.vector.bn_aggr(mv[:, t, :], st[:, t, :]).then_inc(moments_ready, 1)
                    dve.wait_ge(moments_ready, NT * 9 + t + 1)
                    nc.vector.tensor_scalar(veps[:, t:t + 1], mv[:, t, 1:2], EPS, None, ALU.add) \
                        .then_inc(variance_ready, 1)
                t = _tile3(i, 3)
                if t is not None:
                    dve.wait_ge(rstd_ready, 2 * 9 + t + 1)
                    nc.vector.tensor_scalar(xn[:, t, :], x[:, t, :], mv[:, t, 0:1], rstd[:, t:t + 1],
                                            ALU.subtract, ALU.mult).then_inc(rows_normed, 1)
                t = _tile3(i, 13)
                if t is not None:
                    bank = filled(dve, f"y3.{t}")
                    nc.vector.scalar_tensor_tensor(x[:, t, :], bank[:, 0:D], tg[:, 7:8], x[:, t, :],
                                                   ALU.mult, ALU.add).then_inc(misc_emptied_v, 1)
                t = _tile3(i, 6)
                if t is not None:
                    bank = filled(dve, f"router3.{t}")
                    nc.vector.tensor_copy(lg[:, t, :], bank[:, 0:E]).then_inc(misc_emptied_v, 1)
                    emptied(dve, f"router3.{t}")
                    link(nc.vector.max(lmx[:, t, :], lg[:, t, :]))
                    nc.vector.tensor_tensor(rw[:, 0, t:t + 1], lmx[:, t, 1:2], lmx[:, t, 0:1], ALU.subtract) \
                        .then_inc(router_in, 1)
                    link(nc.vector.max_index(lix[:, t, :], lmx[:, t, :], lg[:, t, :]))
                    link(nc.vector.tensor_copy(lixf[:, t, :], lix[:, t, :]))
                    for k in range(2):
                        nc.vector.tensor_scalar(oh[:, k, t, :], iota[:], lixf[:, t, k:k + 1], None, ALU.is_equal)
                t = _tile3(i, 7)
                if t is not None:
                    dve.wait_ge(router_exp, 2 + t + 1)
                    link(nc.vector.tensor_scalar(rw[:, 2, t:t + 1], rw[:, 1, t:t + 1], 1.0, None, ALU.add))
                    link(nc.vector.reciprocal(rw[:, 3, t:t + 1], rw[:, 2, t:t + 1]))
                    link(nc.vector.tensor_tensor(rw[:, 2, t:t + 1], rw[:, 3, t:t + 1], rw[:, 1, t:t + 1], ALU.mult))
                    link(nc.vector.tensor_scalar(oh[:, 0, t, :], oh[:, 0, t, :], rw[:, 3, t:t + 1], None, ALU.mult))
                    nc.vector.scalar_tensor_tensor(cw[:, t, :], oh[:, 1, t, :], rw[:, 2, t:t + 1], oh[:, 0, t, :],
                                                   ALU.mult, ALU.add).then_inc(cw_ready, 1)
                t = _tile3(i, 8)
                if t is not None:
                    bank = filled(dve, f"uv.{t}")
                    if t >= 1:
                        dve.wait_ge(s3_ready, t)
                    link(nc.vector.tensor_copy(sg[:, 1, 256:512], bank[:, 0:256]))
                    nc.vector.tensor_tensor(Sx[:, 1, 256:512], bank[:, 256:512], sg[:, 1, 256:512], ALU.mult) \
                        .then_inc(misc_emptied_v, 1)
                for n in range(2):
                    t = _tile3(i, 8 + n)
                    if t is not None:
                        dve.wait_ge(silu3, 4 * t + 2 + n)
                        e = sg[:, 1, 128 * n:128 * n + 128]
                        nc.vector.reciprocal(e, e).then_inc(silu3, 1)

            def router(n, name, bias):
                bank = filled(dve, name)
                v = bank[:, 0:NT * E].rearrange("p (t e) -> p t e", t=NT)
                nc.vector.tensor_tensor(lg[:], v, bias[:].unsqueeze(1).to_broadcast([P, NT, E]), ALU.add) \
                    .then_inc(misc_emptied_v, 1)
                dve.wait_ge(misc_emptied_v, EMPTIED[AT[name]])
                for t in range(NT):
                    ins = nc.vector.max(lmx[:, t, :], lg[:, t, :])
                link(ins)
                for t in range(NT):
                    ins = nc.vector.max_index(lix[:, t, :], lmx[:, t, :], lg[:, t, :])
                link(ins)
                if n == 1:
                    nc.vector.tensor_tensor(lg[:], lg[:], bc(lmx[:, :, 0], E), ALU.subtract).then_inc(router_in, 1)
                else:
                    nc.vector.tensor_tensor(rw[:, 0, :], lmx[:, :, 1], lmx[:, :, 0], ALU.subtract) \
                        .then_inc(router_in, 1)
                link(nc.vector.tensor_copy(lixf[:], lix[:]))
                iot = iota[:].unsqueeze(1).to_broadcast([P, NT, E])
                nc.vector.tensor_tensor(oh[:, 0], iot, bc(lixf[:, :, 0], E), ALU.is_equal)
                if n != 1:
                    nc.vector.tensor_tensor(oh[:, 1], iot, bc(lixf[:, :, 1], E), ALU.is_equal)
                dve.wait_ge(router_exp, n + 1)
                if n == 1:
                    link(nc.vector.tensor_reduce(rw[:, 2, :], lg[:], AX.X, ALU.add))
                    link(nc.vector.reciprocal(rw[:, 3, :], rw[:, 2, :]))
                    nc.vector.tensor_tensor(cw[:], oh[:, 0], bc(rw[:, 3, :], E), ALU.mult).then_inc(cw_ready, 1)
                else:
                    link(nc.vector.tensor_scalar(rw[:, 2, :], rw[:, 1, :], 1.0, None, ALU.add))
                    link(nc.vector.reciprocal(rw[:, 3, :], rw[:, 2, :]))
                    link(nc.vector.tensor_tensor(rw[:, 2, :], rw[:, 3, :], rw[:, 1, :], ALU.mult))
                    nc.vector.tensor_tensor(oh[:, 0], oh[:, 0], bc(rw[:, 3, :], E), ALU.mult)
                    link(nc.vector.tensor_tensor(oh[:, 1], oh[:, 1], bc(rw[:, 2, :], E), ALU.mult))
                    nc.vector.tensor_tensor(cw[:], oh[:, 0], oh[:, 1], ALU.add).then_inc(cw_ready, 1)

            def split_rows(layer):
                dve.wait_ge(moe[layer]["x_hi"], 1)
                nc.vector.tensor_tensor(xl[:], xnT[:], xh[:].bitcast(F32), ALU.subtract).then_inc(moe[layer]["x_lo"], 1)

            def take_coefficients(layer):
                for n in range(2):
                    bank = filled(dve, f"cwT{layer}.{n}")
                    nc.vector.tensor_copy(cwT[:, 512 * n:512 * n + 512], bank[0:E, :]).then_inc(misc_emptied_v, 1)

            def experts0():
                m = moe[0]
                for j in range(E * 8 + 1):
                    if j < E * 8:
                        e, c = j // 8, j // 2 % 4
                        dve.wait_ge(m["act"], j + 1)
                        dve.wait_ge(m["up"], j + 1)
                        if j >= 2:
                            dve.wait_ge(m["scaled"], j - 1)
                        nc.vector.scalar_tensor_tensor(PR[:, j % 2, :], TP[j % 2], hb2[:, e, c:c + 1], sg[:, j % 2, :],
                                                       ALU.add, ALU.mult).then_inc(m["mixed"], 1)
                    if j >= 1:
                        dve.wait_ge(m["hi"], j)
                        if j >= 3:
                            dve.wait_ge(m["down"], j - 2)
                        k = (j - 1) % 2
                        nc.vector.tensor_tensor(hl[:, k, :], PT[:, k, :], hh[:, k, :].bitcast(F32), ALU.subtract) \
                            .then_inc(m["lo"], 1)

            def split_piece(e, k):
                m, s, a = moe[2], e % 2, PIECE * k
                dve.wait_ge(m["w_hi"], PIECES[2] * e + k + 1)
                nc.vector.tensor_tensor(wl[:, s, a:a + PIECE], ring[:, s, a:a + PIECE],
                                        wh[:, s, a:a + PIECE].bitcast(F32), ALU.subtract).then_inc(m["w_lo"], 1)

            def experts2():
                m = moe[2]
                for j in range(E * 4):
                    e, n = j // 4, j % 2
                    if j < 2:
                        emptied(dve, f"cwB2.{n}")
                    elif e >= 1 and j % 4 == 0:
                        dve.wait_ge(cw_loaded[e], 32)
                    dve.wait_ge(m["act"], j + 1)
                    hi, lo, rows = hidden2(j)
                    if j >= 4:
                        rest_done(dve, j - 4)
                    nc.vector.tensor_tensor(rows, sg[:, j % 2, :], cwB[:, e, 512 * n:512 * n + 512],
                                            ALU.mult).then_inc(m["scaled"], 1)
                    if e + 1 < E and j % 4 in PIECE_AT[2]:
                        split_piece(e + 1, PIECE_AT[2].index(j % 4))
                    dve.wait_ge(m["scaled"], j + 1)
                    if j >= 4:
                        dve.wait_ge(m["down"], j - 3)
                    nc.vector.tensor_copy(hi, rows).then_inc(m["hi"], 1)

            def add_half(name, n, gate):
                rows = x[:, 4 * n:4 * n + 4, :].rearrange("p t d -> p (t d)")
                nc.vector.scalar_tensor_tensor(rows, filled(dve, name), tg[:, gate:gate + 1], rows, ALU.mult, ALU.add) \
                    .then_inc(misc_emptied_v, 1)
                emptied(dve, name)
                nc.vector.tensor_copy(veps[:, 0:1], x[:, 4 * n, 0:1]).then_inc(x_updated, 4)

            def add_experts(layer, gate):
                for n in range(2):
                    add_half(f"yT{layer}.{n}", n, gate)

            def quantize_weight(w, scales, inverse, nchunk):
                link(nc.vector.tensor_reduce(scales, w, AX.X, ALU.max, apply_absolute_value=True))
                link(nc.vector.tensor_scalar(scales, scales, 1.0 / QMAX, None, ALU.mult))
                link(nc.vector.reciprocal(inverse, scales))
                for c in range(nchunk):
                    v = w if nchunk == 1 else w[:, c, :]
                    ins = nc.vector.tensor_scalar(v, v, inverse[:, c:c + 1], QMAX, ALU.mult, ALU.min)
                link(ins)
                link(nc.vector.tensor_scalar(w, w, -QMAX - 1.0, ROUND, ALU.max, ALU.add))
                return nc.vector.tensor_scalar(w, w, ROUND, None, ALU.subtract)

            dve.wait_ge(ld_er, 16)
            link(nc.vector.tensor_copy(erp[:, 0, :], erf[:]))
            link(nc.vector.tensor_tensor(erf[:], erf[:], erp[:, 0, :], ALU.subtract))
            link(nc.vector.tensor_copy(erp[:, 1, :], erf[:]))
            nc.vector.tensor_tensor(erp[:, 2, :], erf[:], erp[:, 1, :], ALU.subtract).then_inc(erparts_ready, 1)
            loaded(dve, "b0")
            nc.vector.tensor_scalar(nbq0, b0[:, 0:1], -SLICE8, None, ALU.mult).then_inc(nbq_ready, 1)
            dve.wait_ge(ld_x, 16)
            norm_rows(0, x)
            loaded(dve, "bv0")
            split_queries("q0")
            values8("v0", bv0)
            loaded(dve, "wg", "wu", "wd", "ident")
            quantize_weight(wg[:], wgs, iwg, NI).then_inc(weights_scaled, 1)
            quantize_weight(wu[:], wus, iwu, NI).then_inc(weights_scaled, 1)
            quantize_weight(wd[:], wds, iwd, 1).then_inc(weights_scaled, 1)
            nc.vector.tensor_scalar(diag[:], ident[:], wds, None, ALU.mult).then_inc(weights_scaled, 1)
            loaded(dve, "maskf", "b1")
            nc.vector.tensor_scalar(nbq1, b1[:, 0:1], -SLICE8, None, ALU.mult).then_inc(nbq_ready, 1)
            for name, dst in (("wgT.0", wgT), ("wuT.0", wuT)):
                bank = filled(dve, name)
                nc.vector.tensor_copy(dst[:], bank[:, 0:NI * CI]).then_inc(misc_emptied_v, 1)
            bank = filled(dve, "wdT.0")
            nc.vector.tensor_copy(wdT[:], bank[0:CI, :].rearrange("p (c d) -> p c d", c=NI)).then_inc(misc_emptied_v, 1)
            bank = filled(dve, "wdrow.0")
            nc.vector.tensor_copy(wdrow[:], bank[:, 0:D]).then_inc(misc_emptied_v, 1)
            loaded(dve, "bv1")
            for n in range(2):
                take_rows(f"v1.{n}", VA[:, 4 * n:4 * n + 4, 0:D], bv1[:].unsqueeze(1).to_broadcast([P, 4, D]))
            dve.wait_ge(gates_ready, 1)
            attention(0)
            norm_rows(1, x, 1)
            loaded(dve, "br0", "iota", "hb2")
            split_rows(0)
            router(0, "router0.0", br0)
            take_coefficients(0)
            experts0()
            add_experts(0, 4)
            norm_rows(2, x, 2)
            dve.wait_ge(ld_mrow, 16)
            link(nc.vector.tensor_scalar(closed, closed, -10000.0, 10000.0, ALU.mult, ALU.add))
            attention(1)
            dve.wait_ge(sig_exp, 1)
            link(nc.vector.tensor_scalar(sg2, sg2, 1.0, None, ALU.add))
            link(nc.vector.reciprocal(sg2, sg2))
            norm_rows(3, x, 3)
            dve.wait_ge(rows_normed, 4 * NT)
            nc.vector.tensor_reduce(amx, xn[:], AX.XY, ALU.max, apply_absolute_value=True).then_inc(xmax_ready, 1)
            dve.wait_ge(xmax_all, 1)
            link(nc.vector.tensor_scalar(sx, amxg, sg2[:, 0:1], 1.0 / QMAX, ALU.mult, ALU.mult))
            nc.vector.tensor_scalar(fg, wgs, sx[0:CI, :], None, ALU.mult)
            nc.vector.tensor_scalar(fu, wus, sx[0:CI, :], None, ALU.mult)
            link(nc.vector.reciprocal(isx, sx))
            emptied(dve, "ln3.0")
            emptied(dve, "ln3.1")
            link(nc.vector.tensor_scalar(qf, xnT[:], isx, QMAX, ALU.mult, ALU.min))
            link(nc.vector.tensor_scalar(qf, qf, -QMAX - 1.0, ROUND, ALU.max, ALU.add))
            nc.vector.tensor_scalar(xq[:], qf, ROUND, None, ALU.subtract).then_inc(xq_ready, 1)
            for j in range(2 * NI):
                c, n = j // 2, j % 2
                dve.wait_ge(l1_silu, j + 1)
                dve.wait_ge(l1_up, j + 1)
                nc.vector.scalar_tensor_tensor(h1[0:CI, c, 512 * n:512 * n + 512], TP[j % 2][0:CI, :], fu[:, c:c + 1],
                                               sg[0:CI, j % 2, :], ALU.mult, ALU.mult).then_inc(l1_hidden, 1)
            dve.wait_ge(l1_hidden, 2 * NI)
            dve.wait_ge(pool_consts, 7)
            nc.vector.tensor_reduce(amh[0:CI, :], h1[0:CI], AX.XY, ALU.max, apply_absolute_value=True) \
                .then_inc(hmax_ready, 1)
            dve.wait_ge(hmax_all, 1)
            link(nc.vector.tensor_scalar(sh, amhg, sg2[:, 1:2], 1.0 / QMAX, ALU.mult, ALU.mult))
            nc.vector.tensor_scalar(fac, sh, tg[:, 5:6], None, ALU.mult)
            nc.vector.reciprocal(ish, sh).then_inc(hscale_ready, 1)
            dve.wait_ge(hscale_ready, 1)
            v = h1[0:CI, :, 0:512]
            link(nc.vector.tensor_scalar(v, v, ish[0:CI, :], ROUND, ALU.mult, ALU.add))
            for n in range(2):
                v = h1[0:CI, :, 512 * n:512 * n + 512]
                if n == 1:
                    dve.wait_ge(hscaled, 1)
                ins = nc.vector.tensor_scalar(v, v, ROUND + QMAX, ROUND - QMAX - 1.0, ALU.min, ALU.max)
                if n == 0:
                    ins.then_inc(hclipped, 1)
                else:
                    link(ins)
            nc.vector.tensor_scalar(h1q[0:CI, :, 512:1024], h1[0:CI, :, 512:1024], ROUND, None, ALU.subtract) \
                .then_inc(hq_ready1, 1)
            for n in range(2):
                dve.wait_ge(l1_down, n + 1)
                y = xn[:, 4 * n:4 * n + 4, :]
                link(nc.vector.tensor_tensor(y, OB[n].rearrange("p (t d) -> p t d", t=4),
                                             wdrow[:].unsqueeze(1).to_broadcast([P, 4, D]), ALU.mult))
                rows = x[:, 4 * n:4 * n + 4, :]
                nc.vector.scalar_tensor_tensor(rows, y, fac, rows, ALU.mult, ALU.add).then_inc(x_updated, 4)
            loaded(dve, "maski")
            nc.vector.tensor_scalar(mk2[:], maski[:], 0.0, None, ALU.not_equal)
            norm_rows(4, x, 4)
            split_queries("q2")
            dve.wait_ge(ld_ctx, 16)
            norm_rows(5, ctxr, dst=ctxr)
            loaded(dve, "lnp")
            for n in range(2):
                bank = filled(dve, f"lnc.{n}")
                nc.vector.tensor_scalar(cnT[:, 512 * n:512 * n + 512], bank, lnp[:, 0:1], lnp[:, 1:2],
                                        ALU.mult, ALU.add).then_inc(misc_emptied_v, 1)
            attention(2)
            for n in range(2):
                add_half(f"wo2.{n}", n, 2)
            norm_rows(6, x, 5)
            loaded(dve, "br2")
            split_rows(2)
            for k in range(PIECES[2]):
                split_piece(0, k)
            router(1, "router2.0", br2)
            take_coefficients(2)
            experts2()
            add_experts(2, 6)
            norm_rows(7, x, 6)
            dve.wait_ge(rows_normed, 8 * NT)
            norm_rows(8, xn)
            loaded(dve, "cos", "sin")
            for n in range(2):
                bank = filled(dve, f"ln8.{n}")
                nc.vector.tensor_scalar(xnT[:, 512 * n:512 * n + 512], bank, lnp[:, 2:3], lnp[:, 3:4],
                                        ALU.mult, ALU.add).then_inc(misc_emptied_v, 1)
            for c in range(4):
                dve.wait_ge(swapped[c], 16 * 4)
                for v, table in ((KT3[:, c, :, 0:S], cos), (k_swapped(c), sin)):
                    nc.vector.tensor_tensor(v, v, table[:].unsqueeze(1).to_broadcast([P, NB, S]), ALU.mult) \
                        .then_inc(rope_in, 1)
            dve.wait_ge(vones, 2)

            def values(kind):
                for t in range(1, NT, 2):
                    k = 4 * (t // 2) + 3
                    bank = filled(dve, f"{kind}.{t}")
                    nc.vector.tensor_copy(VX[:, k, :, 0:DH3], bank.rearrange("p (h e) -> p h e", h=NH3)) \
                        .then_inc(misc_emptied_v, 1)

            values("vl")
            dve.wait_ge(x_updated, 6 * NT)
            loaded(dve, "iota")
            attention(3)

        @block.tensor
        def _(pe):
            def room(name):
                i = AT[name]
                if i >= 2:
                    emptied(pe, MISC[i - 2][0])
                return MB[i % 2]

            def halves(name, w, xT):
                for n in range(2):
                    bank = room(f"{name}.{n}")
                    nc.tensor.matmul(bank, w, xT[:, 512 * n:512 * n + 512], start=True, stop=True) \
                        .then_inc(misc_ready, 1)

            def rows(name, xT, w):
                for n in range(2):
                    bank = room(f"{name}.{n}")
                    for k in range(4):
                        t = 4 * n + k
                        ins = nc.tensor.matmul(bank[:, 128 * k:128 * k + 128], xT[:, 128 * t:128 * t + 128], w,
                                               start=True, stop=True)
                    ins.then_inc(misc_ready, 1)

            def turn_rows(n, name, src=xn):
                for hf in range(2):
                    bank = room(f"{name}.{hf}")
                    for k in range(4):
                        t = 4 * hf + k
                        pe.wait_ge(rows_normed, NT * n + t + 1)
                        ins = nc.tensor.transpose(bank[:, 128 * k:128 * k + 128], src[:, t, :], ident[:])
                    ins.then_inc(misc_ready, 1)

            def turned(name):
                for n in range(2):
                    emptied(pe, f"{name}.{n}")

            def queries(name, w, rows):
                for n in range(2):
                    bank = room(f"{name}.{n}")
                    emptied(pe, f"{rows}.{n}")
                    nc.tensor.matmul(bank, w, xnT[:, 512 * n:512 * n + 512], start=True, stop=True) \
                        .then_inc(misc_ready, 1)

            def rel(r):
                t, h, g, w = UNITS8[r]
                if h == 0 and t % 4 == 0:
                    pe.wait_ge(qs_loaded[t // 4], 16 * NPART)
                bank = room(f"qer.{r}")
                for k in range(g):
                    ins = nc.tensor.matmul(bank[:, k * w:(k + 1) * w], QS[:, t // 4, h + k, t % 4 * P:t % 4 * P + P],
                                           ES[:, S - w:S], start=True, stop=True)
                ins.then_inc(misc_ready, 1)

            def scores(layer, i):
                t, h, g, w = UNITS[layer][i]
                b, u = t // 2, BASE[layer] + i
                bank = SC[u % 2]
                if layer in (0, 2) and h == 0 and t % 4 == 0:
                    pe.wait_ge(ks_loaded[t // 4], 16 * (1 + layer // 2))
                    pe.wait_ge(qs_loaded[t // 4], 16 * NPART * (1 + layer // 2))
                if u >= 2:
                    pe.wait_ge(min_ready if u - 2 < BASE[3] else probs_ready, u - 1)
                if layer in (0, 2):
                    for k in range(g):
                        ins = nc.tensor.matmul(bank[:, k * w:(k + 1) * w],
                                               QS[:, t // 4, h + k, t % 4 * P:t % 4 * P + P],
                                               KS[:, b // 2, h + k, b % 2 * S:b % 2 * S + w], start=True, stop=True)
                elif layer == 1:
                    for k in range(2):
                        ins = nc.tensor.matmul(bank[:, k * S:(k + 1) * S], qf[:, (t + k) * P:(t + k + 1) * P],
                                               k1f[:, b * S:(b + 1) * S], start=True, stop=True)
                else:
                    r = DH3 * (h % 2)
                    g = i // 2
                    pe.wait_ge(pair_lo, 2 * g + 2)
                    (k_hi, k_lo, _), (q_hi, q_lo, _) = pair(g)
                    nc.tensor.matmul(bank, q_hi[r:r + DH3], k_hi[r:r + DH3], start=True, stop=False)
                    nc.tensor.matmul(bank, q_hi[r:r + DH3], k_lo[r:r + DH3], start=False, stop=False)
                    ins = nc.tensor.matmul(bank, q_lo[r:r + DH3], k_hi[r:r + DH3], start=False, stop=True)
                ins.then_inc(scores_ready, 1)

            def turn_probs(layer, i):
                u = BASE[layer] + i
                pe.wait_ge(probs_ready, u + 1)
                if u >= 2:
                    copied(pe, u - 2)
                for k in range(4):
                    ins = nc.tensor.transpose(TP[u % 2][:, P * k:P * k + P], PR[:, u % 2, P * k:P * k + P], ident[:])
                ins.then_inc(probsT_ready, 1)

            def weigh(layer, i):
                t, h, g, w = UNITS[layer][i]
                u = BASE[layer] + i
                k0 = sum(j < i for j in LAST[layer])
                grp = GROUPS[layer] + k0
                if i == 0 or i - 1 in LAST[layer]:
                    behind = grp if layer == 3 else grp - 1
                    if behind > 0:
                        pe.wait_ge(out_read, behind)
                copied(pe, u)
                for k in range(4):
                    pt = PT[:, u % 2, P * k:P * k + P]
                    if layer in (0, 2):
                        hh, jt, last = (h + k, 0, 0) if g == 4 else (h + k // 2, k % 2, 1)
                        a = (DH + 1) * (NH * (t - t % 2 + jt) + hh)
                        ins = nc.tensor.matmul(OB[grp % 2][:, 9 * hh:9 * hh + WIDE], pt, v9[:, a:a + WIDE],
                                               start=(jt == 0), stop=(jt == last))
                    elif layer == 1:
                        it, jt = k // 2, k % 2
                        ins = nc.tensor.matmul(OB[grp % 2][:, 129 * it:129 * it + 129], pt, VA[:, t + jt, :],
                                               start=(jt == 0), stop=(jt == 1))
                    else:
                        a = (DH3 + 1) * (NH3 * (4 * (t // 2) + k) + h)
                        ins = nc.tensor.matmul(OB[h // 4][:, 65 * (h % 4):65 * (h % 4) + WIDE], pt,
                                               arenaB[:, a:a + WIDE], start=(k == 0), stop=(k == 3))
                ins.then_inc(pv_done, 1)

            def attention(layer):
                n = len(UNITS[layer])
                for i in range(n + WEIGH + (13 if layer == 3 else 2)):
                    if layer == 0 and i + LEAD < N8:
                        rel(i + LEAD)
                    if i < n:
                        scores(layer, i)
                    if 0 <= i - TURN < n:
                        turn_probs(layer, i - TURN)
                    if 0 <= i - WEIGH < n:
                        weigh(layer, i - WEIGH)
                    if layer == 3:
                        finished_tile(i)

            def finished_tile(i):
                t = _tile3(i, 1)
                if t is not None:
                    bank = room(f"oT3.{t}")
                    pe.wait_ge(out_read, GROUPS[3] + t + 1)
                    for k in range(4):
                        ins = nc.tensor.transpose(bank[:, P * k:P * k + P], stage3[:, P * k:P * k + P], ident[:])
                    ins.then_inc(misc_ready, 1)
                t = _tile3(i, 2)
                if t is not None:
                    bank = room(f"wo3.{t}")
                    emptied(pe, f"oT3.{t}")
                    for k in range(4):
                        ins = nc.tensor.matmul(bank[:, 0:D], sg[:, 0, P * k:P * k + P], wo3[:, k, :],
                                               start=(k == 0), stop=(k == 3))
                    ins.then_inc(misc_ready, 1)
                t = _tile3(i, 4)
                if t is not None:
                    bank = room(f"ln9.{t}")
                    pe.wait_ge(rows_normed, NT * 9 + t + 1)
                    nc.tensor.transpose(bank[:, 0:P], xn[:, t, :], ident[:]).then_inc(misc_ready, 1)
                t = _tile3(i, 5)
                if t is not None:
                    bank = room(f"router3.{t}")
                    emptied(pe, f"ln9.{t}")
                    nc.tensor.matmul(bank[:, 0:E], xnT[:, P * t:P * t + P], wr3[:], start=True, stop=True) \
                        .then_inc(misc_ready, 1)
                    bank = room(f"uv.{t}")
                    nc.tensor.matmul(bank, xnT[:, P * t:P * t + P], wuv[:], start=True, stop=True) \
                        .then_inc(misc_ready, 1)
                t = _tile3(i, 11)
                if t is not None:
                    bank = room(f"sT.{t}")
                    pe.wait_ge(s3_ready, t + 1)
                    for k in range(2):
                        ins = nc.tensor.transpose(bank[:, P * k:P * k + P], Sx[:, 0, P * k:P * k + P], ident[:])
                    ins.then_inc(misc_ready, 1)
                t = _tile3(i, 12)
                if t is not None:
                    bank = room(f"y3.{t}")
                    emptied(pe, f"sT.{t}")
                    for k in range(2):
                        ins = nc.tensor.matmul(bank[:, 0:D], Sx[:, 1, P * k:P * k + P], wf3[:, k, :],
                                               start=(k == 0), stop=(k == 1))
                    ins.then_inc(misc_ready, 1)

            def logits(name, w):
                bank = room(name)
                for t in range(NT):
                    ins = nc.tensor.matmul(bank[:, E * t:E * t + E], xnT[:, P * t:P * t + P], w[:],
                                           start=True, stop=True)
                ins.then_inc(misc_ready, 1)

            def turn_coefficients(layer, n_cw):
                pe.wait_ge(cw_ready, n_cw)
                for n in range(2):
                    bank = room(f"cwB{layer}.{n}")
                    for k in range(4):
                        ins = nc.tensor.matmul(bank[:, P * k:P * k + P], cw[:, 4 * n + k, 0:1].to_broadcast([P, P]),
                                               ident[:], start=True, stop=True)
                    ins.then_inc(misc_ready, 1)
                for n in range(2):
                    bank = room(f"cwT{layer}.{n}")
                    for k in range(4):
                        ins = nc.tensor.transpose(bank[0:E, P * k:P * k + P], cw[:, 4 * n + k, :], ident[:])
                    ins.then_inc(misc_ready, 1)

            def three(out, w, at, xs_hi, xs_lo, start, stop):
                nc.tensor.matmul(out, wh[:, w, at:at + P], xs_hi, start=start, stop=False)
                nc.tensor.matmul(out, wh[:, w, at:at + P], xs_lo, start=False, stop=False)
                return nc.tensor.matmul(out, wl[:, w, at:at + P], xs_hi, start=False, stop=stop)

            def experts(layer, nch, b):
                m, per = moe[layer], 2 * nch
                nj, down_at = E * per, {0: 1024, 2: 256}[layer]
                pe.wait_ge(m["x_lo"], 1)
                for j in range(nj + 3):
                    if j < nj:
                        e, c, n = j // per, j // 2 % nch, j % 2
                        if j % per == 0:
                            pe.wait_ge(m["w_lo"], PIECES[layer] * e + {0: 4, 2: 1}[layer])
                        x_hi, x_lo = xh[:, 512 * n:512 * n + 512], xl[:, 512 * n:512 * n + 512]
                        if j >= 2:
                            pe.wait_ge(m["act"], j - 1)
                        three(SC[j % 2], e % 2, P * c, x_hi, x_lo, True, True).then_inc(m["gate"], 1)
                        if layer == 0:
                            if j >= 2:
                                pe.wait_ge(m["mixed"], j - 1)
                            three(TP[j % 2], e % 2, 512 + P * c, x_hi, x_lo, True, True).then_inc(m["up"], 1)
                    if j == 1:
                        turn_coefficients(layer, 1 + layer // 2)
                    if j == 8:
                        emptied(pe, f"cwT{layer}.1")
                        for n in range(2):
                            nc.tensor.matmul(OB[n], b[:], cwT[:, 512 * n:512 * n + 512], start=False, stop=False)
                    if j >= 3:
                        i = j - 3
                        e, c, n = i // per, i // 2 % nch, i % 2
                        if i % per == 0:
                            pe.wait_ge(m["w_lo"], PIECES[layer] * (e + 1))
                        if layer == 0:
                            pe.wait_ge(m["lo"], i + 1)
                        else:
                            rest_done(pe, i)
                        hi, lo = hidden2(i)[:2] if layer == 2 else (hh[:, i % 2, :], hl[:, i % 2, :])
                        three(OB[n], e % 2, down_at + P * c, hi, lo, i < 2, i >= nj - 2).then_inc(m["down"], 1)
                for n in range(2):
                    pe.wait_ge(m["summed"], n + 1)
                    bank = room(f"yT{layer}.{n}")
                    for k in range(4):
                        t = 4 * n + k
                        ins = nc.tensor.transpose(bank[:, P * k:P * k + P], xnT[:, P * t:P * t + P], ident[:])
                    ins.then_inc(misc_ready, 1)

            loaded(pe, "wk0")
            pe.wait_ge(ld_ctxT, 16)
            halves("k0", wk0[:], ctxT)
            loaded(pe, "ident")
            turn_rows(0, "ln0")
            loaded(pe, "wq0")
            queries("q0", wq0[:], "ln0")
            loaded(pe, "wv0", "wk2")
            rows("v0", ctxT, wv0[:])
            halves("k2", wk2[:], ctxT)
            pe.wait_ge(es_loaded, 16 * 9)
            for r in range(STAGE):
                rel(r)
            for name, w, k in (("wgT.0", wg, 1), ("wuT.0", wu, 2)):
                bank = room(name)
                pe.wait_ge(weights_scaled, k)
                for c in range(NI):
                    ins = nc.tensor.transpose(bank[:, CI * c:CI * c + CI], w[:, c, :], ident[0:CI, 0:CI])
                ins.then_inc(misc_ready, 1)
            bank = room("wdT.0")
            pe.wait_ge(weights_scaled, 3)
            for c in range(NI):
                ins = nc.tensor.transpose(bank[0:CI, P * c:P * c + P], wd[:, CI * c:CI * c + CI], ident[:])
            ins.then_inc(misc_ready, 1)
            bank = room("wdrow.0")
            pe.wait_ge(weights_scaled, 4)
            nc.tensor.matmul(bank[:, 0:D], ones[:], diag[:], start=True, stop=True).then_inc(misc_ready, 1)
            loaded(pe, "wk1", "wv1")
            halves("k1", wk1[:], ctxT)
            rows("v1", ctxT, wv1[:])
            for r in range(STAGE, LEAD):
                rel(r)
            pe.wait_ge(pool_consts, 7)
            attention(0)
            turn_rows(1, "ln1")
            turned("ln1")
            loaded(pe, "wr0", "hb3")
            logits("router0.0", wr0)
            experts(0, 4, hb3)
            loaded(pe, "wv2", "wq1")
            rows("v2", ctxT, wv2[:])
            turn_rows(2, "ln2")
            queries("q1", wq1[:], "ln2")
            for n in range(2):
                emptied(pe, f"q1.{n}")
            attention(1)
            for n in range(2):
                bank = room(f"mean.{n}")
                for k in range(2):
                    for jt in range(2):
                        t = 2 * (2 * n + k) + jt
                        ins = nc.tensor.matmul(bank[:, 144 * k:144 * k + 144], ones[:],
                                               V9[:, t].rearrange("p h e -> p (h e)"), start=(jt == 0), stop=(jt == 1))
                ins.then_inc(misc_ready, 1)
            turn_rows(3, "ln3")
            emptied(pe, "wdrow.0")
            pe.wait_ge(xq_ready, 1)
            for j in range(2 * NI):
                c, n = j // 2, j % 2
                if j >= 2:
                    pe.wait_ge(l1_silu, j - 1)
                nc.tensor.matmul(SC[j % 2][0:CI, :], wgT[:, CI * c:CI * c + CI], xq[:, 512 * n:512 * n + 512],
                                 start=True, stop=True).then_inc(l1_gate, 1)
                if j >= 2:
                    pe.wait_ge(l1_hidden, j - 1)
                nc.tensor.matmul(TP[j % 2][0:CI, :], wuT[:, CI * c:CI * c + CI], xq[:, 512 * n:512 * n + 512],
                                 start=True, stop=True).then_inc(l1_up, 1)
            for n in range(2):
                pe.wait_ge((hq_ready0, hq_ready1)[n], 1)
                for k in range(4):
                    t = 4 * n + k
                    for c in range(NI):
                        ins = nc.tensor.matmul(OB[n][:, P * k:P * k + P], h1q[0:CI, c, P * t:P * t + P], wdT[:, c, :],
                                               start=(c == 0), stop=(c == NI - 1))
                ins.then_inc(l1_down, 1)
            loaded(pe, "wq2", "wo2")
            turn_rows(4, "ln4")
            queries("q2", wq2[:], "ln4")
            turn_rows(5, "lnc", ctxr)
            attention(2)
            for n in range(2):
                bank = room(f"oT2.{n}")
                for k in range(4):
                    pe.wait_ge(heads_ready, 4 * n + k + 1)
                    ins = nc.tensor.transpose(bank[:, P * k:P * k + P], xn[:, 4 * n + k, :], ident[:])
                ins.then_inc(misc_ready, 1)
            turned("oT2")
            rows("wo2", xnT, wo2[:])
            turn_rows(6, "ln5")
            turned("ln5")
            loaded(pe, "wr2", "gb2")
            logits("router2.0", wr2)
            experts(2, 2, gb2)
            loaded(pe, "wkv3", "wq3", "wo3", "wr3", "wuv", "wf3")
            for c in range(4):
                for n in range(2):
                    bank = room(f"kc.{c}.{n}")
                    nc.tensor.matmul(bank, wkv3[:, P * c:P * c + P], cnT[:, 512 * n:512 * n + 512],
                                     start=True, stop=True).then_inc(misc_ready, 1)
            for t in range(NT):
                bank = room(f"vc.{t}")
                nc.tensor.matmul(bank, cnT[:, P * t:P * t + P], wkv3[:, 512:1024], start=True, stop=True) \
                    .then_inc(misc_ready, 1)
            turn_rows(8, "ln8")
            for n in range(2):
                emptied(pe, f"ln8.{n}")
            for c in range(4):
                for n in range(2):
                    bank = room(f"kl.{c}.{n}")
                    nc.tensor.matmul(bank, wkv3[:, P * c:P * c + P], xnT[:, 512 * n:512 * n + 512],
                                     start=True, stop=True).then_inc(misc_ready, 1)
                    bank = room(f"q3.{c}.{n}")
                    nc.tensor.matmul(bank, wq3[:, P * c:P * c + P], xnT[:, 512 * n:512 * n + 512],
                                     start=True, stop=True).then_inc(misc_ready, 1)
            for t in range(NT):
                bank = room(f"vl.{t}")
                nc.tensor.matmul(bank, xnT[:, P * t:P * t + P], wkv3[:, 512:1024], start=True, stop=True) \
                    .then_inc(misc_ready, 1)
            pe.wait_ge(rope_done, 4)
            pe.wait_ge(vones, 2)
            for n in ("q3.3.1", "vl.6", "vl.7"):
                emptied(pe, n)
            attention(3)


def _constants():
    half = DH3 // 2
    inv = (1.0 / np.float32(10000.0) ** (np.arange(0, DH3, 2, dtype=np.float32) / np.float32(DH3))).astype(np.float32)
    ang = (np.arange(S, dtype=np.float32)[None, :] * inv[:, None]).astype(np.float32)
    c, s = np.cos(ang).astype(np.float32), np.sin(ang).astype(np.float32)
    cos = np.concatenate([c] * 4, 0)
    sin = np.concatenate([-s, s, -s, s], 0)
    i, j = np.arange(P)[:, None], np.arange(P)[None, :]
    return {
        "ident": np.eye(P, dtype=np.float32),
        "maskf": np.concatenate([np.zeros((P, P)), np.where(j <= i, 0.0, BIG)], 1).astype(np.float32),
        "iota": np.tile(np.arange(E, dtype=np.float32), (P, 1)),
        "cos": np.ascontiguousarray(cos), "sin": np.ascontiguousarray(sin),
    }


def _lay_out(a):
    g = {k: np.asarray(v) for k, v in a.items()}
    ctx = g["ctx_1024"].reshape(TOK, D)
    wkv = g["L3_xattn_Wkv"]
    lay = {
        "x": g["x"].reshape(TOK, D), "ctx": ctx, "ctxT": ctx.T,
        "erT": g["L0_xattn_Er"].T, "mrow": g["mask_BxS2_ff1"].reshape(TOK),
        "gates": np.concatenate([g["g_xattn"], g["g_ffn"]]),
        "clips": np.concatenate([g["L1_ffn_clip_x"], g["L1_ffn_clip_down"]]),
        "wq0": g["L0_xattn_Wq"].T, "wk0": g["L0_xattn_Wk"].T, "wv0": g["L0_xattn_Wv"].T,
        "b0": np.stack([g["L0_xattn_bq"], g["L0_xattn_bk"]], 1), "bv0": g["L0_xattn_bv"],
        "wq1": g["L1_xattn_Wq"], "wk1": g["L1_xattn_Wk"], "wv1": g["L1_xattn_Wv"],
        "b1": np.stack([g["L1_xattn_bq"], g["L1_xattn_bk"]], 1), "bv1": g["L1_xattn_bv"],
        "wq2": g["L2_xattn_WQ"], "wk2": g["L2_xattn_WK"], "wv2": g["L2_xattn_WV"], "wo2": g["L2_xattn_WO"],
        "maski": g["mask_BxS2_ik0"].reshape(NT, P).T,
        "wr0": g["L0_ffn_Wr"], "br0": g["L0_ffn_br"],
        "hb1": g["L0_ffn_b1"].reshape(E, 4, P).transpose(2, 0, 1),
        "hb2": g["L0_ffn_b2"].reshape(E, 4, P).transpose(2, 0, 1), "hb3": g["L0_ffn_b3"],
        "f1": g["L0_ffn_W1"], "f2": g["L0_ffn_W2"], "f3": g["L0_ffn_W3"],
        "wr2": g["L2_ffn_Wg"], "br2": g["L2_ffn_bg"],
        "gb1": g["L2_ffn_b1"].reshape(E, 2, P).transpose(2, 0, 1), "gb2": g["L2_ffn_b2"],
        "g1": g["L2_ffn_W1"], "g2": g["L2_ffn_W2"],
        "wg": g["L1_ffn_w_gate"].reshape(NI, CI, D).transpose(1, 0, 2),
        "wu": g["L1_ffn_w_up"].reshape(NI, CI, D).transpose(1, 0, 2), "wd": g["L1_ffn_w_down"],
        "lnp": np.stack([g["L3_xattn_gamma_x"], g["L3_xattn_beta_x"], g["L3_xattn_gamma_l"], g["L3_xattn_beta_l"]], 1),
        "wq3": g["L3_xattn_Wq"], "wkv3": wkv,
        "wo3": g["L3_xattn_Wo"].reshape(4, P, D).transpose(1, 0, 2).reshape(P, 512),
        "wr3": g["L3_ffn_gate_w"],
        "wuv": np.concatenate([g["L3_ffn_Wu"].transpose(1, 0, 2).reshape(D, 256),
                               g["L3_ffn_Wv"].transpose(1, 0, 2).reshape(D, 256)], 1),
        "wf3": g["L3_ffn_Wo"].reshape(2, P, D).transpose(1, 0, 2).reshape(P, 256),
    }
    return {k: np.ascontiguousarray(v) for k, v in lay.items()}


def kernel(**inputs):
    import concourse.bacc as bacc
    from concourse.bass_utils import run_bass_kernel_spmd

    arrays = {**_lay_out(inputs), **_constants()}
    nc = bacc.Bacc("TRN2", target_bir_lowering=False, num_devices=1)
    aps = {k: nc.dram_tensor("in_" + k + "_dram", v.shape, mybir.dt.from_np(v.dtype), kind="ExternalInput").ap()
           for k, v in arrays.items()}
    out = nc.dram_tensor("out_dram", (TOK, D), F32, kind="ExternalOutput").ap()
    build(nc, aps, out)
    r = run_bass_kernel_spmd(nc, [{"in_" + k + "_dram": v for k, v in arrays.items()}], core_ids=[0])
    return np.asarray(r.results[0]["out_dram"]).reshape(NB, S, D)
```
